# Optimizing a Trainium2 kernel written in Bass

```python
import numpy as np
import jax
import jax.numpy as jnp

def _softmax(x, axis=-1):
    return jax.nn.softmax(x, axis=axis)

def _gelu(x):
    return jax.nn.gelu(x, approximate=True)

def _silu(x):
    return jax.nn.silu(x)

def _sigmoid(x):
    return jax.nn.sigmoid(x)

def _layernorm(x, axis=-1, eps=1e-05):
    m = jnp.mean(x, axis=axis, keepdims=True)
    v = jnp.var(x, axis=axis, keepdims=True)
    return (x - m) / jnp.sqrt(v + eps)

def _scatter_add(tgt, idx, src, axis=0):
    return tgt.at[idx].add(src)

def _segment_sum(src, seg, n):
    return jax.ops.segment_sum(src, seg, n)
kernel_name = 'mk_vit_tower_cls_d1_tok_img1024_r4_9eadd8'

def setup_inputs(seed: int=0):
    np.random.seed(seed)
    _w = jnp.asarray

    def _rec_inputs():
        import jax
        import jax.numpy as jnp
        _rk = jax.random.key(seed)
        x = -0.000392918 + 0.999932 * jax.random.normal(jax.random.fold_in(_rk, 1), (8, 256, 256, 1), jnp.float32)
        cls_tok = 0.02 * jax.random.normal(jax.random.fold_in(_rk, 5), (1, 1, 256), jnp.float32)
        return (x, cls_tok)
    x, cls_tok = _rec_inputs()

    def _L0_tok_setup():
        import jax, jax.numpy as jnp
        import numpy as np
        INV_SQRT2 = 0.7071067811865476
        LEVEL = 3

        def _split(x, axis):
            ax = axis % x.ndim
            sl0 = [slice(None)] * x.ndim
            sl0[ax] = slice(0, None, 2)
            sl1 = [slice(None)] * x.ndim
            sl1[ax] = slice(1, None, 2)
            x0, x1 = (x[tuple(sl0)], x[tuple(sl1)])
            return ((x0 + x1) * INV_SQRT2, (x0 - x1) * INV_SQRT2)

        def _merge(lo, hi, axis):
            ax = axis % lo.ndim
            e = (lo + hi) * INV_SQRT2
            o = (lo - hi) * INV_SQRT2
            s = jnp.stack([e, o], axis=ax + 1)
            shape = list(lo.shape)
            shape[ax] *= 2
            return s.reshape(shape)

        def _dwt2(x):
            lo, hi = _split(x, -1)
            a, h = _split(lo, -2)
            v, d = _split(hi, -2)
            return (a, h, v, d)

        def _idwt2(a, h, v, d):
            lo = _merge(a, h, -2)
            hi = _merge(v, d, -2)
            return _merge(lo, hi, -1)
        key = jax.random.key(seed)
        ks = jax.random.split(key, 8)
        B, H, W = (16, 256, 256)
        x = jax.random.normal(ks[0], (B, H, W, 1), dtype=jnp.float32)
        na = H // 8 * (W // 8)
        n2 = H // 4 * (W // 4)
        n1 = H // 2 * (W // 2)
        scale = 0.02
        Wa = jax.random.normal(ks[1], (na, 1), dtype=jnp.float32) * scale
        ba = jnp.zeros((1,), jnp.float32)
        Wd1 = jax.random.normal(ks[2], (3 * na, 3), dtype=jnp.float32) * scale
        bd1 = jnp.zeros((3,), jnp.float32)
        Wd2 = jax.random.normal(ks[3], (3 * n2, 3), dtype=jnp.float32) * scale
        bd2 = jnp.zeros((3,), jnp.float32)
        Wd3 = jax.random.normal(ks[4], (3 * n1, 3), dtype=jnp.float32) * scale
        bd3 = jnp.zeros((3,), jnp.float32)
        return {'x': x, 'Wa': Wa, 'ba': ba, 'Wd1': Wd1, 'bd1': bd1, 'Wd2': Wd2, 'bd2': bd2, 'Wd3': Wd3, 'bd3': bd3}
    _L0_tok_all = _L0_tok_setup()
    _L0_tok_in = {k: v for k, v in _L0_tok_all.items() if k in ('Wa', 'ba', 'Wd1', 'bd1', 'Wd2', 'bd2', 'Wd3', 'bd3')}
    del _L0_tok_all

    def _L0_attn_setup():
        import jax, jax.numpy as jnp
        import numpy as np
        L, H, D, DH, DF = (4, 16, 256, 64, 1024)
        B, S = (4, 256)

        def layer_norm(x, g, b):
            mu = jnp.mean(x, axis=-1, keepdims=True)
            var = jnp.mean((x - mu) ** 2, axis=-1, keepdims=True)
            return (x - mu) * jax.lax.rsqrt(var + 1e-05) * g + b

        def pos_encoding(seq_len, d):
            pos = jnp.arange(seq_len - 1, -1, -1, dtype=jnp.float32)
            freq = 1.0 / 10000.0 ** (jnp.arange(0, d, 2, dtype=jnp.float32) / d)
            ang = pos[:, None] * freq[None, :]
            return jnp.concatenate([jnp.sin(ang), jnp.cos(ang)], axis=-1)
        key = jax.random.key(seed)
        ks = jax.random.split(key, 16)
        s = 0.02
        return {'x': jax.random.normal(ks[0], (B, S, D), jnp.float32), 'W_qkv': jax.random.normal(ks[1], (L, D, 3 * H * DH), jnp.float32) * s, 'W_r': jax.random.normal(ks[2], (L, D, H * DH), jnp.float32) * s, 'W_o': jax.random.normal(ks[3], (L, H * DH, D), jnp.float32) * s, 'u': jax.random.normal(ks[4], (H, DH), jnp.float32) * s, 'v': jax.random.normal(ks[5], (H, DH), jnp.float32) * s, 'ln1_g': jnp.ones((L, D), jnp.float32), 'ln1_b': jnp.zeros((L, D), jnp.float32), 'W_ff1': jax.random.normal(ks[6], (L, D, DF), jnp.float32) * s, 'b_ff1': jnp.zeros((L, DF), jnp.float32), 'W_ff2': jax.random.normal(ks[7], (L, DF, D), jnp.float32) * s, 'b_ff2': jnp.zeros((L, D), jnp.float32), 'ln2_g': jnp.ones((L, D), jnp.float32), 'ln2_b': jnp.zeros((L, D), jnp.float32)}
    _L0_attn_all = _L0_attn_setup()
    _L0_attn_in = {k: v for k, v in _L0_attn_all.items() if k in ('W_qkv', 'W_r', 'W_o', 'u', 'v', 'ln1_g', 'ln1_b', 'W_ff1', 'b_ff1', 'W_ff2', 'b_ff2', 'ln2_g', 'ln2_b')}
    del _L0_attn_all

    def _L0_ffn_setup():
        import jax, jax.numpy as jnp
        import numpy as np
        D_MODEL = 256
        FFN_DIM = 512
        NUM_EXPERTS = 8
        NUM_GROUPS = 4
        EXPERTS_PER_GROUP = NUM_EXPERTS // NUM_GROUPS
        TOP_K = 2
        GROUPS_TOP_K = 1
        EPS = 1e-09

        def _topk_normalized(scores, k):
            vals, idx = jax.lax.top_k(scores, k)
            vals = vals / (jnp.sum(vals, axis=-1, keepdims=True) + EPS)
            return (vals, idx)
        key = jax.random.key(seed)
        ks = jax.random.split(key, 6)
        B, S = (2, 256)
        x = jax.random.normal(ks[0], (B, S, D_MODEL), dtype=jnp.float32)
        sd = 0.02
        macro_w = jax.random.normal(ks[1], (D_MODEL, NUM_GROUPS), dtype=jnp.float32) * sd
        micro_w = jax.random.normal(ks[2], (NUM_GROUPS, D_MODEL, EXPERTS_PER_GROUP), dtype=jnp.float32) * sd
        gate_w = jax.random.normal(ks[3], (NUM_EXPERTS, D_MODEL, FFN_DIM), dtype=jnp.float32) * sd
        up_w = jax.random.normal(ks[4], (NUM_EXPERTS, D_MODEL, FFN_DIM), dtype=jnp.float32) * sd
        down_w = jax.random.normal(ks[5], (NUM_EXPERTS, FFN_DIM, D_MODEL), dtype=jnp.float32) * sd
        return {'x': x, 'macro_w': macro_w, 'micro_w': micro_w, 'gate_w': gate_w, 'up_w': up_w, 'down_w': down_w}
    _L0_ffn_all = _L0_ffn_setup()
    _L0_ffn_in = {k: v for k, v in _L0_ffn_all.items() if k in ('macro_w', 'micro_w', 'gate_w', 'up_w', 'down_w')}
    del _L0_ffn_all
    return {'x': x, 'cls_tok': cls_tok, 'L0_tok_Wa': _L0_tok_in['Wa'], 'L0_tok_ba': _L0_tok_in['ba'], 'L0_tok_Wd1': _L0_tok_in['Wd1'], 'L0_tok_bd1': _L0_tok_in['bd1'], 'L0_tok_Wd2': _L0_tok_in['Wd2'], 'L0_tok_bd2': _L0_tok_in['bd2'], 'L0_tok_Wd3': _L0_tok_in['Wd3'], 'L0_tok_bd3': _L0_tok_in['bd3'], 'L0_attn_W_qkv': _L0_attn_in['W_qkv'], 'L0_attn_W_r': _L0_attn_in['W_r'], 'L0_attn_W_o': _L0_attn_in['W_o'], 'L0_attn_u': _L0_attn_in['u'], 'L0_attn_v': _L0_attn_in['v'], 'L0_attn_ln1_g': _L0_attn_in['ln1_g'], 'L0_attn_ln1_b': _L0_attn_in['ln1_b'], 'L0_attn_W_ff1': _L0_attn_in['W_ff1'], 'L0_attn_b_ff1': _L0_attn_in['b_ff1'], 'L0_attn_W_ff2': _L0_attn_in['W_ff2'], 'L0_attn_b_ff2': _L0_attn_in['b_ff2'], 'L0_attn_ln2_g': _L0_attn_in['ln2_g'], 'L0_attn_ln2_b': _L0_attn_in['ln2_b'], 'L0_ffn_macro_w': _L0_ffn_in['macro_w'], 'L0_ffn_micro_w': _L0_ffn_in['micro_w'], 'L0_ffn_gate_w': _L0_ffn_in['gate_w'], 'L0_ffn_up_w': _L0_ffn_in['up_w'], 'L0_ffn_down_w': _L0_ffn_in['down_w']}

def reference(x, cls_tok, L0_tok_Wa, L0_tok_ba, L0_tok_Wd1, L0_tok_bd1, L0_tok_Wd2, L0_tok_bd2, L0_tok_Wd3, L0_tok_bd3, L0_attn_W_qkv, L0_attn_W_r, L0_attn_W_o, L0_attn_u, L0_attn_v, L0_attn_ln1_g, L0_attn_ln1_b, L0_attn_W_ff1, L0_attn_b_ff1, L0_attn_W_ff2, L0_attn_b_ff2, L0_attn_ln2_g, L0_attn_ln2_b, L0_ffn_macro_w, L0_ffn_micro_w, L0_ffn_gate_w, L0_ffn_up_w, L0_ffn_down_w):
    import jax
    import jax.numpy as jnp

    def _L0_tok_ref(x, Wa, ba, Wd1, bd1, Wd2, bd2, Wd3, bd3):
        import jax, jax.numpy as jnp
        import numpy as np
        INV_SQRT2 = 0.7071067811865476
        LEVEL = 3

        def _split(x, axis):
            ax = axis % x.ndim
            sl0 = [slice(None)] * x.ndim
            sl0[ax] = slice(0, None, 2)
            sl1 = [slice(None)] * x.ndim
            sl1[ax] = slice(1, None, 2)
            x0, x1 = (x[tuple(sl0)], x[tuple(sl1)])
            return ((x0 + x1) * INV_SQRT2, (x0 - x1) * INV_SQRT2)

        def _merge(lo, hi, axis):
            ax = axis % lo.ndim
            e = (lo + hi) * INV_SQRT2
            o = (lo - hi) * INV_SQRT2
            s = jnp.stack([e, o], axis=ax + 1)
            shape = list(lo.shape)
            shape[ax] *= 2
            return s.reshape(shape)

        def _dwt2(x):
            lo, hi = _split(x, -1)
            a, h = _split(lo, -2)
            v, d = _split(hi, -2)
            return (a, h, v, d)

        def _idwt2(a, h, v, d):
            lo = _merge(a, h, -2)
            hi = _merge(v, d, -2)
            return _merge(lo, hi, -1)
        img = x[..., 0]
        B = img.shape[0]
        details = []
        cur = img
        for _ in range(LEVEL):
            cur, h, v, d = _dwt2(cur)
            details.append((h, v, d))
        aw = jax.nn.sigmoid(cur.reshape(B, -1) @ Wa + ba)
        rec = cur * aw[:, :, None]
        det_params = [(Wd1, bd1), (Wd2, bd2), (Wd3, bd3)]
        for (h, v, d), (Wd, bd) in zip(reversed(details), det_params):
            flat = jnp.stack([h, v, d], axis=1).reshape(B, -1)
            w = jax.nn.softmax(flat @ Wd + bd, axis=-1)
            rec = _idwt2(rec, h * w[:, 0, None, None], v * w[:, 1, None, None], d * w[:, 2, None, None])
        return rec

    def _L0_attn_ref(x, W_qkv, W_r, W_o, u, v, ln1_g, ln1_b, W_ff1, b_ff1, W_ff2, b_ff2, ln2_g, ln2_b):
        import jax, jax.numpy as jnp
        import numpy as np
        L, H, D, DH, DF = (4, 16, 256, 64, 1024)
        B, S = (4, 256)

        def layer_norm(x, g, b):
            mu = jnp.mean(x, axis=-1, keepdims=True)
            var = jnp.mean((x - mu) ** 2, axis=-1, keepdims=True)
            return (x - mu) * jax.lax.rsqrt(var + 1e-05) * g + b

        def pos_encoding(seq_len, d):
            pos = jnp.arange(seq_len - 1, -1, -1, dtype=jnp.float32)
            freq = 1.0 / 10000.0 ** (jnp.arange(0, d, 2, dtype=jnp.float32) / d)
            ang = pos[:, None] * freq[None, :]
            return jnp.concatenate([jnp.sin(ang), jnp.cos(ang)], axis=-1)
        b, s_len, _ = x.shape
        r = pos_encoding(s_len, D)
        h = x
        inv_sqrt_d = 1.0 / jnp.sqrt(jnp.float32(DH))
        for i in range(L):
            qkv = h @ W_qkv[i]
            q, k, val = jnp.split(qkv, 3, axis=-1)
            q = q.reshape(b, s_len, H, DH)
            k = k.reshape(b, s_len, H, DH)
            val = val.reshape(b, s_len, H, DH)
            kr = (r @ W_r[i]).reshape(s_len, H, DH)
            AC = jnp.einsum('bqhd,bkhd->bhqk', q + u, k)
            BD = jnp.einsum('bqhd,khd->bhqk', q + v, kr)
            prob = jax.nn.softmax((AC + BD) * inv_sqrt_d, axis=-1)
            vec = jnp.einsum('bhqk,bkhd->bqhd', prob, val).reshape(b, s_len, H * DH)
            h = layer_norm(h + vec @ W_o[i], ln1_g[i], ln1_b[i])
            ff = jax.nn.relu(h @ W_ff1[i] + b_ff1[i]) @ W_ff2[i] + b_ff2[i]
            h = layer_norm(ff, ln2_g[i], ln2_b[i])
        return h

    def _L0_ffn_ref(x, macro_w, micro_w, gate_w, up_w, down_w):
        import jax, jax.numpy as jnp
        import numpy as np
        D_MODEL = 256
        FFN_DIM = 512
        NUM_EXPERTS = 8
        NUM_GROUPS = 4
        EXPERTS_PER_GROUP = NUM_EXPERTS // NUM_GROUPS
        TOP_K = 2
        GROUPS_TOP_K = 1
        EPS = 1e-09

        def _topk_normalized(scores, k):
            vals, idx = jax.lax.top_k(scores, k)
            vals = vals / (jnp.sum(vals, axis=-1, keepdims=True) + EPS)
            return (vals, idx)
        B, S, D = x.shape
        T = B * S
        xf = x.reshape(T, D)
        macro_scores = jax.nn.sigmoid(xf @ macro_w)
        mv, mi = _topk_normalized(macro_scores, GROUPS_TOP_K)
        macro_full = jnp.sum(jax.nn.one_hot(mi, NUM_GROUPS, dtype=xf.dtype) * mv[..., None], axis=1)
        micro_scores = jax.nn.sigmoid(jnp.einsum('td,gde->tge', xf, micro_w))
        uv, ui = _topk_normalized(micro_scores, TOP_K)
        micro_full = jnp.sum(jax.nn.one_hot(ui, EXPERTS_PER_GROUP, dtype=xf.dtype) * uv[..., None], axis=2)
        w = (macro_full[:, :, None] * micro_full).reshape(T, NUM_EXPERTS)
        gate = jax.nn.silu(jnp.einsum('td,edf->tef', xf, gate_w))
        up = jnp.einsum('td,edf->tef', xf, up_w)
        h = gate * up
        out = jnp.einsum('te,tef,efd->td', w, h, down_w)
        return out.reshape(B, S, D)
    h = _L0_tok_ref(x, L0_tok_Wa, L0_tok_ba, L0_tok_Wd1, L0_tok_bd1, L0_tok_Wd2, L0_tok_bd2, L0_tok_Wd3, L0_tok_bd3)
    h = jnp.concatenate([jnp.broadcast_to(cls_tok, (h.shape[0], 1, h.shape[2])), h], axis=1)
    h = h + _L0_attn_ref(_layernorm(h, axis=-1), L0_attn_W_qkv, L0_attn_W_r, L0_attn_W_o, L0_attn_u, L0_attn_v, L0_attn_ln1_g, L0_attn_ln1_b, L0_attn_W_ff1, L0_attn_b_ff1, L0_attn_W_ff2, L0_attn_b_ff2, L0_attn_ln2_g, L0_attn_ln2_b)
    h = h + _L0_ffn_ref(_layernorm(h, axis=-1), L0_ffn_macro_w, L0_ffn_micro_w, L0_ffn_gate_w, L0_ffn_up_w, L0_ffn_down_w)
    return h

_drawn_inputs = setup_inputs


def setup_inputs(seed=0):
    import zlib

    import numpy as np

    out = dict(_drawn_inputs(seed))
    spreads = {'L0_tok_bd1': (0.0, 0.8),
     'L0_tok_bd2': (0.0, 0.8),
     'L0_tok_bd3': (0.0, 0.8),
     'L0_attn_ln1_g': (1.0, 0.2),
     'L0_attn_ln1_b': (0.0, 0.1),
     'L0_attn_b_ff1': (0.0, 0.1),
     'L0_attn_b_ff2': (0.0, 0.1),
     'L0_attn_ln2_g': (1.0, 0.2),
     'L0_attn_ln2_b': (0.0, 0.1)}
    factors = {'cls_tok': 12.459,
     'L0_attn_W_r': 8.0,
     'L0_attn_u': 64.0,
     'L0_attn_v': 8.0,
     'L0_ffn_macro_w': 5.516,
     'L0_ffn_micro_w': 8.0,
     'L0_ffn_gate_w': 4.006,
     'L0_ffn_up_w': 3.969,
     'L0_ffn_down_w': 4.011}
    for name, (base, spread) in spreads.items():
        noise = np.random.default_rng([zlib.crc32(name.encode()), seed]).standard_normal(out[name].shape)
        drawn = base * np.exp(spread * noise) if base else spread * noise
        out[name] = jnp.asarray(drawn.astype(out[name].dtype))
    for name, factor in factors.items():
        out[name] = (out[name] * factor).astype(out[name].dtype)
    return out
```

```python
from contextlib import ExitStack

import numpy as np

import concourse.bass as bass
from concourse import mybir

F32 = mybir.dt.float32
F16 = mybir.dt.float16
ALU = mybir.AluOpType
ACT = mybir.ActivationFunctionType
AX = mybir.AxisListType

P = 128
B = 8
IMG = 256
D = IMG
KC = D // P
S = IMG + 1
CLS = IMG
L, H, DH, DF = 4, 16, 64, 1024
HD = H * DH
NP = HD // P
QT = 2
FC = DF // P
EPS = 1e-5
WS = 16.0
NT = B * QT + 1
E_N, E_F, E_G, E_K = 8, 512, 4, 2
EFC = E_F // P
TOKENS = B * S

C_QKV, C_R, C_O, C_1, C_2 = 0, 6144, 8192, 10240, 12288
W_COLS = 14336
E_COLS = 3072
SPLIT = 256

G1, B1, G2, B2, BF2, BF1 = 0, 2, 4, 6, 8, 10
PAR_COLS = 18


def const_arrays():
    pos = np.arange(S - 1, -1, -1, dtype=np.float32)
    freq = (np.float32(1.0) / np.power(np.float32(10000.0), np.arange(0, D, 2, dtype=np.float32) / np.float32(D))).astype(np.float32)
    ang = pos[:, None] * freq[None, :]
    r = np.concatenate([np.sin(ang), np.cos(ang)], axis=-1).astype(np.float32)
    r = np.concatenate([r[1:], r[:1]], axis=0)
    rT = np.ascontiguousarray(r.T.reshape(KC, P, S).transpose(1, 0, 2))
    p = np.arange(P)
    head = 2 * np.arange(NP)[None, :] + (p[:, None] >= DH)
    hmask = (head[:, :, None] == np.arange(H)[None, None, :]).astype(np.float32)
    sel = np.zeros((P, NP, P), np.float32)
    for c in range(NP):
        for m in range(P):
            sel[2 * c + (m >= DH), c, m] = 1.0
    return {"c_rT": rT, "c_hmask": hmask, "c_sel": sel, "c_ident": np.eye(P, dtype=np.float32)}


def token_stage(nc, io, keep):
    with ExitStack() as ctx:
        sb = lambda n, s, d=F32: ctx.enter_context(nc.sbuf_tensor(n, s, d))
        sem = lambda n: ctx.enter_context(nc.semaphore(n))
        img = sb("img", [P, B, 8, 64])
        wd = [sb("wd_l1", [P, 384, 3]), sb("wd_l2", [P, 96, 3]), sb("wd_l3", [P, 24, 3])]
        wa = sb("wa", [P, 8])
        bias = sb("gate_bias", [P, 10])
        scale = sb("gate_scale", [P, 10])
        half = sb("half", [P, 2, B, 8, 32])
        det = [sb("det1", [P, B, 3, 128]), sb("det2", [P, B, 3, 32]), sb("det3", [P, B, 3, 8])]
        app = [sb("app1", [P, B, 4, 32]), sb("app2", [P, B, 2, 16]), sb("app3", [P, B, 1, 8])]
        junk = sb("junk", [P, 384])
        part = sb("part", [P, B, 10])
        z = sb("z", [P, B, 10])
        top = sb("top", [P, B, 3])
        e = sb("e", [P, B, 10])
        den = sb("den", [P, B, 4])
        gate = sb("gate", [P, B, 10])
        ones = sb("ones", [P, P])
        xt = sb("xt", [P, NT, D])
        stats = sb("stats", [P, NT, 6])
        mv = sb("mv", [P, NT, 2])
        rstd = sb("rstd", [P, 3, NT])
        hs = sb("hs", [P, B, 2, KC, S], F16)
        wst = sb("wst", [P, 2, 2048])
        cls_row = sb("cls_row", [B, D])
        bank = [ctx.enter_context(nc.psum_tensor(f"ta{i}", [P, 512], F32)) for i in range(8)]
        ident = keep["ident"]

        img_in, wd_in, small_in = sem("img_in"), sem("wd_in"), sem("small_in")
        dve = sem("dve_step")
        const_ok, part_ok, tot_ok, logit_ok, exp_ok, rec_ok = map(sem, (
            "const_ok", "part_ok", "tot_ok", "logit_ok", "exp_ok", "rec_ok"))
        h0_out, h0_in, var_ok, ln_ok, y0_ok, xn_ok = map(sem, (
            "h0_out", "h0_in", "var_ok", "ln_ok", "y0_ok", "xn_ok"))
        tr_ok, hi_ok, lo_ok, hd_out = map(sem, ("tr_ok", "hi_ok", "lo_ok", "hd_out"))
        w_in = [sem("w_in0"), sem("w_in1")]
        w_hi, w_lo = map(sem, ("w_hi", "w_lo"))
        NW = W_COLS // 2048
        block = ctx.enter_context(nc.Block())

        @block.sync
        def _(sp):
            sp.dma_start(img[:, :, :, :], io["x"]).then_inc(img_in, 16)
            for i, n in enumerate(("wd3", "wd2", "wd1")):
                sp.dma_start(wd[i][:, :, :], io[n]).then_inc(wd_in, 16)
            sp.dma_start(wa[:, :], io["wa"]).then_inc(wd_in, 16)
            sp.dma_start(bias[:, :], io["gate_bias"].partition_broadcast(P)).then_inc(wd_in, 16)
            sp.dma_start(ident[:, :], io["c_ident"]).then_inc(small_in, 16)
            sp.dma_start(cls_row[:, :], io["cls_tok"].partition_broadcast(B)).then_inc(small_in, 16)
            for i in range(NW):
                if i >= 2:
                    sp.wait_ge(w_lo, i - 1)
                sp.dma_start(wst[:, i % 2, :], io["w"][0, :, i * 2048:(i + 1) * 2048]).then_inc(w_in[i % 2], 16)
            sp.wait_ge(small_in, 32)
            sp.dma_start(io["h0"][B * IMG:TOKENS, :], cls_row[:, :]).then_inc(h0_out, 16)
            sp.wait_ge(rec_ok, 1)
            for b in range(B):
                for cg in range(4):
                    sp.dma_start(
                        io["h0"][b * IMG:(b + 1) * IMG, cg * 64:(cg + 1) * 64].rearrange("(br r) c -> br r c", r=8),
                        img[cg * 32:(cg + 1) * 32, b, :, :]).then_inc(h0_out, 16)
            sp.wait_ge(h0_out, 16 * (1 + 4 * B))
            sp.dma_start(xt[:, 0:NT - 1, :], io["h0"][0:B * IMG, :].rearrange("(t p) d -> p t d", p=P)).then_inc(h0_in, 16)
            sp.dma_start(xt[0:B, NT - 1, :], io["h0"][B * IMG:TOKENS, :]).then_inc(h0_in, 16)
            sp.wait_ge(lo_ok, B + 1)
            sp.dma_start(io["hd"].rearrange("b p n -> p b n"), hs[:, :, :, :, :].rearrange("p b t k s -> p b (t k s)")).then_inc(hd_out, 16)
            sp.wait_ge(hd_out, 16)

        @block.gpsimd
        def _(pool):
            pool.memset(ones[:, :], 1.0).then_inc(const_ok, 1)
            for a, b_, v in ((0, 1, -0.125), (1, 4, 0.125), (4, 7, 0.25), (7, 10, 0.5)):
                pool.memset(scale[:, a:b_], v).then_inc(const_ok, 1)
            pool.memset(mv[:, :, :], 1.0).then_inc(const_ok, 1)

        @block.scalar
        def _(act):
            nc.scalar.preload_act_table_set("natural_log_exp_and_others")
            for i in range(NW):
                act.wait_ge(w_in[i % 2], 16 * (i // 2 + 1))
                act.activation(keep["w"][:, 0, i * 2048:(i + 1) * 2048], wst[:, i % 2, :], ACT.Copy, scale=WS).then_inc(w_hi, 1)
            act.wait_ge(logit_ok, 1)
            act.activation(e[:, :, :], z[:, :, :], ACT.Exp).then_inc(exp_ok, 1)
            act.wait_ge(var_ok, 1)
            act.activation(rstd[:, 0, :], rstd[:, 2, :], ACT.Ln).then_inc(ln_ok, 1)
            act.wait_ge(ln_ok, 1)
            act.activation(rstd[:, 1, :], rstd[:, 0, :], ACT.Exp, scale=-0.5).then_inc(y0_ok, 1)
            for b in range(B + 1):
                act.wait_ge(tr_ok, b + 1)
                if b < B:
                    dst, src = hs[:, b, 0, :, 0:IMG], bank[b][:, :].rearrange("p (k s) -> p k s", k=KC)
                else:
                    dst, src = hs[:, :, 0, :, CLS].rearrange("p b k -> p k b"), bank[0][:, 0:KC * B].rearrange("p (k b) -> p k b", k=KC)
                act.activation(dst, src, ACT.Copy).then_inc(hi_ok, 1)

        @block.vector
        def _(v):
            n = [0]

            def step(ins, wait=True):
                ins.then_inc(dve, 1)
                n[0] += 1
                if wait:
                    v.wait_ge(dve, n[0])

            def split_weights(i):
                v.wait_ge(w_hi, i + 1)
                c = slice(i * 2048, (i + 1) * 2048)
                v.scalar_tensor_tensor(keep["w"][:, 1, c], wst[:, i % 2, :], WS, keep["w"][:, 0, c],
                                       ALU.mult, ALU.subtract).then_inc(w_lo, 1)

            v.wait_ge(img_in, 16)
            src = img[:, :, :, :]
            for lv in range(3):
                r, c = 8 >> lv, 32 >> lv
                lo, hi = half[:, 0, :, 0:r, 0:c], half[:, 1, :, 0:r, 0:c]
                step(v.tensor_tensor(lo, src[:, :, :, 0:2 * c:2], src[:, :, :, 1:2 * c:2], ALU.add), False)
                step(v.tensor_tensor(hi, src[:, :, :, 0:2 * c:2], src[:, :, :, 1:2 * c:2], ALU.subtract))
                d = det[lv][:, :, :, :].rearrange("p b k (r c) -> p b k r c", c=c)
                for out, x, op in ((app[lv][:, :, :, :], lo, ALU.add), (d[:, :, 0], lo, ALU.subtract),
                                   (d[:, :, 1], hi, ALU.add), (d[:, :, 2], hi, ALU.subtract)):
                    step(v.tensor_tensor(out, x[:, :, 0:r:2, :], x[:, :, 1:r:2, :], op), False)
                v.wait_ge(dve, n[0])
                src = app[lv][:, :, :, :]
                split_weights(2 * lv)
                split_weights(2 * lv + 1)
            split_weights(6)
            v.wait_ge(wd_in, 16 * 5)
            for b in range(B):
                for col, a, w in [(0, app[2][:, b, 0, :], wa[:, :])] + [
                        (1 + 3 * (2 - lv) + k, det[lv][:, b, :, :].rearrange("p k n -> p (k n)"), wd[lv][:, :, k])
                        for lv in range(3) for k in range(3)]:
                    step(v.tensor_tensor_reduce(junk[:, 0:a.shape[1]], a, w, 1.0, 0.0, ALU.mult, ALU.add,
                                                part[:, b, col:col + 1]))
            v.sem_inc(part_ok, 1)
            v.wait_ge(tot_ok, 1)
            v.wait_ge(const_ok, 6)
            bc = lambda t, m: t.unsqueeze(1).broadcast_to([P, B, m])
            step(v.tensor_tensor(z[:, :, :], bank[0][:, 0:B * 10].rearrange("p (b m) -> p b m", m=10), bc(scale[:, :], 10), ALU.mult))
            step(v.tensor_scalar(bias[:, 0:1], bias[:, 0:1], -1.0, None, ALU.mult))
            step(v.tensor_tensor(z[:, :, :], z[:, :, :], bc(bias[:, :], 10), ALU.add))
            z3 = z[:, :, 1:10].rearrange("p b (l k) -> p b l k", k=3)
            step(v.tensor_reduce(top[:, :, :], z3, AX.X, ALU.max))
            v.tensor_tensor(z3, z3, top[:, :, :].unsqueeze(3).broadcast_to([P, B, 3, 3]), ALU.subtract).then_inc(logit_ok, 1)
            v.wait_ge(exp_ok, 1)
            step(v.tensor_scalar(den[:, :, 0:1], e[:, :, 0:1], 1.0, None, ALU.add), False)
            step(v.tensor_reduce(den[:, :, 1:4], e[:, :, 1:10].rearrange("p b (l k) -> p b l k", k=3), AX.X, ALU.add))
            step(v.memset(e[:, :, 0:1], 1.0))
            step(v.reciprocal(den[:, :, :], den[:, :, :]))
            for i, f in ((0, 1 / 64), (1, 1 / 64), (2, 1 / 16), (3, 1 / 4)):
                step(v.tensor_scalar(den[:, :, i:i + 1], den[:, :, i:i + 1], f, None, ALU.mult), False)
            v.wait_ge(dve, n[0])
            step(v.tensor_tensor(gate[:, :, 0:1], e[:, :, 0:1], den[:, :, 0:1], ALU.mult), False)
            step(v.tensor_tensor(gate[:, :, 1:10].rearrange("p b (l k) -> p b l k", k=3),
                                 e[:, :, 1:10].rearrange("p b (l k) -> p b l k", k=3),
                                 den[:, :, 1:4].unsqueeze(3).broadcast_to([P, B, 3, 3]), ALU.mult))
            a3 = app[2][:, :, 0, :]
            step(v.tensor_tensor(a3, a3, gate[:, :, 0:1].broadcast_to([P, B, 8]), ALU.mult), False)
            for lv in range(3):
                g = gate[:, :, 1 + 3 * (2 - lv):4 + 3 * (2 - lv)]
                m = (4 >> lv) * (32 >> lv)
                step(v.tensor_tensor(det[lv][:, :, :, :], det[lv][:, :, :, :], g.unsqueeze(3).broadcast_to([P, B, 3, m]), ALU.mult), False)
            v.wait_ge(dve, n[0])
            for lv in (2, 1, 0):
                r, c = 8 >> lv, 32 >> lv
                lo, hi = half[:, 0, :, 0:r, 0:c], half[:, 1, :, 0:r, 0:c]
                d = det[lv][:, :, :, :].rearrange("p b k (r c) -> p b k r c", c=c)
                a = app[lv][:, :, :, :]
                for out, x, y in ((lo, a, d[:, :, 0]), (hi, d[:, :, 1], d[:, :, 2])):
                    step(v.tensor_tensor(out[:, :, 0:r:2, :], x, y, ALU.add), False)
                    step(v.tensor_tensor(out[:, :, 1:r:2, :], x, y, ALU.subtract), False)
                v.wait_ge(dve, n[0])
                dst = img[:, :, :, :] if lv == 0 else app[lv - 1][:, :, :, :]
                step(v.tensor_tensor(dst[:, :, :, 0:2 * c:2], lo, hi, ALU.add), False)
                step(v.tensor_tensor(dst[:, :, :, 1:2 * c:2], lo, hi, ALU.subtract))
            v.sem_inc(rec_ok, 1)
            v.wait_ge(h0_in, 32)
            layer_norm_rows(v, step, xt, xt, stats, mv, rstd, var_ok, y0_ok)
            v.sem_inc(xn_ok, 1)
            for b in range(B + 1):
                v.wait_ge(hi_ok, b + 1)
                if b < B:
                    dst, hi, src = hs[:, b, 1, :, 0:IMG], hs[:, b, 0, :, 0:IMG], bank[b][:, :].rearrange("p (k s) -> p k s", k=KC)
                else:
                    q = lambda t: hs[:, :, t, :, CLS].rearrange("p b k -> p k b")
                    dst, hi, src = q(1), q(0), bank[0][:, 0:KC * B].rearrange("p (k b) -> p k b", k=KC)
                v.tensor_tensor(dst, src, hi, ALU.subtract).then_inc(lo_ok, 1)
            v.wait_ge(lo_ok, B + 1)
            for t in range(2):
                step(v.tensor_copy(keep["hcls"][:, t, :, :], hs[:, :, t, :, CLS].rearrange("p b k -> p k b")))

        @block.tensor
        def _(pe):
            pe.wait_ge(const_ok, 6)
            pe.wait_ge(part_ok, 1)
            pe.matmul(bank[0][:, 0:B * 10], ones[:, :], part[:, :, :].rearrange("p b m -> p (b m)"), start=True, stop=True).then_inc(tot_ok, 1)
            pe.wait_ge(small_in, 32)
            pe.wait_ge(xn_ok, 1)
            for b in range(B):
                for k in range(KC):
                    for j in range(QT):
                        t = pe.transpose(bank[b][:, (k * QT + j) * P:(k * QT + j + 1) * P], xt[:, QT * b + j, k * P:(k + 1) * P], ident[:, :])
                t.then_inc(tr_ok, 1)
            pe.wait_ge(lo_ok, 1)
            for k in range(KC):
                t = pe.transpose(bank[0][:, k * B:(k + 1) * B], xt[0:B, NT - 1, k * P:(k + 1) * P], ident[0:B, 0:B])
            t.then_inc(tr_ok, 1)


def layer_norm_rows(v, step, x, out, stats, mv, rstd, var_ok, y0_ok):
    rows = lambda t: P if t < NT - 1 else B
    for t in range(NT):
        step(v.bn_stats(stats[0:rows(t), t, :], x[0:rows(t), t, :]), t == NT - 1)
    for t in range(NT):
        step(v.bn_aggr(mv[0:rows(t), t, :], stats[0:rows(t), t, :]), t == NT - 1)
    var, y, y2 = rstd[:, 2, :], rstd[:, 1, :], rstd[:, 0, :]
    step(v.tensor_scalar(var, mv[:, :, 1], EPS, None, ALU.add))
    v.sem_inc(var_ok, 1)
    v.wait_ge(y0_ok, 1)
    step(v.tensor_tensor(y2, y, y, ALU.mult))
    step(v.tensor_tensor(y2, y2, var, ALU.mult))
    step(v.tensor_scalar(y2, y2, -0.5, 1.5, ALU.mult, ALU.add))
    step(v.tensor_tensor(y, y, y2, ALU.mult))
    for t in range(NT):
        step(v.tensor_scalar(out[0:rows(t), t, :], x[0:rows(t), t, :], mv[0:rows(t), t, 0:1], rstd[0:rows(t), 1, t:t + 1],
                             ALU.subtract, ALU.mult), t == NT - 1)


class At:

    def __init__(self, eng, g):
        self.eng, self.g, self.kept = eng, g, {}

    def __call__(self, per, off):
        if isinstance(self.g, int):
            return per * self.g + off
        if per not in self.kept:
            self.kept[per] = self.eng.snap(self.g * per)
        return self.kept[per] + off if off else self.kept[per]

    def now(self, per, off, reg):
        value = self(per, off)
        if isinstance(value, int):
            return value
        self.eng.reg_mov(reg, value)
        return reg

    def prepare(self, *pers):
        for per in pers:
            self(per, 0)


VBD_IMAGE = H * (2 * HD + DH)


def vbd_rows(vbd, b):
    return vbd[b, 0:H * 2 * HD].rearrange("(h n) -> h n", h=H)


def vbd_diagonal(vbd, t):
    return vbd.rearrange("b (h n) -> b h n", h=H)[:, :, t * HD:t * HD + DH]


def iterations(eng, body, layer_start, layer_end):
    with eng.Fori(0, L) as l:
        l8 = eng.snap(l * B)
        layer_start(l, At(eng, l8), At(eng, l))
        body(At(eng, l8), 0, True, False)
        with eng.Fori(1, B - 1) as b:
            g = eng.snap(l8 + b)
            body(At(eng, g), b, False, False)
        last = eng.snap(l8 + (B - 1))
        body(At(eng, last), B - 1, False, True)
        layer_end(At(eng, eng.snap(l8 + B)), l)


def attention_stage(nc, io, keep):
    with ExitStack() as ctx:
        sb = lambda n, s, d=F32: ctx.enter_context(nc.sbuf_tensor(n, s, d))
        sem = lambda n: ctx.enter_context(nc.semaphore(n))
        W, ident, hcls = keep["w"], keep["ident"], keep["hcls"]
        par = sb("par", [P, PAR_COLS])
        uv = sb("uv", [P, 2, NP])
        u16 = sb("u16", [P, NP])
        hmask = sb("hmask", [P, NP, H])
        wm = sb("wm", [P, NP, H])
        rT2 = sb("rT2", [P, 2, KC, S], F16)
        kr16 = sb("kr16", [P, NP, S])
        cc = sb("cc", [H, S])
        cb = sb("cb", [P, H, S])
        hin = sb("hin", [P, 2, KC, S], F16)
        hres = sb("hres", [P, 2, KC, S], F16)
        hmid = hres
        hout = sb("hout", [P, 2, KC, S], F16)
        rq = sb("rq", [P, 2, NP, S], F16)
        rk = sb("rk", [P, 2, NP, S], F16)
        qs = sb("qs", [P, H, S], F16)
        kh = sb("kh", [P, H, S], F16)
        kl = sb("kl", [P, H, S], F16)
        qbd = sb("qbd", [P, H, H], F16)
        vs = sb("vs", [P, 2, QT, HD], F16)
        vbd = sb("vbd", [P, 2, HD], F16)
        E = sb("E", [P, 2, QT, S])
        ec = sb("ec", [H, S])
        nb = sb("nb", [P, QT * H])
        nbc = sb("nbc", [H, 1])
        sums = sb("sums", [P, QT, H])
        sumc = sb("sumc", [H, 1])
        rs = sb("rs", [P, QT, H])
        ecr = sb("ecr", [H, 2, 1])
        ecol = sb("ecol", [P, QT, H])
        pt = sb("pt", [P, H, 2, QT, S], F16)
        hid = pt[:, 0:4, :, :, :].rearrange("p h t k s -> p (h t k s)").rearrange("p (t f s) -> p t f s", t=2, f=FC)
        pkr = sb("pkr", [P, 2, 2, S], F16)
        sel = sb("sel", [P, NP, P], F16)
        ident16 = sb("ident16", [P, P], F16)
        mean_w = sb("mean_w", [P, P])
        o2 = sb("o2", [P, 2, NP, S], F16)
        vcl = o2[0:B, :, :, :].rearrange("b t c s -> b (t c s)")[:, 0:2 * HD].rearrange("b (t n) -> b t n", t=2)
        x = sb("x", [P, KC, S])
        sq = sb("sq", [P, KC, S])
        y = sb("y", [P, S])
        t1 = sb("t1", [P, S])
        rel = sb("rel", [P, 2, S])
        eps = sb("eps", [P, 1])
        wf = sb("wf", [P, 2, SPLIT])
        wh = sb("wh", [P, 2, 2, SPLIT], F16)
        bank = [ctx.enter_context(nc.psum_tensor(f"bk{i}", [P, 512], F32)) for i in range(8)]
        ident_s = ident[0:H, 0:H]

        w_names = ("w_qkv_in", "w_r_in", "w_o_in", "w_1_in", "w_2_in")
        w_sem = {n: sem(n) for n in w_names}
        const_in, const_ok, par_in, setup_ok = map(sem, ("const_in", "const_ok2", "par_in", "setup_ok"))
        zero_out, hin_in, hres_in, vbd_in, stack_in, hd_out, vbd_out = map(sem, ("zero_out", "hin_in", "hres_in", "vbd_in", "stack_in", "hd_out2", "vbd_out"))
        vcls_done, kr_done, cc_done, cb_done = map(sem, ("vcls_done", "kr_done", "cc_done", "cb_done"))
        proj_done, v_done = sem("proj_done"), sem("v_done")
        cs_done, s_done, t_done, clst_done, key_done = map(sem, ("cs_done", "s_done", "t_done", "clst_done", "key_done"))
        rb_done, o_done, wo_done, mean_done, var_done, ff1_done, ff2_done = map(sem, (
            "rb_done", "o_done", "wo_done", "mean_done", "var_done", "ff1_done", "ff2_done"))
        vcls_hi, kr_ok, proj_hi, v_hi = map(sem, ("vcls_hi", "kr_ok", "proj_hi", "v_hi"))
        e_ok, ec_ok, p_hi, pc_hi, key_hi, rb_ok, o_hi = map(sem, ("e_ok", "ec_ok", "p_hi", "pc_hi", "key_hi", "rb_ok", "o_hi"))
        x_ok, sq_ok, lnv_ok, y0_ok, z_hi, relu_ok, ff1_hi = map(sem, ("x_ok", "sq_ok", "lnv_ok", "y0_ok2", "z_hi", "relu_ok", "ff1_hi"))
        wm_ok, cc_ok, cb_ok, vcls_lo, k_sum, proj_lo, v_lo = map(sem, ("wm_ok", "cc_ok", "cb_ok", "vcls_lo", "k_sum", "proj_lo", "v_lo"))
        qbd_ok, sc_ok, s_ok, ecol_ok, p_lo, pc_lo, rs_ok, key_lo, on_ok, o_lo = map(sem, (
            "qbd_ok", "sc_ok", "s_ok", "ecol_ok", "p_lo", "pc_lo", "rs_ok", "key_lo", "on_ok", "o_lo"))
        xc_ok, newton, z_ok, z_lo, hcls_ok, ff1_lo = map(sem, ("xc_ok", "newton", "z_ok", "z_lo", "hcls_ok", "ff1_lo"))
        split_in = [sem("split_in0"), sem("split_in1")]
        split_out = [sem("split_out0"), sem("split_out1")]
        scaled, split_hi, split_lo, prep_ok = map(sem, ("scaled", "split_hi", "split_lo", "prep_ok"))
        SETUP = 8
        SCORE = 1.0 / (DH ** 0.5 * WS * WS)
        block = ctx.enter_context(nc.Block())

        TERMS = ((0, 0), (0, 1), (1, 0))
        wcol = lambda t, base, k, n, m: W[:, t, base + k * n + m * P:base + k * n + (m + 1) * P]

        @block.sync
        def _(sp):
            for dst, n in ((hmask[:, :, :], "c_hmask"), (x[:, :, :], "c_rT"), (uv[:, :, :], "uv")):
                sp.dma_start(dst, io[n]).then_inc(const_in, 16)
            sp.dma_start(cb[:, 0:4, :].rearrange("p h s -> p (h s)")[:, 0:NP * P], io["c_sel"].rearrange("p c m -> p (c m)")).then_inc(const_in, 16)

            sp.wait_ge(const_ok, 5)
            for b in range(B):
                sp.dma_start(vbd_rows(io["vbd"], b), vbd[0:H, :, :].rearrange("h t n -> h (t n)")).then_inc(zero_out, 16)
            sp.wait_ge(zero_out, 16 * B)

            count = sp.alloc_register("sp_count")

            def stack(at):
                used = at.now(32, 0, count)
                sp.wait_ge(proj_lo, at(16, 16))
                sp.wait_ge(s_done, used)
                for a in range(2):
                    rows = slice(64 * a, 64 * a + 64)
                    for dst, src, lo in ((qs, rq, (0, 1)), (kh, rk, (0, 0)), (kl, rk, (1, 1))):
                        for half in range(2):
                            sp.dma_start(dst[64 * half:64 * half + 64, a:H:2, :], src[rows, lo[half], :, :]).then_inc(stack_in, 16)

            def body(at, b, first, last):
                at.prepare(4, 8, 16)
                if not last:
                    at1 = At(sp, at.g + 1)
                    at1.prepare(16, 32)
                sp.wait_ge(o_done, at(8, 0))
                sp.dma_start(vbd[0:H, :, :].rearrange("h t n -> h (t n)"), vbd_rows(io["vbd"], b)).then_inc(vbd_in, 16)
                sp.wait_ge(ff1_done, at(8, 0))
                sp.dma_start(hres[:, :, :, :].rearrange("p t k s -> p (t k s)"), io["hd"][b]).then_inc(hres_in, 16)
                if not last:
                    sp.wait_ge(v_done, at(4, 4))
                    sp.dma_start(hin[:, :, :, :].rearrange("p t k s -> p (t k s)"), io["hd"][b + 1]).then_inc(hin_in, 16)
                if not first:
                    store(at(4, 0), at(16, -16), b - 1)
                if not last:
                    stack(at1)

            def store(z_count, stored, b):
                sp.wait_ge(z_lo, z_count)
                if not (isinstance(stored, int) and stored <= 0):
                    sp.wait_ge(hd_out, stored)
                sp.dma_start(io["hd"][b], hout[:, :, :, :].rearrange("p t k s -> p (t k s)")).then_inc(hd_out, 16)

            def load_w(name, a, b, l):
                sp.dma_start(W[:, :, a:b], io["w_split"][l, :, :, a:b]).then_inc(w_sem[name], 16)

            for l in range(L):
                g = l * B
                at = At(sp, g)
                if l:
                    sp.wait_ge(z_lo, 4 * g)
                sp.dma_start(par[:, :], io["par"][l]).then_inc(par_in, 16)
                if l:
                    sp.wait_ge(v_done, 4 * g)
                    sp.wait_ge(hd_out, 16 * g)
                sp.dma_start(hin[:, :, :, :].rearrange("p t k s -> p (t k s)"), io["hd"][0]).then_inc(hin_in, 16)
                sp.wait_ge(vcls_lo, 2 * (l + 1))
                for t in range(2):
                    sp.dma_start(vbd_diagonal(io["vbd"], t), vcl[:, t, :].rearrange("b (h d) -> b h d", h=H)).then_inc(vbd_out, 16)
                stack(at)
                sp.wait_ge(vbd_out, 32 * (l + 1))
                body(At(sp, g), 0, True, False)
                with sp.Fori(1, B - 1) as b:
                    body(At(sp, sp.snap(b + g)), b, False, False)
                body(At(sp, g + B - 1), B - 1, False, True)
                if l + 1 < L:
                    sp.wait_ge(prep_ok, l + 1)
                    load_w("w_qkv_in", C_QKV, C_R, l + 1)
                    load_w("w_r_in", C_R, C_O, l + 1)
                    sp.wait_ge(wo_done, 2 * (g + B))
                    load_w("w_o_in", C_O, C_1, l + 1)
                    sp.wait_ge(ff1_done, 8 * (g + B))
                    load_w("w_1_in", C_1, C_2, l + 1)
                    sp.wait_ge(ff2_done, 2 * (g + B))
                    load_w("w_2_in", C_2, W_COLS, l + 1)
                store(4 * (g + B), 16 * (g + B - 1), B - 1)
            sp.wait_ge(hd_out, 16 * L * B)

        @block.gpsimd
        def _(pool):
            pool.memset(mean_w[:, :], 1.0 / D).then_inc(const_ok, 1)
            pool.memset(qbd[:, :, :], 0.0).then_inc(const_ok, 1)
            pool.memset(vbd[:, :, :], 0.0).then_inc(const_ok, 1)
            pool.memset(pkr[:, :, :, :], 0.0).then_inc(const_ok, 1)
            pool.memset(eps[:, :], EPS).then_inc(const_ok, 1)

            in_count, out_count, step_count = (pool.alloc_register(f"pool_{n}_count") for n in ("in", "out", "step"))

            def pair(src, dst, n):
                for i in range(2):
                    pool.dma_start(wf[:, i, :], src(i)).then_inc(split_in[i], 16)
                for i in range(2):
                    pool.reg_mov(in_count, n * 16 + 16)
                    pool.reg_mov(out_count, n * 16)
                    pool.reg_mov(step_count, n * 2 + (i + 1))
                    pool.wait_ge(const_ok, 5)
                    pool.wait_ge(split_in[i], in_count)
                    pool.tensor_scalar(wf[:, i, :], wf[:, i, :], WS, 1.0, ALU.mult, ALU.mult).then_inc(scaled, 1)
                    pool.wait_ge(const_ok, 5)
                    pool.wait_ge(scaled, step_count)
                    pool.wait_ge(split_out[i], out_count)
                    pool.tensor_copy(wh[:, i, 0, :], wf[:, i, :]).then_inc(split_hi, 1)
                    pool.wait_ge(split_hi, n * 2 + (i + 1))
                    pool.tensor_tensor(wh[:, i, 1, :], wf[:, i, :], wh[:, i, 0, :], ALU.subtract).then_inc(split_lo, 1)
                    pool.wait_ge(split_lo, n * 2 + (i + 1))
                    pool.dma_start(dst(i), wh[:, i, :, :]).then_inc(split_out[i], 16)

            per_l, per_e = W_COLS // (2 * SPLIT), E_COLS // (2 * SPLIT)
            with pool.Fori(1, L) as l:
                with pool.Fori(0, per_l) as j:
                    n = pool.snap((l - 1) * per_l + j)
                    c = pool.snap(j * (2 * SPLIT))
                    pair(lambda i: io["w"][l, :, bass.ds(c + i * SPLIT, SPLIT)],
                         lambda i: io["w_split"][l, :, :, bass.ds(c + i * SPLIT, SPLIT)], n)
                done = pool.snap(l * per_l)
                for i in range(2):
                    pool.wait_ge(split_out[i], done * 16)
                pool.sem_inc(prep_ok, 1)
            with pool.Fori(0, E_N) as e:
                with pool.Fori(0, per_e) as j:
                    n = pool.snap(e * per_e + j + (L - 1) * per_l)
                    c = pool.snap(j * (2 * SPLIT))
                    pair(lambda i: io["we"][e, :, bass.ds(c + i * SPLIT, SPLIT)],
                         lambda i: io["we_split"][e, :, :, bass.ds(c + i * SPLIT, SPLIT)], n)
            for i in range(2):
                pool.wait_ge(split_out[i], 16 * ((L - 1) * per_l + E_N * per_e))

        @block.tensor
        def _(pe):
            mm = pe.matmul

            def project(at, j):
                if j >= 2:
                    pe.wait_ge(proj_lo, at(16, j - 1))
                for i, (k, (a, m)) in enumerate((k, t) for k in range(KC) for t in TERMS):
                    r = mm(bank[4 + j % 2][:, 0:S], wcol(a, C_QKV, k, 3 * HD, j), hin[:, m, k, :], start=i == 0, stop=i == 5)
                r.then_inc(proj_done, 1)

            def project_v(at, u):
                if u >= 2:
                    pe.wait_ge(v_lo, at(4, u - 1))
                tt, half = divmod(u, 2)
                c0 = C_QKV + 2 * HD + half * 512
                for i, (k, (a, m)) in enumerate((k, t) for k in range(KC) for t in TERMS):
                    r = mm(bank[6 + u % 2][:, :], hin[:, m, k, tt * P:(tt + 1) * P],
                           W[:, a, c0 + k * 3 * HD:c0 + k * 3 * HD + 512], start=i == 0, stop=i == 5)
                r.then_inc(v_done, 1)

            def mean_of(at, call, bk):
                pe.wait_ge(x_ok, at(4, 2 * call + 2))
                for k in range(KC):
                    r = mm(bank[bk][:, 0:S], mean_w[:, :], x[:, k, :], start=k == 0, stop=k == KC - 1)
                r.then_inc(mean_done, 1)

            def var_of(at, call, bk):
                pe.wait_ge(sq_ok, at(4, 2 * call + 2))
                for k in range(KC):
                    r = mm(bank[bk][:, 0:S], mean_w[:, :], sq[:, k, :], start=k == 0, stop=k == KC - 1)
                r.then_inc(var_done, 1)

            pe.wait_ge(const_ok, 5)
            pe.wait_ge(setup_ok, SETUP)

            def layer_start(l, at, atl):
                pe.wait_ge(w_sem["w_qkv_in"], atl(16, 0))
                pe.wait_ge(w_sem["w_r_in"], atl(16, 0))
                pe.wait_ge(hcls_ok, at(1, 0))
                for half in range(2):
                    c0 = C_QKV + 2 * HD + half * 512
                    for i, (k, (a, m)) in enumerate((k, t) for k in range(KC) for t in TERMS):
                        r = mm(bank[6 + half][0:B, :], hcls[:, m, k, :], W[:, a, c0 + k * 3 * HD:c0 + k * 3 * HD + 512],
                               start=i == 0, stop=i == 5)
                    r.then_inc(vcls_done, 1)
                for j in range(NP):
                    if j >= 2:
                        pe.wait_ge(kr_ok, atl(8, j - 1))
                    for i, (k, (a, m)) in enumerate((k, t) for k in range(KC) for t in TERMS):
                        r = mm(bank[j % 2][:, 0:S], wcol(a, C_R, k, HD, j), rT2[:, m, k, :], start=i == 0, stop=i == 5)
                    r.then_inc(kr_done, 1)
                pe.wait_ge(hin_in, atl(16 * B, 16))
                for j in range(2 * NP):
                    project(at, j)
                pe.wait_ge(vcls_lo, atl(2, 2))
                for u in range(4):
                    project_v(at, u)
                pe.wait_ge(kr_ok, atl(8, 8))
                for c in range(NP):
                    r = mm(bank[2][0:H, 0:S], wm[:, c, :], kr16[:, c, :], start=c == 0, stop=c == NP - 1)
                r.then_inc(cc_done, 1)
                for h in range(H):
                    if h >= 2:
                        pe.wait_ge(cb_ok, atl(16, h - 1))
                    mm(bank[h % 2][:, 0:S], wm[:, h // 2, h:h + 1].broadcast_to([P, P]), kr16[:, h // 2, :],
                       start=True, stop=True).then_inc(cb_done, 1)
                pe.wait_ge(cb_ok, atl(16, 16))
                pe.wait_ge(cc_ok, atl(1, 1))

            def transposes(at, h):
                pe.wait_ge(e_ok, at(32, 2 * h + 2))
                if h >= 2:
                    pe.wait_ge(p_lo, at(16, h - 1))
                for kt in range(QT):
                    for qt in range(QT):
                        r = pe.transpose(bank[2 + h % 2][:, (kt * QT + qt) * P:(kt * QT + qt + 1) * P],
                                         E[:, h % 2, qt, kt * P:(kt + 1) * P], ident[:, :])
                r.then_inc(t_done, 1)

            def body(at, b, first, last):
                at1 = None if last else At(pe, at.g + 1)
                pe.wait_ge(v_lo, at(4, 4))
                if not first:
                    mean_of(at, -1, 7)
                pe.wait_ge(stack_in, at(192, 192))
                pe.wait_ge(qbd_ok, at(1, 1))
                for h in range(H):
                    for i, k_ in enumerate((kh, kl)):
                        r = mm(bank[6][0:H, 0:S], qbd[:, h, :], k_[:, h, :], start=h + i == 0, stop=h + i == H)
                r.then_inc(cs_done, 1)
                if not last:
                    pe.wait_ge(hin_in, at(16, 32))
                for h in range(H):
                    for qt in range(QT):
                        if h:
                            pe.wait_ge(s_ok, at(32, 2 * h + qt - 1))
                        q = qs[:, h, qt * P:(qt + 1) * P]
                        mm(bank[qt][:, 0:S], q, kh[:, h, :], start=True, stop=False)
                        mm(bank[qt][:, 0:S], q, kl[:, h, :], start=False, stop=True).then_inc(s_done, 1)
                    if not last:
                        project(at1, h)
                    if h == 0 and not first:
                        var_of(at, -1, 7)
                    if h:
                        transposes(at, h - 1)
                    if h == 1:
                        pe.wait_ge(setup_ok, SETUP)
                        pe.wait_ge(ec_ok, at(1, 1))
                        pe.wait_ge(sc_ok, at(1, 1))
                        for kt in range(QT):
                            r = pe.transpose(bank[6][:, kt * H:(kt + 1) * H], ec[:, kt * P:(kt + 1) * P], ident_s)
                        r.then_inc(clst_done, 1)
                transposes(at, H - 1)
                pe.wait_ge(ecol_ok, at(16, 16))
                pe.wait_ge(rs_ok, at(3, 3))
                pe.wait_ge(pc_lo, at(1, 1))
                for i, src in enumerate((ecol, rs)):
                    for qt in range(QT):
                        r = pe.transpose(bank[6][0:H, (i * QT + qt) * P:(i * QT + qt + 1) * P], src[:, qt, :], ident[:, :])
                r.then_inc(key_done, 1)
                pe.wait_ge(key_lo, at(2, 2))
                pe.wait_ge(p_lo, at(16, 16))
                pe.wait_ge(vbd_in, at(16, 16))
                if not first:
                    pe.wait_ge(z_lo, at(4, 0))
                for c in range(NP):
                    if c >= 2:
                        pe.wait_ge(rb_ok, at(8, c - 1))
                    for i in range(2):
                        r = mm(bank[c % 2][:, 0:S], sel[:, c, :], pkr[:, i, 1, :], start=i == 0, stop=i == 1)
                    r.then_inc(rb_done, 1)
                    if c >= 2:
                        pe.wait_ge(on_ok, at(8, c - 1))
                    o = bank[6 + c % 2]
                    for i, (a, m) in enumerate(TERMS):
                        mm(o[:, 0:S], vbd[:, a, c * P:(c + 1) * P], pkr[:, m, 0, :], start=i == 0, stop=False)
                    for kt in range(QT):
                        for i, (a, m) in enumerate(TERMS):
                            for s_ in range(2):
                                h = 2 * c + s_
                                r = mm(o[DH * s_:DH * (s_ + 1), 0:S], vs[:, a, kt, h * DH:(h + 1) * DH], pt[:, h, m, kt, :],
                                       start=False, stop=(kt == QT - 1 and i == 2))
                    r.then_inc(o_done, 1)
                pe.wait_ge(hres_in, at(16, 16))
                for m_ in range(KC):
                    for i in range(2):
                        mm(bank[4 + m_][:, 0:S], ident16[:, :], hres[:, i, m_, :], start=i == 0, stop=False)
                    for c in range(NP):
                        if m_ == 0:
                            pe.wait_ge(o_lo, at(8, c + 1))
                        for i, (a, m) in enumerate(TERMS):
                            r = mm(bank[4 + m_][:, 0:S], wcol(a, C_O, c, D, m_), o2[:, m, c, :], start=False, stop=(c == NP - 1 and i == 2))
                    r.then_inc(wo_done, 1)
                if not last:
                    project_v(at1, 0)
                mean_of(at, 0, 2)
                if not last:
                    project_v(at1, 1)
                var_of(at, 0, 3)
                if not last:
                    project_v(at1, 2)
                    project_v(at1, 3)
                pe.wait_ge(z_lo, at(4, 2))
                for j in range(FC):
                    if j >= 2:
                        pe.wait_ge(ff1_hi, at(8, j - 1))
                    for i, (k, (a, m)) in enumerate((k, t) for k in range(KC) for t in TERMS):
                        r = mm(bank[j % 2][:, 0:S], wcol(a, C_1, k, DF, j), hmid[:, m, k, :], start=i == 0, stop=i == 5)
                    r.then_inc(ff1_done, 1)
                for m_ in range(KC):
                    for c in range(FC):
                        if m_ == 0:
                            pe.wait_ge(ff1_lo, at(8, c + 1))
                        for i, (a, m) in enumerate(TERMS):
                            r = mm(bank[4 + m_][:, 0:S], wcol(a, C_2, c, D, m_), hid[:, m, c, :], start=c + i == 0, stop=(c == FC - 1 and i == 2))
                    r.then_inc(ff2_done, 1)

            def layer_end(at, l):
                mean_of(at, -1, 7)
                var_of(at, -1, 7)

            iterations(pe, body, layer_start, layer_end)

        @block.scalar
        def _(act):
            def project_hi(at, j):
                if j < NP:
                    act.wait_ge(proj_done, at(16, j + 1))
                    act.activation(rq[:, 0, j, :], bank[4 + j % 2][:, 0:S], ACT.Identity, bias=u16[:, j:j + 1]).then_inc(proj_hi, 1)
                else:
                    act.wait_ge(k_sum, at(8, j - NP + 1))
                    act.activation(rk[:, 0, j - NP, :], rel[:, j % 2, :], ACT.Copy).then_inc(proj_hi, 1)

            def v_part(at, u):
                act.wait_ge(v_done, at(4, u + 1))
                tt, half = divmod(u, 2)
                act.activation(vs[:, 0, tt, half * 512:half * 512 + 512], bank[6 + u % 2][:, :], ACT.Copy).then_inc(v_hi, 1)

            def squares(at, call):
                for k in range(KC):
                    act.wait_ge(xc_ok, at(4, 2 * call + k + 1))
                    act.activation(sq[:, k, :], x[:, k, :], ACT.Square).then_inc(sq_ok, 1)

            def first_rstd(at, call, bk):
                act.wait_ge(var_done, at(2, call + 1))
                act.activation(y[:, :], bank[bk][:, 0:S], ACT.Ln, bias=eps[:, 0:1]).then_inc(lnv_ok, 1)
                act.wait_ge(lnv_ok, at(2, call + 1))
                act.activation(y[:, :], y[:, :], ACT.Exp, scale=-0.5).then_inc(y0_ok, 1)

            def norm_hi(at, call, dst, beta):
                for k in range(KC):
                    act.wait_ge(z_ok, at(4, 2 * call + k + 1))
                    act.activation(dst[:, 0, k, :], x[:, k, :], ACT.Identity, bias=par[:, beta + k:beta + k + 1]).then_inc(z_hi, 1)

            nc.scalar.preload_act_table_set("natural_log_exp_and_others")
            act.wait_ge(const_ok, 5)
            act.wait_ge(setup_ok, SETUP)

            def layer_start(l, at, atl):
                act.wait_ge(vbd_out, atl(32, 0))
                for half in range(2):
                    act.wait_ge(vcls_done, atl(2, half + 1))
                    act.activation(vcl[:, 0, half * 512:half * 512 + 512], bank[6 + half][0:B, :], ACT.Copy).then_inc(vcls_hi, 1)
                for j in range(NP):
                    act.wait_ge(kr_done, atl(8, j + 1))
                    act.activation(kr16[:, j, :], bank[j % 2][:, 0:S], ACT.Copy).then_inc(kr_ok, 1)
                for j in range(2 * NP):
                    project_hi(at, j)
                for u in range(4):
                    v_part(at, u)
                for h in range(H):
                    act.wait_ge(cb_done, atl(16, h + 1))
                    act.activation(cb[:, h, :], bank[h % 2][:, 0:S], ACT.Copy).then_inc(cb_ok, 1)

            def p_part(at, h):
                act.wait_ge(t_done, at(16, h + 1))
                act.activation(pt[:, h, 0, :, 0:IMG], bank[2 + h % 2][:, :].rearrange("p (k s) -> p k s", k=QT), ACT.Copy).then_inc(p_hi, 1)

            def o_part(at, c):
                act.wait_ge(on_ok, at(8, c + 1))
                act.activation(o2[:, 0, c, :], x[:, c % 2, :], ACT.Copy).then_inc(o_hi, 1)

            def body(at, b, first, last):
                at1 = None if last else At(act, at.g + 1)
                if not first:
                    squares(at, -1)
                act.wait_ge(sc_ok, at(1, 1))
                act.activation(ec[:, :], ec[:, :], ACT.Exp, bias=nbc[:, 0:1], scale=-1.0, accum_out=sumc[:, 0:1]).then_inc(ec_ok, 1)
                for h in range(H):
                    for qt in range(QT):
                        act.wait_ge(s_ok, at(32, 2 * h + qt + 1))
                        act.activation(E[:, h % 2, qt, :], E[:, h % 2, qt, :], ACT.Exp, bias=nb[:, 2 * h + qt:2 * h + qt + 1],
                                       scale=-1.0, accum_out=sums[:, qt, h:h + 1]).then_inc(e_ok, 1)
                    if not last:
                        project_hi(at1, h)
                    if h == 1 and not first:
                        first_rstd(at, -1, 7)
                    if h == 3 and not first:
                        act.wait_ge(hd_out, at(16, -16))
                        norm_hi(at, -1, hout, B2)
                    if h == 2:
                        act.wait_ge(clst_done, at(1, 1))
                        act.activation(pt[:, :, 0, :, CLS], bank[6][:, 0:QT * H].rearrange("p (k h) -> p h k", k=QT), ACT.Copy).then_inc(pc_hi, 1)
                    if h:
                        p_part(at, h - 1)
                p_part(at, H - 1)
                act.wait_ge(key_done, at(1, 1))
                act.activation(pkr[0:H, 0, :, 0:IMG], bank[6][0:H, :].rearrange("p (t s) -> p t s", t=2), ACT.Copy).then_inc(key_hi, 1)
                act.activation(pkr[0:H, 0, :, CLS:S], ecr[:, :, :], ACT.Copy).then_inc(key_hi, 1)
                for c in range(NP):
                    act.wait_ge(rb_done, at(8, c + 1))
                    if c >= 2:
                        act.wait_ge(on_ok, at(8, c - 1))
                    act.activation(sq[:, c % 2, :], bank[c % 2][:, 0:S], ACT.Copy, scale=1.0 / WS).then_inc(rb_ok, 1)
                    if c:
                        o_part(at, c - 1)
                o_part(at, NP - 1)
                for m in range(KC):
                    act.wait_ge(wo_done, at(2, m + 1))
                    act.activation(x[:, m, :], bank[4 + m][:, 0:S], ACT.Copy, scale=1.0 / WS).then_inc(x_ok, 1)
                if not last:
                    v_part(at1, 0)
                squares(at, 0)
                if not last:
                    v_part(at1, 1)
                first_rstd(at, 0, 3)
                if not last:
                    v_part(at1, 2)
                norm_hi(at, 0, hmid, B1)
                if not last:
                    v_part(at1, 3)
                for j in range(FC):
                    act.wait_ge(ff1_done, at(8, j + 1))
                    if j >= 2:
                        act.wait_ge(ff1_lo, at(8, j - 1))
                    bf = par[:, BF1 + j:BF1 + j + 1]
                    act.activation(rel[:, j % 2, :], bank[j % 2][:, 0:S], ACT.Relu, bias=bf, scale=1.0 / WS).then_inc(relu_ok, 1)
                    act.activation(hid[:, 0, j, :], bank[j % 2][:, 0:S], ACT.Relu, bias=bf, scale=1.0 / WS).then_inc(ff1_hi, 1)
                for m in range(KC):
                    act.wait_ge(ff2_done, at(2, m + 1))
                    act.activation(x[:, m, :], bank[4 + m][:, 0:S], ACT.Identity, bias=par[:, BF2 + m:BF2 + m + 1], scale=1.0 / WS).then_inc(x_ok, 1)

            def start(l, at, atl):
                act.wait_ge(par_in, atl(16, 16))
                layer_start(l, at, atl)

            def layer_end(at, l):
                squares(at, -1)
                first_rstd(at, -1, 7)
                act.wait_ge(hd_out, at(16, -16))
                norm_hi(at, -1, hout, B2)

            iterations(act, body, start, layer_end)

        @block.vector
        def _(v):
            n = [0]
            count = v.alloc_register("dve_count")

            def setup(ins):
                n[0] += 1
                ins.then_inc(setup_ok, 1)
                v.wait_ge(setup_ok, n[0])

            v.wait_ge(const_in, 64)
            v.wait_ge(const_ok, 5)
            setup(v.tensor_scalar(u16[:, :], uv[:, 0, :], WS, None, ALU.mult))
            setup(v.tensor_tensor(uv[:, 1, :], uv[:, 1, :], uv[:, 0, :], ALU.subtract))
            setup(v.tensor_scalar(uv[:, 1, :], uv[:, 1, :], WS, None, ALU.mult))
            setup(v.tensor_tensor(wm[:, :, :], hmask[:, :, :], uv[:, 1, :].unsqueeze(2).broadcast_to([P, NP, H]), ALU.mult))
            setup(v.tensor_scalar(ident16[:, :], ident[:, :], WS, None, ALU.mult))
            setup(v.tensor_copy(sel[:, :, :].rearrange("p c m -> p (c m)"), cb[:, 0:4, :].rearrange("p h s -> p (h s)")[:, 0:NP * P]))
            setup(v.tensor_copy(rT2[:, 0, :, :], x[:, :, :]))
            setup(v.tensor_tensor(rT2[:, 1, :, :], x[:, :, :], rT2[:, 0, :, :], ALU.subtract))

            def k_add(at, j):
                v.wait_ge(proj_done, at(16, j + 1))
                v.wait_ge(proj_lo, at(16, j - 1))
                v.tensor_tensor(rel[:, j % 2, :], bank[4 + j % 2][:, 0:S], kr16[:, j - NP, :], ALU.add).then_inc(k_sum, 1)

            def project_lo(at, j):
                v.wait_ge(proj_hi, at(16, j + 1))
                if j < NP:
                    v.scalar_tensor_tensor(rq[:, 1, j, :], bank[4 + j % 2][:, 0:S], u16[:, j:j + 1], rq[:, 0, j, :],
                                           ALU.add, ALU.subtract).then_inc(proj_lo, 1)
                else:
                    v.tensor_tensor(rk[:, 1, j - NP, :], rel[:, j % 2, :], rk[:, 0, j - NP, :], ALU.subtract).then_inc(proj_lo, 1)

            def v_part(at, u):
                v.wait_ge(v_hi, at(4, u + 1))
                tt, half = divmod(u, 2)
                c = slice(half * 512, half * 512 + 512)
                v.tensor_tensor(vs[:, 1, tt, c], bank[6 + u % 2][:, :], vs[:, 0, tt, c], ALU.subtract).then_inc(v_lo, 1)

            def centre(at, call, bk):
                v.wait_ge(mean_done, at(2, call + 1))
                for k in range(KC):
                    v.tensor_tensor(x[:, k, :], x[:, k, :], bank[bk][:, 0:S], ALU.subtract).then_inc(xc_ok, 1)

            def scale(at, call, bk, gamma):
                v.wait_ge(y0_ok, at(2, call + 1))
                steps = (lambda: v.scalar_tensor_tensor(t1[:, :], bank[bk][:, 0:S], EPS, y[:, :], ALU.add, ALU.mult),
                         lambda: v.tensor_tensor(t1[:, :], t1[:, :], y[:, :], ALU.mult),
                         lambda: v.tensor_scalar(t1[:, :], t1[:, :], -0.5, 1.5, ALU.mult, ALU.add),
                         lambda: v.tensor_tensor(y[:, :], y[:, :], t1[:, :], ALU.mult))
                for i, f in enumerate(steps):
                    f().then_inc(newton, 1)
                    v.wait_ge(newton, at(8, 4 * call + i + 1))
                for k in range(KC):
                    v.scalar_tensor_tensor(x[:, k, :], x[:, k, :], par[:, gamma + k:gamma + k + 1], y[:, :],
                                           ALU.mult, ALU.mult).then_inc(z_ok, 1)

            def norm_lo(at, call, dst, beta):
                for k in range(KC):
                    v.wait_ge(z_hi, at(4, 2 * call + k + 1))
                    v.scalar_tensor_tensor(dst[:, 1, k, :], x[:, k, :], par[:, beta + k:beta + k + 1], dst[:, 0, k, :],
                                           ALU.add, ALU.subtract).then_inc(z_lo, 1)

            def keep_cls(at, b):
                v.wait_ge(z_lo, at(4, 0))
                v.tensor_copy(hcls[:, :, :, b], hout[:, :, :, CLS]).then_inc(hcls_ok, 1)

            def layer_start(l, at, atl):
                for half in range(2):
                    v.wait_ge(vcls_hi, atl(2, half + 1))
                    c = slice(half * 512, half * 512 + 512)
                    v.tensor_tensor(vcl[:, 1, c], bank[6 + half][0:B, :], vcl[:, 0, c], ALU.subtract).then_inc(vcls_lo, 1)
                for j in range(2 * NP):
                    if j == NP:
                        v.wait_ge(kr_ok, atl(8, 8))
                    if j >= NP:
                        k_add(at, j)
                    project_lo(at, j)
                for u in range(4):
                    v_part(at, u)
                v.wait_ge(cc_done, atl(1, 1))
                v.tensor_copy(cc[:, :], bank[2][0:H, 0:S]).then_inc(cc_ok, 1)
                v.wait_ge(cc_ok, atl(1, 1))

            def p_part(at, h):
                v.wait_ge(p_hi, at(16, h + 1))
                v.tensor_tensor(pt[:, h, 1, :, 0:IMG], bank[2 + h % 2][:, :].rearrange("p (k s) -> p k s", k=QT),
                                pt[:, h, 0, :, 0:IMG], ALU.subtract).then_inc(p_lo, 1)

            def key_col(at, h):
                v.wait_ge(e_ok, at(32, 2 * h + 2))
                v.tensor_copy(ecol[:, :, h:h + 1], E[:, h % 2, :, CLS:S]).then_inc(ecol_ok, 1)

            def o_part(at, c):
                v.wait_ge(o_hi, at(8, c + 1))
                v.tensor_tensor(o2[:, 1, c, :], x[:, c % 2, :], o2[:, 0, c, :], ALU.subtract).then_inc(o_lo, 1)

            def body(at, b, first, last):
                at1 = None if last else At(v, at.g + 1)
                if not first:
                    centre(at, -1, 7)
                v.wait_ge(stack_in, at(192, 192))
                v.tensor_copy(qbd[:, :, :].rearrange("p h j -> p (h j)")[:, 0:H * H:H + 1], qs[:, :, CLS]).then_inc(qbd_ok, 1)
                cs_count = at.now(1, 1, count)
                v.wait_ge(setup_ok, SETUP)
                v.wait_ge(cs_done, cs_count)
                v.tensor_tensor_reduce(ec[:, :], bank[6][0:H, 0:S], cc[:, :], -SCORE, 3e38, ALU.add, ALU.min, nbc[:, :]).then_inc(sc_ok, 1)
                for h in range(H):
                    if h >= 2:
                        v.wait_ge(t_done, at(16, h - 1))
                        v.wait_ge(ecol_ok, at(16, h - 1))
                    for qt in range(QT):
                        s_count = at.now(32, 2 * h + qt + 1, count)
                        v.wait_ge(setup_ok, SETUP)
                        v.wait_ge(s_done, s_count)
                        v.tensor_tensor_reduce(E[:, h % 2, qt, :], bank[qt][:, 0:S], cb[:, h, :], -SCORE, 3e38,
                                               ALU.add, ALU.min, nb[:, 2 * h + qt:2 * h + qt + 1]).then_inc(s_ok, 1)
                    if h:
                        key_col(at, h - 1)
                    if not last:
                        if h >= NP:
                            k_add(at1, h)
                        if h:
                            project_lo(at1, h - 1)
                    if h >= 2:
                        p_part(at, h - 2)
                    if h == 2 and not first:
                        scale(at, -1, 7, G2)
                    if h == 3:
                        v.wait_ge(pc_hi, at(1, 1))
                        v.tensor_tensor(pt[:, :, 1, :, CLS], bank[6][:, 0:QT * H].rearrange("p (k h) -> p h k", k=QT),
                                        pt[:, :, 0, :, CLS], ALU.subtract).then_inc(pc_lo, 1)
                    if h == 4 and not first:
                        norm_lo(at, -1, hout, B2)
                        keep_cls(at, b - 1)
                key_col(at, H - 1)
                v.reciprocal(rs[:, :, :], sums[:, :, :]).then_inc(rs_ok, 1)
                v.wait_ge(ec_ok, at(1, 1))
                v.tensor_copy(ecr[:, 0, :], ec[:, CLS:S]).then_inc(rs_ok, 1)
                v.reciprocal(ecr[:, 1, :], sumc[:, :]).then_inc(rs_ok, 1)
                p_part(at, H - 2)
                if not last:
                    project_lo(at1, H - 1)
                p_part(at, H - 1)
                v.wait_ge(key_hi, at(2, 2))
                v.tensor_tensor(pkr[0:H, 1, :, 0:IMG], bank[6][0:H, :].rearrange("p (t s) -> p t s", t=2),
                                pkr[0:H, 0, :, 0:IMG], ALU.subtract).then_inc(key_lo, 1)
                v.tensor_tensor(pkr[0:H, 1, :, CLS:S], ecr[:, :, :], pkr[0:H, 0, :, CLS:S], ALU.subtract).then_inc(key_lo, 1)
                for c in range(NP):
                    v.wait_ge(o_done, at(8, c + 1))
                    v.wait_ge(rb_ok, at(8, c + 1))
                    if c >= 2:
                        v.wait_ge(o_lo, at(8, c - 1))
                    v.tensor_tensor(x[:, c % 2, :], bank[6 + c % 2][:, 0:S], sq[:, c % 2, :], ALU.mult).then_inc(on_ok, 1)
                    if c:
                        o_part(at, c - 1)
                o_part(at, NP - 1)
                centre(at, 0, 2)
                if not last:
                    v_part(at1, 0)
                    v_part(at1, 1)
                scale(at, 0, 3, G1)
                norm_lo(at, 0, hmid, B1)
                if not last:
                    v_part(at1, 2)
                    v_part(at1, 3)
                for j in range(FC):
                    v.wait_ge(relu_ok, at(8, j + 1))
                    v.wait_ge(ff1_hi, at(8, j + 1))
                    v.tensor_tensor(hid[:, 1, j, :], rel[:, j % 2, :], hid[:, 0, j, :], ALU.subtract).then_inc(ff1_lo, 1)

            def layer_end(at, l):
                centre(at, -1, 7)
                scale(at, -1, 7, G2)
                norm_lo(at, -1, hout, B2)
                keep_cls(at, B - 1)

            def start(l, at, atl):
                v.wait_ge(par_in, atl(16, 16))
                layer_start(l, at, atl)

            iterations(v, body, start, layer_end)


def expert_stage(nc, io, keep):
    with ExitStack() as ctx:
        sb = lambda n, s, d=F32: ctx.enter_context(nc.sbuf_tensor(n, s, d))
        sem = lambda n: ctx.enter_context(nc.semaphore(n))
        ident = keep["ident"]
        ident_h = sb("ident_h", [P, P], F16)
        ha = sb("ha", [P, B, 2, KC, S], F16)
        y = sb("y_rows", [P, NT, D])
        xn = sb("xn_rows", [P, NT, D])
        xT = sb("xT_cols", [P, 2, KC, TOKENS], F16)
        stats = sb("stats2", [P, NT, 6])
        mv = sb("mv2", [P, NT, 2])
        rstd = sb("rstd2", [P, 3, NT])
        rw = sb("rw", [P, KC, E_G + E_N])
        rw2 = sb("rw2", [P, 2, KC, E_G + E_N], F16)
        s_ = sb("route_s", [P, NT, E_G + E_N])
        top = sb("route_top", [P, NT, 1])
        val = sb("route_val", [P, NT, 1])
        eq = sb("route_eq", [P, NT, E_G])
        rem = sb("route_rem", [P, NT, 1])
        pair_sum = sb("route_pair", [P, NT, E_G])
        wgt = sb("route_w", [P, E_N, NT])
        we = sb("we_sb", [P, 2, 2, E_COLS], F16)
        gs = sb("gate_silu", [P, 2, 512])
        hf = sb("hidden_f", [P, 2, 512])
        hd = sb("hidden", [P, 2, 2, EFC, 512], F16)
        hc = sb("hidden_cls", [P, 2, EFC, B], F16)
        bank = [ctx.enter_context(nc.psum_tensor(f"ex{i}", [P, 512], F32)) for i in range(8)]

        ha_in, h0_in, rw_in = map(sem, ("ha_in", "h0_in3", "rw_in"))
        we_in = [sem("we_in0"), sem("we_in1")]
        zero_ok, identh_ok, res_done, h1_ok, var_ok, y0_ok, ln_ok, xn_ok = map(sem, (
            "zero_ok", "identh_ok", "res_done", "h1_ok", "var_ok3", "y0_ok3", "ln_ok3", "xn_ok3"))
        tr_done, xt_hi, xt_lo, route_done, rexp_ok, route_ok, dve = map(sem, (
            "tr_done", "xt_hi", "xt_lo", "route_done", "rexp_ok", "route_ok", "dve_step3"))
        gu_done, silu_ok, hf_ok, h_hi, h_lo, dn_done, acc_ok, out_done = map(sem, (
            "gu_done", "silu_ok", "hf_ok", "h_hi", "h_lo", "dn_done", "acc_ok", "out_done"))
        TERMS = ((0, 0), (0, 1), (1, 0))
        GATE, UP, DOWN = 0, 1024, 2048
        BLOCKS = [(i * 512, 512) for i in range(4)] + [(B * IMG, B)]
        PER = len(BLOCKS) * EFC
        cols = lambda t: slice(t * P, (t + 1) * P) if t < NT - 1 else slice(B * IMG, TOKENS)
        rows = lambda t: P if t < NT - 1 else B
        ORDER = (("h", 0), ("h", 1), ("d", 0), ("h", 2), ("d", 1), ("h", 3), ("h", 4), ("d", 2), ("d", 3), ("d", 4))
        tiles = lambda n: range(4 * n, 4 * n + 4) if n < 4 else (NT - 1,)
        block = ctx.enter_context(nc.Block())

        def images(b):
            if b < B:
                return bank[b][:, :].rearrange("p (k s) -> p k s", k=KC), (lambda t: xT[:, t, :, b * IMG:(b + 1) * IMG])
            return bank[0][:, 0:KC * B].rearrange("p (k b) -> p k b", k=KC), (lambda t: xT[:, t, :, B * IMG:TOKENS])

        def hidden(nb, t, f):
            return hd[:, nb % 2, t, f, :] if nb < 4 else hc[:, t, f, :]

        @block.sync
        def _(sp):
            sp.dma_start(ha[:, :, :, :, :].rearrange("p b t k s -> p b (t k s)"), io["hd"].rearrange("b p n -> p b n")).then_inc(ha_in, 16)
            sp.dma_start(y[:, 0:NT - 1, :], io["h0"][0:B * IMG, :].rearrange("(t p) d -> p t d", p=P)).then_inc(h0_in, 16)
            sp.dma_start(y[0:B, NT - 1, :], io["h0"][B * IMG:TOKENS, :]).then_inc(h0_in, 16)
            sp.dma_start(rw[:, :, :], io["rw"]).then_inc(rw_in, 16)
            for e in range(E_N):
                if e >= 2:
                    sp.wait_ge(dn_done, NT * (e - 1))
                sp.dma_start(we[:, e % 2, :, :], io["we_split"][e]).then_inc(we_in[e % 2], 16)
            for b in range(B):
                sp.wait_ge(acc_ok, NT * (E_N - 1) + QT * (b + 1))
                sp.dma_start(io["out"][b, 1:S, :].rearrange("(j p) d -> p j d", p=P), y[:, QT * b:QT * b + QT, :]).then_inc(out_done, 16)
            sp.wait_ge(acc_ok, NT * E_N)
            sp.dma_start(io["out"][:, 0, :], y[0:B, NT - 1, :]).then_inc(out_done, 16)
            sp.wait_ge(out_done, 16 * (B + 1))

        @block.gpsimd
        def _(pool):
            pool.memset(mv[:, :, :], 1.0).then_inc(zero_ok, 1)
            pool.memset(s_[:, :, :], 0.0).then_inc(zero_ok, 1)

        @block.scalar
        def _(act):
            nc.scalar.preload_act_table_set("natural_log_exp_and_others")
            act.wait_ge(var_ok, 1)
            act.activation(rstd[:, 0, :], rstd[:, 2, :], ACT.Ln).then_inc(ln_ok, 1)
            act.wait_ge(ln_ok, 1)
            act.activation(rstd[:, 1, :], rstd[:, 0, :], ACT.Exp, scale=-0.5).then_inc(y0_ok, 1)
            for b in range(B + 1):
                act.wait_ge(tr_done, b + 1)
                src, dst = images(b)
                act.activation(dst(0), src, ACT.Copy).then_inc(xt_hi, 1)
            act.wait_ge(route_done, 1)
            act.wait_ge(zero_ok, 2)
            n = E_G + E_N
            act.activation(s_[:, 0:NT - 1, :], bank[1][:, 0:(NT - 1) * n].rearrange("p (t n) -> p t n", n=n), ACT.Exp, scale=-1.0 / WS).then_inc(rexp_ok, 1)
            act.activation(s_[0:B, NT - 1, :], bank[1][0:B, (NT - 1) * n:NT * n], ACT.Exp, scale=-1.0 / WS).then_inc(rexp_ok, 1)
            nc.scalar.preload_act_table(ACT.Silu)

            def expert(at):
                i = 0
                for kind, nb in ORDER:
                    if kind == "d":
                        continue
                    w = BLOCKS[nb][1]
                    for f in range(EFC):
                        act.wait_ge(gu_done, at(PER, i + 1))
                        act.activation(gs[:, f % 2, 0:w], bank[f % 2][:, 0:w], ACT.Silu, scale=1.0 / WS).then_inc(silu_ok, 1)
                        act.wait_ge(hf_ok, at(PER, i + 1))
                        act.activation(hidden(nb, 0, f), hf[:, f % 2, 0:w], ACT.Copy).then_inc(h_hi, 1)
                        i += 1

            with act.Fori(0, E_N // 2) as ep:
                for eo in range(2):
                    expert(At(act, act.snap(ep * 2 + eo)))

        @block.vector
        def _(v):
            n = [0]

            def step(ins, wait=True):
                ins.then_inc(dve, 1)
                n[0] += 1
                if wait:
                    v.wait_ge(dve, n[0])

            v.tensor_copy(ident_h[:, :], ident[:, :]).then_inc(identh_ok, 1)
            v.wait_ge(rw_in, 16)
            step(v.tensor_scalar(rw[:, :, :], rw[:, :, :], WS, None, ALU.mult))
            step(v.tensor_copy(rw2[:, 0, :, :], rw[:, :, :]))
            step(v.tensor_tensor(rw2[:, 1, :, :], rw[:, :, :], rw2[:, 0, :, :], ALU.subtract))
            v.wait_ge(h0_in, 32)
            for b in range(B + 1):
                v.wait_ge(res_done, b + 1)
                if b < B:
                    r = y[:, QT * b:QT * b + QT, :]
                    src = bank[b][:, :].rearrange("p (j d) -> p j d", j=QT)
                else:
                    r, src = y[0:B, NT - 1, :], bank[0][0:B, 0:D]
                v.tensor_tensor(r, src, r, ALU.add).then_inc(h1_ok, 1)
            v.wait_ge(h1_ok, B + 1)
            v.wait_ge(zero_ok, 2)
            layer_norm_rows(v, step, y, xn, stats, mv, rstd, var_ok, y0_ok)
            v.sem_inc(xn_ok, 1)
            for b in range(B + 1):
                v.wait_ge(xt_hi, b + 1)
                src, dst = images(b)
                v.tensor_tensor(dst(1), src, dst(0), ALU.subtract).then_inc(xt_lo, 1)
            v.wait_ge(rexp_ok, 2)
            step(v.tensor_scalar(s_[:, :, :], s_[:, :, :], 1.0, None, ALU.add))
            step(v.reciprocal(s_[:, :, :], s_[:, :, :]))
            g, m = s_[:, :, 0:E_G], s_[:, :, E_G:].rearrange("p t (g e) -> p t g e", e=E_K)
            step(v.tensor_reduce(top[:, :, :], g, AX.X, ALU.max))
            step(v.tensor_tensor(eq[:, :, :], g, top[:, :, :].broadcast_to([P, NT, E_G]), ALU.is_equal), False)
            step(v.tensor_scalar(val[:, :, :], top[:, :, :], 1e-9, None, ALU.add))
            step(v.reciprocal(val[:, :, :], val[:, :, :]), False)
            step(v.memset(rem[:, :, :], 1.0))
            step(v.tensor_tensor(val[:, :, :], val[:, :, :], top[:, :, :], ALU.mult))
            step(v.tensor_scalar(val[:, :, :], val[:, :, :], 1.0 / WS, None, ALU.mult))
            for i in range(E_G):
                step(v.tensor_tensor(eq[:, :, i:i + 1], eq[:, :, i:i + 1], rem[:, :, :], ALU.mult))
                step(v.tensor_tensor(rem[:, :, :], rem[:, :, :], eq[:, :, i:i + 1], ALU.subtract))
            step(v.tensor_tensor(eq[:, :, :], eq[:, :, :], val[:, :, :].broadcast_to([P, NT, E_G]), ALU.mult))
            step(v.tensor_reduce(pair_sum[:, :, :], m, AX.X, ALU.add))
            step(v.tensor_scalar(pair_sum[:, :, :], pair_sum[:, :, :], 1e-9, None, ALU.add))
            step(v.reciprocal(pair_sum[:, :, :], pair_sum[:, :, :]))
            step(v.tensor_tensor(eq[:, :, :], eq[:, :, :], pair_sum[:, :, :], ALU.mult))
            for i in range(E_K):
                out = wgt[:, :, :].rearrange("p (g e) t -> p e t g", e=E_K)[:, i]
                step(v.tensor_tensor(out, m[:, :, :, i], eq[:, :, :], ALU.mult))
            v.sem_inc(route_ok, 1)

            def expert(at, e):
                v.wait_ge(acc_ok, at(NT, 0))
                i = j = 0
                for kind, nb in ORDER:
                    if kind == "h":
                        w = BLOCKS[nb][1]
                        if nb < 2:
                            v.wait_ge(dn_done, at(NT, 0))
                        elif nb < 4:
                            v.wait_ge(dn_done, at(NT, 4 * (nb - 1)))
                        for f in range(EFC):
                            v.wait_ge(silu_ok, at(PER, i + 1))
                            if i or True:
                                v.wait_ge(h_lo, at(PER, i - 1)) if i >= 2 else v.wait_ge(h_lo, at(PER, 0))
                            v.scalar_tensor_tensor(hf[:, f % 2, 0:w], bank[2 + f % 2][:, 0:w], 1.0 / WS, gs[:, f % 2, 0:w],
                                                   ALU.mult, ALU.mult).then_inc(hf_ok, 1)
                            v.wait_ge(h_hi, at(PER, i + 1))
                            v.tensor_tensor(hidden(nb, 1, f), hf[:, f % 2, 0:w], hidden(nb, 0, f), ALU.subtract).then_inc(h_lo, 1)
                            i += 1
                    else:
                        for t in tiles(nb):
                            v.wait_ge(dn_done, at(NT, j + 1))
                            r = rows(t)
                            v.scalar_tensor_tensor(y[0:r, t, :], bank[4 + j % 4][0:r, 0:D], wgt[0:r, e, t:t + 1], y[0:r, t, :],
                                                   ALU.mult, ALU.add).then_inc(acc_ok, 1)
                            j += 1

            with v.Fori(0, E_N // 2) as ep:
                for eo in range(2):
                    e = v.snap(ep * 2 + eo)
                    expert(At(v, e), e)

        @block.tensor
        def _(pe):
            mm = pe.matmul
            pe.wait_ge(identh_ok, 1)
            pe.wait_ge(ha_in, 16)
            for b in range(B + 1):
                if b == B:
                    pe.wait_ge(h1_ok, 1)
                for j in range(QT if b < B else 1):
                    for k in range(KC):
                        for t in range(2):
                            lhs = ha[:, b, t, k, j * P:(j + 1) * P] if b < B else ha[:, :, t, k, CLS]
                            out = bank[b % B][0:P if b < B else B, j * D + k * P:j * D + (k + 1) * P]
                            r = mm(out, lhs, ident_h[:, :], start=t == 0, stop=t == 1)
                r.then_inc(res_done, 1)
            pe.wait_ge(xn_ok, 1)
            for b in range(B):
                for k in range(KC):
                    for j in range(QT):
                        r = pe.transpose(bank[b][:, (k * QT + j) * P:(k * QT + j + 1) * P], xn[:, QT * b + j, k * P:(k + 1) * P], ident[:, :])
                r.then_inc(tr_done, 1)
            pe.wait_ge(xt_lo, 1)
            for k in range(KC):
                r = pe.transpose(bank[0][:, k * B:(k + 1) * B], xn[0:B, NT - 1, k * P:(k + 1) * P], ident[0:B, 0:B])
            r.then_inc(tr_done, 1)
            pe.wait_ge(xt_lo, B + 1)
            n = E_G + E_N
            for t in range(NT):
                for i, (k, a, m) in enumerate((k, a, m) for k in range(KC) for a in range(2) for m in range(2)):
                    r = mm(bank[1][0:rows(t), t * n:(t + 1) * n], xT[:, m, k, cols(t)], rw2[:, a, k, :], start=i == 0, stop=i == 7)
            r.then_inc(route_done, 1)
            pe.wait_ge(rexp_ok, 2)
            pe.wait_ge(route_ok, 1)

            def expert(at, eo, loads):
                pe.wait_ge(we_in[eo], loads)
                i = j = 0
                for kind, nb in ORDER:
                    if kind == "h":
                        c0, w = BLOCKS[nb]
                        for f in range(EFC):
                            pe.wait_ge(hf_ok, at(PER, i - 1)) if i >= 2 else pe.wait_ge(hf_ok, at(PER, 0))
                            for base, bk in ((GATE, f % 2), (UP, 2 + f % 2)):
                                for q, (k, (a, m)) in enumerate((k, t) for k in range(KC) for t in TERMS):
                                    c = base + k * E_F + f * P
                                    r = mm(bank[bk][:, 0:w], we[:, eo, a, c:c + P], xT[:, m, k, c0:c0 + w], start=q == 0, stop=q == 5)
                            r.then_inc(gu_done, 1)
                            i += 1
                    else:
                        last_h = 4 * (nb + 1) if nb < 4 else PER
                        pe.wait_ge(h_lo, at(PER, last_h))
                        for ti, t in enumerate(tiles(nb)):
                            pe.wait_ge(acc_ok, at(NT, j - 3)) if j >= 4 else pe.wait_ge(acc_ok, at(NT, 0))
                            r0 = rows(t)
                            s0 = slice(ti * P, ti * P + r0)
                            for q, (f, (a, m)) in enumerate((f, tm) for f in range(EFC) for tm in TERMS):
                                c = DOWN + f * D
                                r = mm(bank[4 + j % 4][0:r0, 0:D], hidden(nb, m, f)[:, s0], we[:, eo, a, c:c + D],
                                       start=q == 0, stop=q == EFC * 3 - 1)
                            r.then_inc(dn_done, 1)
                            j += 1

            with pe.Fori(0, E_N // 2) as ep:
                for eo in range(2):
                    expert(At(pe, pe.snap(ep * 2 + eo)), eo, pe.snap(ep * 16 + 16))


def vit_tower(nc, io):
    half = lambda n, s: nc.dram_tensor(n, s, F16, kind="Internal").ap()
    io["hd"] = half("hd_dram", [B, P, 2 * KC * S])
    io["w_split"] = half("w_split_dram", [L, P, 2, W_COLS])
    io["we_split"] = half("we_split_dram", [E_N, P, 2, E_COLS])
    io["vbd"] = half("vbd_dram", [B, VBD_IMAGE])
    io["h0"] = nc.dram_tensor("h0_dram", [TOKENS, D], F32, kind="Internal").ap()
    with ExitStack() as ctx:
        sb = lambda n, s, d=F32: ctx.enter_context(nc.sbuf_tensor(n, s, d))
        keep = {"ident": sb("ident", [P, P])}
        with ExitStack() as inner:
            keep["w"] = inner.enter_context(nc.sbuf_tensor("w_sb", [P, 2, W_COLS], F16))
            keep["hcls"] = inner.enter_context(nc.sbuf_tensor("hcls", [P, 2, KC, B], F16))
            token_stage(nc, io, keep)
            attention_stage(nc, io, keep)
        expert_stage(nc, io, keep)


def laid_out(i):
    g = lambda n: np.asarray(i[n])
    by_row = lambda w: w.reshape(w.shape[0], -1, P, w.shape[2]).transpose(0, 2, 1, 3).reshape(w.shape[0], P, -1)
    by_col = lambda a: a.reshape(L, -1, P).transpose(0, 2, 1)

    def wavelet(w, n):
        r, c = n // 32, n // 4
        return w.reshape(3, 32, r, 4, c, 3).transpose(3, 1, 0, 2, 4, 5).reshape(P, 3 * r * c, 3)

    a = {
        "x": g("x").reshape(B, 32, 8, 4, 64).transpose(3, 1, 0, 2, 4).reshape(P, B, 8, 64),
        "cls_tok": g("cls_tok").reshape(D),
        "wa": g("L0_tok_Wa").reshape(32, 4, 8).transpose(1, 0, 2).reshape(P, 8),
        "wd1": wavelet(g("L0_tok_Wd1"), 32), "wd2": wavelet(g("L0_tok_Wd2"), 64), "wd3": wavelet(g("L0_tok_Wd3"), 128),
        "gate_bias": np.concatenate([g("L0_tok_" + n) for n in ("ba", "bd1", "bd2", "bd3")]),
        "w": np.concatenate([by_row(g("L0_attn_" + n)) for n in ("W_qkv", "W_r", "W_o", "W_ff1", "W_ff2")], axis=2),
        "par": np.concatenate([by_col(g("L0_attn_" + n)) for n in ("ln1_g", "ln1_b", "ln2_g", "ln2_b", "b_ff2", "b_ff1")], axis=2),
        "uv": np.stack([g("L0_attn_" + n).reshape(NP, P).T for n in ("u", "v")], axis=1),
        "we": np.concatenate([by_row(g("L0_ffn_" + n)) for n in ("gate_w", "up_w", "down_w")], axis=2),
        "rw": np.concatenate([g("L0_ffn_macro_w"), g("L0_ffn_micro_w").transpose(1, 0, 2).reshape(D, E_N)], axis=1)
        .reshape(KC, P, E_G + E_N).transpose(1, 0, 2),
    }
    return {k: np.ascontiguousarray(x) for k, x in {**a, **const_arrays()}.items()}


def kernel(**inputs):
    from concourse import bacc
    from concourse.bass_utils import run_bass_kernel_spmd

    nc = bacc.Bacc("TRN2", target_bir_lowering=False, num_devices=1)
    arrays = {f"in_{n}_dram": a for n, a in laid_out(inputs).items()}
    io = {n[3:-5]: nc.dram_tensor(n, a.shape, mybir.dt.from_np(a.dtype), kind="ExternalInput").ap() for n, a in arrays.items()}
    io["out"] = nc.dram_tensor("out_dram", [B, S, D], F32, kind="ExternalOutput").ap()
    vit_tower(nc, io)
    return run_bass_kernel_spmd(nc, [arrays], core_ids=[0]).results[0]["out_dram"]
```

```python
from contextlib import ExitStack

import numpy as np

import concourse.bass as bass
from concourse import mybir

F32 = mybir.dt.float32
F16 = mybir.dt.float16
ALU = mybir.AluOpType
ACT = mybir.ActivationFunctionType
AX = mybir.AxisListType

P = 128
B = 8
IMG = 256
D = IMG
KC = D // P
S = IMG + 1
CLS = IMG
L, H, DH, DF = 4, 16, 64, 1024
HD = H * DH
NP = HD // P
QT = 2
FC = DF // P
EPS = 1e-5
WS = 16.0
NT = B * QT + 1
E_N, E_F, E_G, E_K = 8, 512, 4, 2
EFC = E_F // P
TOKENS = B * S

C_QKV, C_R, C_1, C_O, C_2 = 0, 6144, 8192, 10240, 12288
W_COLS = 14336
E_COLS = 3072
SPLIT = 256

G1, B1, G2, B2, BF2, BF1 = 0, 2, 4, 6, 8, 10
PAR_COLS = 18
BF1W = PAR_COLS
PAR_ALL = BF1W + FC


def const_arrays():
    pos = np.arange(S - 1, -1, -1, dtype=np.float32)
    freq = (np.float32(1.0) / np.power(np.float32(10000.0), np.arange(0, D, 2, dtype=np.float32) / np.float32(D))).astype(np.float32)
    ang = pos[:, None] * freq[None, :]
    r = np.concatenate([np.sin(ang), np.cos(ang)], axis=-1).astype(np.float32)
    r = np.concatenate([r[1:], r[:1]], axis=0)
    rT = np.ascontiguousarray(r.T.reshape(KC, P, S).transpose(1, 0, 2))
    p = np.arange(P)
    head = 2 * np.arange(NP)[None, :] + (p[:, None] >= DH)
    hmask = (head[:, :, None] == np.arange(H)[None, None, :]).astype(np.float32)
    sel = np.zeros((P, NP, P), np.float32)
    for c in range(NP):
        for m in range(P):
            sel[2 * c + (m >= DH), c, m] = 1.0
    return {"c_rT": rT, "c_hmask": hmask, "c_sel": sel, "c_ident": np.eye(P, dtype=np.float32)}


def token_stage(nc, io, keep):
    with ExitStack() as ctx:
        sb = lambda n, s, d=F32: ctx.enter_context(nc.sbuf_tensor(n, s, d))
        sem = lambda n: ctx.enter_context(nc.semaphore(n))
        img = sb("img", [P, B, 8, 64])
        wd = [sb("wd_l1", [P, 384, 3]), sb("wd_l2", [P, 96, 3]), sb("wd_l3", [P, 24, 3])]
        wa = sb("wa", [P, 8])
        bias = sb("gate_bias", [P, 10])
        scale = sb("gate_scale", [P, 10])
        half = sb("half", [P, 2, B, 8, 32])
        det = [sb("det1", [P, B, 3, 128]), sb("det2", [P, B, 3, 32]), sb("det3", [P, B, 3, 8])]
        app = [sb("app1", [P, B, 4, 32]), sb("app2", [P, B, 2, 16]), sb("app3", [P, B, 1, 8])]
        junk = sb("junk", [P, 384])
        part = sb("part", [P, B, 10])
        z = sb("z", [P, B, 10])
        top = sb("top", [P, B, 3])
        e = sb("e", [P, B, 10])
        den = sb("den", [P, B, 4])
        gate = sb("gate", [P, B, 10])
        ones = sb("ones", [P, P])
        xt = sb("xt", [P, NT, D])
        stats = sb("stats", [P, NT, 6])
        mv = sb("mv", [P, NT, 2])
        rstd = sb("rstd", [P, 3, NT])
        hs = sb("hs", [P, B, 2, KC, S], F16)
        wst = sb("wst", [P, 2, 2048])
        wmean = sb("wmean", [P, 2048 // SPLIT])
        cls_row = sb("cls_row", [B, D])
        bank = [ctx.enter_context(nc.psum_tensor(f"ta{i}", [P, 512], F32)) for i in range(8)]
        ident = keep["ident"]

        img_in, wd_in, small_in = sem("img_in"), sem("wd_in"), sem("small_in")
        dve = sem("dve_step")
        const_ok, part_ok, tot_ok, logit_ok, exp_ok, rec_ok = map(sem, (
            "const_ok", "part_ok", "tot_ok", "logit_ok", "exp_ok", "rec_ok"))
        h0_out, h0_in, var_ok, ln_ok, y0_ok, xn_ok = map(sem, (
            "h0_out", "h0_in", "var_ok", "ln_ok", "y0_ok", "xn_ok"))
        tr_ok, hi_ok, lo_ok, hd_out = map(sem, ("tr_ok", "hi_ok", "lo_ok", "hd_out"))
        w_in = [sem("w_in0"), sem("w_in1")]
        w_hi, w_lo, w_centred = map(sem, ("w_hi", "w_lo", "w_centred"))
        NW = W_COLS // 2048
        CJ = 2048 // SPLIT
        block = ctx.enter_context(nc.Block())

        @block.sync
        def _(sp):
            sp.dma_start(img[:, :, :, :], io["x"]).then_inc(img_in, 16)
            for i, n in enumerate(("wd3", "wd2", "wd1")):
                sp.dma_start(wd[i][:, :, :], io[n]).then_inc(wd_in, 16)
            sp.dma_start(wa[:, :], io["wa"]).then_inc(wd_in, 16)
            sp.dma_start(bias[:, :], io["gate_bias"].partition_broadcast(P)).then_inc(wd_in, 16)
            sp.dma_start(ident[:, :], io["c_ident"]).then_inc(small_in, 16)
            sp.dma_start(cls_row[:, :], io["cls_tok"].partition_broadcast(B)).then_inc(small_in, 16)
            for i in range(NW):
                if i >= 2:
                    sp.wait_ge(w_lo, i - 1)
                sp.dma_start(wst[:, i % 2, :].rearrange("p (j c) -> p j c", c=SPLIT),
                             io["w"][0, i * CJ:(i + 1) * CJ].rearrange("j p c -> p j c")).then_inc(w_in[i % 2], 16)
            sp.wait_ge(small_in, 32)
            sp.dma_start(io["h0"][B * IMG:TOKENS, :], cls_row[:, :]).then_inc(h0_out, 16)
            sp.wait_ge(rec_ok, 1)
            for b in range(B):
                for cg in range(4):
                    sp.dma_start(
                        io["h0"][b * IMG:(b + 1) * IMG, cg * 64:(cg + 1) * 64].rearrange("(br r) c -> br r c", r=8),
                        img[cg * 32:(cg + 1) * 32, b, :, :]).then_inc(h0_out, 16)
            sp.wait_ge(h0_out, 16 * (1 + 4 * B))
            sp.dma_start(xt[:, 0:NT - 1, :], io["h0"][0:B * IMG, :].rearrange("(t p) d -> p t d", p=P)).then_inc(h0_in, 16)
            sp.dma_start(xt[0:B, NT - 1, :], io["h0"][B * IMG:TOKENS, :]).then_inc(h0_in, 16)
            sp.wait_ge(lo_ok, B + 1)
            sp.dma_start(io["hd"].rearrange("b p n -> p b n"), hs[:, :, :, :, :].rearrange("p b t k s -> p b (t k s)")).then_inc(hd_out, 16)
            sp.wait_ge(hd_out, 16)

        @block.gpsimd
        def _(pool):
            pool.memset(ones[:, :], 1.0).then_inc(const_ok, 1)
            for a, b_, v in ((0, 1, -0.125), (1, 4, 0.125), (4, 7, 0.25), (7, 10, 0.5)):
                pool.memset(scale[:, a:b_], v).then_inc(const_ok, 1)
            pool.memset(mv[:, :, :], 1.0).then_inc(const_ok, 1)

        @block.scalar
        def _(act):
            nc.scalar.preload_act_table_set("natural_log_exp_and_others")
            for i in range(NW):
                act.wait_ge(w_in[i % 2], 16 * (i // 2 + 1))
                if i * 2048 >= C_O:
                    act.wait_ge(w_centred, i - C_O // 2048 + 1)
                act.activation(keep["w"][:, 0, i * 2048:(i + 1) * 2048], wst[:, i % 2, :], ACT.Copy, scale=WS).then_inc(w_hi, 1)
            act.wait_ge(logit_ok, 1)
            act.activation(e[:, :, :], z[:, :, :], ACT.Exp).then_inc(exp_ok, 1)
            act.wait_ge(var_ok, 1)
            act.activation(rstd[:, 0, :], rstd[:, 2, :], ACT.Ln).then_inc(ln_ok, 1)
            act.wait_ge(ln_ok, 1)
            act.activation(rstd[:, 1, :], rstd[:, 0, :], ACT.Exp, scale=-0.5).then_inc(y0_ok, 1)
            for b in range(B + 1):
                act.wait_ge(tr_ok, b + 1)
                if b < B:
                    dst, src = hs[:, b, 0, :, 0:IMG], bank[b][:, :].rearrange("p (k s) -> p k s", k=KC)
                else:
                    dst, src = hs[:, :, 0, :, CLS].rearrange("p b k -> p k b"), bank[0][:, 0:KC * B].rearrange("p (k b) -> p k b", k=KC)
                act.activation(dst, src, ACT.Copy).then_inc(hi_ok, 1)

        @block.vector
        def _(v):
            n = [0]

            def step(ins, wait=True):
                ins.then_inc(dve, 1)
                n[0] += 1
                if wait:
                    v.wait_ge(dve, n[0])

            def centre_weights(i):
                t = wst[:, i % 2, :].rearrange("p (j c) -> p j c", c=SPLIT)
                v.wait_ge(w_in[i % 2], 16 * (i // 2 + 1))
                step(v.tensor_reduce(wmean[:, :], t, AX.X, ALU.add))
                step(v.tensor_scalar(wmean[:, :], wmean[:, :], -1.0 / SPLIT, None, ALU.mult))
                v.tensor_tensor(t, t, wmean[:, :].unsqueeze(2).broadcast_to([P, CJ, SPLIT]), ALU.add).then_inc(w_centred, 1)

            def split_weights(i):
                if i * 2048 >= C_O:
                    centre_weights(i)
                v.wait_ge(w_hi, i + 1)
                c = slice(i * 2048, (i + 1) * 2048)
                v.scalar_tensor_tensor(keep["w"][:, 1, c], wst[:, i % 2, :], WS, keep["w"][:, 0, c],
                                       ALU.mult, ALU.subtract).then_inc(w_lo, 1)

            v.wait_ge(img_in, 16)
            src = img[:, :, :, :]
            for lv in range(3):
                r, c = 8 >> lv, 32 >> lv
                lo, hi = half[:, 0, :, 0:r, 0:c], half[:, 1, :, 0:r, 0:c]
                step(v.tensor_tensor(lo, src[:, :, :, 0:2 * c:2], src[:, :, :, 1:2 * c:2], ALU.add), False)
                step(v.tensor_tensor(hi, src[:, :, :, 0:2 * c:2], src[:, :, :, 1:2 * c:2], ALU.subtract))
                d = det[lv][:, :, :, :].rearrange("p b k (r c) -> p b k r c", c=c)
                for out, x, op in ((app[lv][:, :, :, :], lo, ALU.add), (d[:, :, 0], lo, ALU.subtract),
                                   (d[:, :, 1], hi, ALU.add), (d[:, :, 2], hi, ALU.subtract)):
                    step(v.tensor_tensor(out, x[:, :, 0:r:2, :], x[:, :, 1:r:2, :], op), False)
                v.wait_ge(dve, n[0])
                src = app[lv][:, :, :, :]
                split_weights(2 * lv)
                split_weights(2 * lv + 1)
            split_weights(6)
            v.wait_ge(wd_in, 16 * 5)
            for b in range(B):
                for col, a, w in [(0, app[2][:, b, 0, :], wa[:, :])] + [
                        (1 + 3 * (2 - lv) + k, det[lv][:, b, :, :].rearrange("p k n -> p (k n)"), wd[lv][:, :, k])
                        for lv in range(3) for k in range(3)]:
                    step(v.tensor_tensor_reduce(junk[:, 0:a.shape[1]], a, w, 1.0, 0.0, ALU.mult, ALU.add,
                                                part[:, b, col:col + 1]))
            v.sem_inc(part_ok, 1)
            v.wait_ge(tot_ok, 1)
            v.wait_ge(const_ok, 6)
            bc = lambda t, m: t.unsqueeze(1).broadcast_to([P, B, m])
            step(v.tensor_tensor(z[:, :, :], bank[0][:, 0:B * 10].rearrange("p (b m) -> p b m", m=10), bc(scale[:, :], 10), ALU.mult))
            step(v.tensor_scalar(bias[:, 0:1], bias[:, 0:1], -1.0, None, ALU.mult))
            step(v.tensor_tensor(z[:, :, :], z[:, :, :], bc(bias[:, :], 10), ALU.add))
            z3 = z[:, :, 1:10].rearrange("p b (l k) -> p b l k", k=3)
            step(v.tensor_reduce(top[:, :, :], z3, AX.X, ALU.max))
            v.tensor_tensor(z3, z3, top[:, :, :].unsqueeze(3).broadcast_to([P, B, 3, 3]), ALU.subtract).then_inc(logit_ok, 1)
            v.wait_ge(exp_ok, 1)
            step(v.tensor_scalar(den[:, :, 0:1], e[:, :, 0:1], 1.0, None, ALU.add), False)
            step(v.tensor_reduce(den[:, :, 1:4], e[:, :, 1:10].rearrange("p b (l k) -> p b l k", k=3), AX.X, ALU.add))
            step(v.memset(e[:, :, 0:1], 1.0))
            step(v.reciprocal(den[:, :, :], den[:, :, :]))
            for i, f in ((0, 1 / 64), (1, 1 / 64), (2, 1 / 16), (3, 1 / 4)):
                step(v.tensor_scalar(den[:, :, i:i + 1], den[:, :, i:i + 1], f, None, ALU.mult), False)
            v.wait_ge(dve, n[0])
            step(v.tensor_tensor(gate[:, :, 0:1], e[:, :, 0:1], den[:, :, 0:1], ALU.mult), False)
            step(v.tensor_tensor(gate[:, :, 1:10].rearrange("p b (l k) -> p b l k", k=3),
                                 e[:, :, 1:10].rearrange("p b (l k) -> p b l k", k=3),
                                 den[:, :, 1:4].unsqueeze(3).broadcast_to([P, B, 3, 3]), ALU.mult))
            a3 = app[2][:, :, 0, :]
            step(v.tensor_tensor(a3, a3, gate[:, :, 0:1].broadcast_to([P, B, 8]), ALU.mult), False)
            for lv in range(3):
                g = gate[:, :, 1 + 3 * (2 - lv):4 + 3 * (2 - lv)]
                m = (4 >> lv) * (32 >> lv)
                step(v.tensor_tensor(det[lv][:, :, :, :], det[lv][:, :, :, :], g.unsqueeze(3).broadcast_to([P, B, 3, m]), ALU.mult), False)
            v.wait_ge(dve, n[0])
            for lv in (2, 1, 0):
                r, c = 8 >> lv, 32 >> lv
                lo, hi = half[:, 0, :, 0:r, 0:c], half[:, 1, :, 0:r, 0:c]
                d = det[lv][:, :, :, :].rearrange("p b k (r c) -> p b k r c", c=c)
                a = app[lv][:, :, :, :]
                for out, x, y in ((lo, a, d[:, :, 0]), (hi, d[:, :, 1], d[:, :, 2])):
                    step(v.tensor_tensor(out[:, :, 0:r:2, :], x, y, ALU.add), False)
                    step(v.tensor_tensor(out[:, :, 1:r:2, :], x, y, ALU.subtract), False)
                v.wait_ge(dve, n[0])
                dst = img[:, :, :, :] if lv == 0 else app[lv - 1][:, :, :, :]
                step(v.tensor_tensor(dst[:, :, :, 0:2 * c:2], lo, hi, ALU.add), False)
                step(v.tensor_tensor(dst[:, :, :, 1:2 * c:2], lo, hi, ALU.subtract))
            v.sem_inc(rec_ok, 1)
            v.wait_ge(h0_in, 32)
            layer_norm_rows(v, step, xt, xt, stats, mv, rstd, var_ok, y0_ok)
            v.sem_inc(xn_ok, 1)
            for b in range(B + 1):
                v.wait_ge(hi_ok, b + 1)
                if b < B:
                    dst, hi, src = hs[:, b, 1, :, 0:IMG], hs[:, b, 0, :, 0:IMG], bank[b][:, :].rearrange("p (k s) -> p k s", k=KC)
                else:
                    q = lambda t: hs[:, :, t, :, CLS].rearrange("p b k -> p k b")
                    dst, hi, src = q(1), q(0), bank[0][:, 0:KC * B].rearrange("p (k b) -> p k b", k=KC)
                v.tensor_tensor(dst, src, hi, ALU.subtract).then_inc(lo_ok, 1)
            v.wait_ge(lo_ok, B + 1)
            for t in range(2):
                step(v.tensor_copy(keep["hcls"][:, t, :, :], hs[:, :, t, :, CLS].rearrange("p b k -> p k b")))

        @block.tensor
        def _(pe):
            pe.wait_ge(const_ok, 6)
            pe.wait_ge(part_ok, 1)
            pe.matmul(bank[0][:, 0:B * 10], ones[:, :], part[:, :, :].rearrange("p b m -> p (b m)"), start=True, stop=True).then_inc(tot_ok, 1)
            pe.wait_ge(small_in, 32)
            pe.wait_ge(xn_ok, 1)
            for b in range(B):
                for k in range(KC):
                    for j in range(QT):
                        t = pe.transpose(bank[b][:, (k * QT + j) * P:(k * QT + j + 1) * P], xt[:, QT * b + j, k * P:(k + 1) * P], ident[:, :])
                t.then_inc(tr_ok, 1)
            pe.wait_ge(lo_ok, 1)
            for k in range(KC):
                t = pe.transpose(bank[0][:, k * B:(k + 1) * B], xt[0:B, NT - 1, k * P:(k + 1) * P], ident[0:B, 0:B])
            t.then_inc(tr_ok, 1)


def layer_norm_rows(v, step, x, out, stats, mv, rstd, var_ok, y0_ok):
    rows = lambda t: P if t < NT - 1 else B
    for t in range(NT):
        step(v.bn_stats(stats[0:rows(t), t, :], x[0:rows(t), t, :]), t == NT - 1)
    for t in range(NT):
        step(v.bn_aggr(mv[0:rows(t), t, :], stats[0:rows(t), t, :]), t == NT - 1)
    var, y, y2 = rstd[:, 2, :], rstd[:, 1, :], rstd[:, 0, :]
    step(v.tensor_scalar(var, mv[:, :, 1], EPS, None, ALU.add))
    v.sem_inc(var_ok, 1)
    v.wait_ge(y0_ok, 1)
    step(v.tensor_tensor(y2, y, y, ALU.mult))
    step(v.tensor_tensor(y2, y2, var, ALU.mult))
    step(v.tensor_scalar(y2, y2, -0.5, 1.5, ALU.mult, ALU.add))
    step(v.tensor_tensor(y, y, y2, ALU.mult))
    for t in range(NT):
        step(v.tensor_scalar(out[0:rows(t), t, :], x[0:rows(t), t, :], mv[0:rows(t), t, 0:1], rstd[0:rows(t), 1, t:t + 1],
                             ALU.subtract, ALU.mult), t == NT - 1)


class At:

    def __init__(self, eng, g):
        self.eng, self.g, self.kept = eng, g, {}

    def __call__(self, per, off):
        if isinstance(self.g, int):
            return per * self.g + off
        if per not in self.kept:
            self.kept[per] = self.eng.snap(self.g * per)
        return self.kept[per] + off if off else self.kept[per]

    def put(self, reg, per, off):
        value = self(per, off)
        if isinstance(value, int):
            return value
        self.eng.reg_mov(reg, value)
        return reg

    def prepare(self, *pers):
        for per in pers:
            self(per, 0)


VBD_IMAGE = H * (2 * HD + DH)


def vbd_rows(vbd, b):
    return vbd[b, 0:H * 2 * HD].rearrange("(h n) -> h n", h=H)


def vbd_diagonal(vbd, t):
    return vbd.rearrange("b (h n) -> b h n", h=H)[:, :, t * HD:t * HD + DH]


class Kind:

    def __init__(self, first, last, last_layer, opening, final):
        self.first, self.last, self.last_layer = first, last, last_layer
        self.ln2 = not opening
        self.next = not final
        self.entry = first and not opening
        self.closing = last and not final


OPENING = Kind(True, False, False, True, False)
MIDDLE = Kind(False, False, False, False, False)
CLOSING = Kind(False, True, False, False, False)
ENTRY = Kind(True, False, False, False, False)
TAIL = Kind(False, False, True, False, False)
FINAL = Kind(False, True, True, False, True)


def iterations(eng, body):
    body(At(eng, 0), 0, 0, OPENING)
    with eng.Fori(0, L - 1) as l:
        l8 = eng.snap(l * B)
        with eng.Fori(1, B - 1) as b:
            body(At(eng, eng.snap(l8 + b)), l, b, MIDDLE)
        body(At(eng, eng.snap(l8 + (B - 1))), l, B - 1, CLOSING)
        body(At(eng, eng.snap(l8 + B)), eng.snap(l + 1), 0, ENTRY)
    with eng.Fori(1, B - 1) as b:
        body(At(eng, eng.snap(b + (L - 1) * B)), L - 1, b, TAIL)
    body(At(eng, L * B - 1), L - 1, B - 1, FINAL)


PLAIN, CENTRED = C_O // SPLIT, (W_COLS - C_O) // SPLIT
E_CHUNKS = E_COLS // SPLIT


def chunk_plan(b, kind):
    if kind.first:
        return (("we", None, E_CHUNKS, False),)
    if kind is MIDDLE:
        return (("w", PLAIN + (b - 1) * 2, 2, True), ("w", (b - 1) * 6, 6, False))
    if kind is CLOSING:
        return (("w", PLAIN + 12, 2, True), ("w", 36, 4, False), ("w", PLAIN + 14, 2, True))
    if kind is TAIL:
        return (("we", L * E_CHUNKS + (b - 1) * 8, 8, False),)
    return ()


def chunks_before(at, l, kind):
    if isinstance(at.g, int):
        return 4 * at.g + 2 * l + (0 if kind.first else 2)
    return at.eng.snap(at.g * 4 + l * 2 + (0 if kind.first else 2))


def attention_stage(nc, io, keep):
    with ExitStack() as ctx:
        sb = lambda n, s, d=F32: ctx.enter_context(nc.sbuf_tensor(n, s, d))
        sem = lambda n: ctx.enter_context(nc.semaphore(n))
        W, ident, hcls = keep["w"], keep["ident"], keep["hcls"]
        par_all = sb("par_all", [P, L, PAR_ALL])
        par = sb("par", [P, PAR_ALL])
        uv = sb("uv", [P, 2, NP])
        u16 = sb("u16", [P, NP])
        hmask = sb("hmask", [P, NP, H])
        wm = sb("wm", [P, NP, H])
        rT2 = sb("rT2", [P, 2, KC, S], F16)
        kr16 = sb("kr16", [P, NP, S])
        cc = sb("cc", [H, S])
        cb = sb("cb", [P, H, S])
        hin = sb("hin", [P, 2, KC, S], F16)
        hres = sb("hres", [P, 2, KC, S], F16)
        hmid = hres
        hout = sb("hout", [P, 2, KC, S], F16)
        rq = sb("rq", [P, 2, NP, S], F16)
        rk = sb("rk", [P, 2, NP, S], F16)
        qs = sb("qs", [P, H, S], F16)
        kh = sb("kh", [P, H, S], F16)
        kl = sb("kl", [P, H, S], F16)
        qbd = sb("qbd", [P, 2, NP, H], F16)
        vs = sb("vs", [P, 2, QT, HD], F16)
        vbd = sb("vbd", [P, 2, HD], F16)
        E = sb("E", [P, 2, QT, S])
        ec = sb("ec", [H, S])
        nb = sb("nb", [P, QT * H])
        nbc = sb("nbc", [H, 1])
        sums = sb("sums", [P, QT, H])
        sumc = sb("sumc", [H, 1])
        rs = sb("rs", [P, QT, H])
        ecr = sb("ecr", [H, 2, 1])
        ecol = sb("ecol", [P, QT, H])
        pt = sb("pt", [P, H, 2, QT, S], F16)
        hid = pt[:, 0:4, :, :, :].rearrange("p h t k s -> p (h t k s)").rearrange("p (t f s) -> p t f s", t=2, f=FC)
        pkr = sb("pkr", [P, 2, 2, S], F16)
        sel = sb("sel", [P, NP, P], F16)
        res_w = sb("res_w", [P, 2, P], F16)
        mean_w = sb("mean_w", [P, P])
        o2 = sb("o2", [P, 2, NP, S], F16)
        vcl = o2[0:B, :, :, :].rearrange("b t c s -> b (t c s)")[:, 0:2 * HD].rearrange("b (t n) -> b t n", t=2)
        x = sb("x", [P, KC, S])
        sq = sb("sq", [P, KC, S])
        y = sb("y", [P, S])
        t1 = sb("t1", [P, S])
        rel = sb("rel", [P, 2, S])
        eps = sb("eps", [P, 1])
        wf = sb("wf", [P, 2, SPLIT])
        wh = sb("wh", [P, 2, 2, SPLIT], F16)
        row_mean = sb("row_mean", [P, 2])
        b2_mean = sb("b2_mean", [P, L])
        bank = [ctx.enter_context(nc.psum_tensor(f"bk{i}", [P, 512], F32)) for i in range(8)]
        ident_s = ident[0:H, 0:H]

        const_in, const_ok, setup_ok = map(sem, ("const_in", "const_ok2", "setup_ok"))
        zero_out, hin_in, hres_in, vbd_in, stack_in, hd_out, vbd_out, cc_out, cb_in = map(sem, (
            "zero_out", "hin_in", "hres_in", "vbd_in", "stack_in", "hd_out2", "vbd_out", "cc_out", "cb_in"))
        w_sem = {n: sem(n) for n in ("w_qkv_in", "w_r_in", "w_o_in", "w_1_in", "w_2_in")}
        vcls_done, kr_done, cc_done, proj_done, v_done = map(sem, ("vcls_done", "kr_done", "cc_done", "proj_done", "v_done"))
        cs_done, s_done, t_done, clst_done, key_done = map(sem, ("cs_done", "s_done", "t_done", "clst_done", "key_done"))
        rb_done, o_done, wo_done, var1_done, ff1_done, ff2_done, var2_done = map(sem, (
            "rb_done", "o_done", "wo_done", "var1_done", "ff1_done", "ff2_done", "var2_done"))
        vcls_hi, kr_ok, q_ok, v_hi, ecol_ok = map(sem, ("vcls_hi", "kr_ok", "q_ok", "v_hi", "ecol_ok"))
        e_ok, ec_ok, p_hi, pc_hi, key_hi, rb_ok, o_hi = map(sem, ("e_ok", "ec_ok", "p_hi", "pc_hi", "key_hi", "rb_ok", "o_hi"))
        sq1_ok, ln1_ok, y1_ok, z1_hi, relu_ok, ff1_hi = map(sem, ("sq1_ok", "ln1_ok", "y1_ok", "z1_hi", "relu_ok", "ff1_hi"))
        sq2_ok, ln2_ok, y2_ok, z2_hi = map(sem, ("sq2_ok", "ln2_ok", "y2_ok", "z2_hi"))
        cc_ok, vcls_lo, k_ok, v_lo = map(sem, ("cc_ok", "vcls_lo", "k_ok", "v_lo"))
        qbd_ok, sc_ok, s_ok, p_lo, pc_lo, rs_ok, key_lo, on_ok, o_lo = map(sem, (
            "qbd_ok", "sc_ok", "s_ok", "p_lo", "pc_lo", "rs_ok", "key_lo", "on_ok", "o_lo"))
        par_ok, x1_ok, sum1_ok, newton1, z1_ok, z1_lo, rel_ok, ff1_lo = map(sem, (
            "par_ok", "x1_ok", "sum1_ok", "newton1", "z1_ok", "z1_lo", "rel_ok", "ff1_lo"))
        x2_ok, sum2_ok, vy_ok, sum_ok, mean_ok = map(sem, ("x2_ok", "sum2_ok", "vy_ok", "chunk_sum_ok", "chunk_mean_ok"))
        proj_hi, proj_lo, newton2, scaled2, z2_ok, z2_lo, hcls_ok = map(sem, (
            "proj_hi", "proj_lo", "newton2", "scaled2", "z2_ok", "z2_lo", "hcls_ok"))
        split_in = [sem("split_in0"), sem("split_in1")]
        split_out = [sem("split_out0"), sem("split_out1")]
        scaled, split_hi, split_lo = map(sem, ("scaled", "split_hi", "split_lo"))
        SETUP = 10 + 3 * L
        CONST = 5
        SCORE = 1.0 / (DH ** 0.5 * WS * WS)
        block = ctx.enter_context(nc.Block())

        TERMS = ((0, 0), (0, 1), (1, 0))
        OB = (7, 0, 2)
        RB = (1, 6)
        VB = (6, 7, 0, 1)
        FB = (2, 6, 7)
        wcol = lambda t, base, k, n, m: W[:, t, base + k * n + m * P:base + k * n + (m + 1) * P]
        chunk_at = lambda s: s // 2 + NP * (s % 2)
        slots = lambda h, kind: () if not kind.next else (h,) if not kind.closing else () if h < NP else (2 * h - H, 2 * h - H + 1)
        flat = lambda t: t[:, :, :, :].rearrange("p t k s -> p (t k s)")

        @block.sync
        def _(sp):
            for dst, src in ((hmask[:, :, :], io["c_hmask"]), (x[:, :, :], io["c_rT"]), (uv[:, :, :], io["uv"]),
                             (par_all[:, :, 0:PAR_COLS], io["par"]),
                             (cb[:, 0:4, 0:IMG], io["c_sel"].rearrange("p c m -> p (c m)").rearrange("p (h s) -> p h s", h=4)),
                             (cb[:, 4:4 + L, 0:IMG], io["b2"].partition_broadcast(P).rearrange("p (l d) -> p l d", l=L))):
                sp.dma_start(dst, src).then_inc(const_in, 16)
            sp.dma_start(flat(hin), io["hd"][0]).then_inc(hin_in, 16)
            sp.wait_ge(const_ok, CONST)
            for b in range(B):
                sp.dma_start(vbd_rows(io["vbd"], b), vbd[0:H, :, :].rearrange("h t n -> h (t n)")).then_inc(zero_out, 16)
            sp.wait_ge(zero_out, 16 * B)
            count = sp.alloc_register("sp_count")

            def hold(signal, n):
                if not isinstance(n, int):
                    sp.reg_mov(count, n)
                    n = count
                sp.wait_ge(const_ok, CONST)
                sp.wait_ge(signal, n)

            def store_vcls(atl):
                hold(vcls_lo, atl(2, 2))
                for t in range(2):
                    sp.dma_start(vbd_diagonal(io["vbd"], t), vcl[:, t, :].rearrange("b (h d) -> b h d", h=H)).then_inc(vbd_out, 16)
                hold(vbd_out, atl(32, 32))

            def stack(at):
                hold(proj_lo, at(16, 16))
                hold(s_done, at(32, 0))
                for a in range(2):
                    rows = slice(64 * a, 64 * a + 64)
                    for dst, src, lo in ((qs, rq, (0, 1)), (kh, rk, (0, 0)), (kl, rk, (1, 1))):
                        for half in range(2):
                            sp.dma_start(dst[64 * half:64 * half + 64, a:H:2, :], src[rows, lo[half], :, :]).then_inc(stack_in, 16)

            def chunk_list(l, b, kind):
                out = []
                for name, base, n, _ in chunk_plan(b, kind):
                    for i in range(n):
                        if name == "we":
                            j = (l * E_CHUNKS if base is None else base) + i
                            out.append((io["we"][j], io["we_split"][j]))
                        else:
                            j = base + i
                            out.append((io["w"][l + 1, j], io["w_split"][l + 1, :, :, bass.ds(j * SPLIT, SPLIT)]))
                return out

            def load_w(name, a, b, l):
                sp.dma_start(W[:, :, a:b], io["w_split"][l + 1, :, :, a:b]).then_inc(w_sem[name], 16)

            def body(at, l, b, kind):
                at.prepare(2, 4, 8, 16)
                n0 = chunks_before(at, l, kind)
                at1 = At(sp, at.g + 1)
                at1.prepare(16, 32)
                plan = chunk_list(l, b, kind)

                def load_chunk(c):
                    hold(split_lo, n0 * 2 + (c - 1) if c >= 2 else n0 * 2)
                    sp.dma_start(wf[:, c % 2, :], plan[c][0]).then_inc(split_in[c % 2], 16)

                if not kind.entry:
                    hold(o_done, at(8, 0))
                    sp.dma_start(vbd[0:H, :, :].rearrange("h t n -> h (t n)"), vbd_rows(io["vbd"], b)).then_inc(vbd_in, 16)
                hold(ff1_done, at(8, 0))
                sp.dma_start(flat(hres), io["hd"][b]).then_inc(hres_in, 16)
                if kind.next:
                    hold(v_done, at(4, 4))
                    sp.dma_start(flat(hin), io["hd"][0 if kind.closing else b + 1]).then_inc(hin_in, 16)
                if kind.closing:
                    for i in range(2):
                        hold(split_out[i], n0 * 16)
                    load_w("w_r_in", C_R, C_1, l)
                    load_w("w_qkv_in", C_QKV, C_R, l)
                for c in range(2 if plan else 0):
                    load_chunk(c)
                if kind.ln2:
                    store(at, (B if kind.entry else b) - 1)
                if kind.entry:
                    store_vcls(At(sp, l))
                    sp.dma_start(vbd[0:H, :, :].rearrange("h t n -> h (t n)"), vbd_rows(io["vbd"], b)).then_inc(vbd_in, 16)
                if kind.next:
                    stack(at1)
                for c in range(len(plan)):
                    hold(split_lo, n0 * 2 + (c + 1))
                    sp.dma_start(plan[c][1], wh[:, c % 2, :, :]).then_inc(split_out[c % 2], 16)
                    if c + 2 < len(plan):
                        load_chunk(c + 2)
                if kind.closing:
                    for i in range(2):
                        hold(split_out[i], (n0 + 4) * 16)
                    hold(wo_done, at(2, 2))
                    load_w("w_o_in", C_O, C_2, l)
                    hold(ff1_done, at(8, 8))
                    load_w("w_1_in", C_1, C_O, l)
                    hold(ff2_done, at(2, 2))
                    load_w("w_2_in", C_2, W_COLS, l)

            def store(at, b):
                hold(z2_lo, at(2, 0))
                hold(hd_out, at(16, -16))
                sp.dma_start(io["hd"][b], flat(hout)).then_inc(hd_out, 16)

            store_vcls(At(sp, 0))
            stack(At(sp, 0))
            iterations(sp, body)
            store(At(sp, L * B), B - 1)
            sp.wait_ge(hd_out, 16 * L * B)
            for i in range(2):
                sp.wait_ge(split_out[i], 16 * ((L - 1) * (PLAIN + CENTRED) + E_N * E_CHUNKS) // 2)

        @block.gpsimd
        def _(pool):
            count, count2 = pool.alloc_register("pool_count"), pool.alloc_register("pool_count2")
            pool.memset(mean_w[:, :], 1.0 / D).then_inc(const_ok, 1)
            pool.memset(qbd[:, :, :, :], 0.0).then_inc(const_ok, 1)
            pool.memset(vbd[:, :, :], 0.0).then_inc(const_ok, 1)
            pool.memset(pkr[:, :, :, :], 0.0).then_inc(const_ok, 1)
            pool.memset(eps[:, :], EPS).then_inc(const_ok, 1)

            def split_projection(at, s):
                j = chunk_at(s)
                dst = rq if j < NP else rk
                n = at.put(count, 8, s // 2 + 1)
                pool.wait_ge(const_ok, CONST)
                pool.wait_ge(q_ok if j < NP else k_ok, n)
                pool.tensor_scalar(dst[:, 0, j % NP, :], rel[:, s % 2, :], 1.0, 1.0, ALU.mult, ALU.mult).then_inc(proj_hi, 1)
                pool.wait_ge(proj_hi, at(16, s + 1))
                pool.tensor_tensor(dst[:, 1, j % NP, :], rel[:, s % 2, :], dst[:, 0, j % NP, :], ALU.subtract).then_inc(proj_lo, 1)

            def ln2_newton(at):
                pool.wait_ge(vy_ok, at(1, 0))
                pool.tensor_tensor(t1[:, :], t1[:, :], y[:, :], ALU.mult).then_inc(newton2, 1)
                n = at.put(count, 3, -2)
                pool.wait_ge(const_ok, CONST)
                pool.wait_ge(newton2, n)
                pool.tensor_scalar(t1[:, :], t1[:, :], -0.5, 1.5, ALU.mult, ALU.add).then_inc(newton2, 1)
                pool.wait_ge(newton2, at(3, -1))
                pool.tensor_tensor(y[:, :], y[:, :], t1[:, :], ALU.mult).then_inc(newton2, 1)

            def ln2_normalise(at):
                for k in range(KC):
                    pool.wait_ge(newton2, at(3, 0))
                    pool.tensor_tensor(x[:, k, :], x[:, k, :], y[:, :], ALU.mult).then_inc(scaled2, 1)

            def ln2_gain(at):
                for k in range(KC):
                    n = at.put(count, 2, k - 1)
                    pool.wait_ge(const_ok, CONST)
                    pool.wait_ge(scaled2, n)
                    pool.tensor_scalar(x[:, k, :], x[:, k, :], par[:, G2 + k:G2 + k + 1], par[:, B2 + k:B2 + k + 1],
                                       ALU.mult, ALU.add).then_inc(z2_ok, 1)

            def ln2_lo(at, b):
                for k in range(KC):
                    pool.wait_ge(z2_hi, at(2, k - 1))
                    pool.tensor_tensor(hout[:, 1, k, :], x[:, k, :], hout[:, 0, k, :], ALU.subtract).then_inc(z2_lo, 1)
                n = at.put(count, 2, 0)
                pool.wait_ge(const_ok, CONST)
                pool.wait_ge(z2_lo, n)
                pool.tensor_copy(hcls[:, :, :, b], hout[:, :, :, CLS]).then_inc(hcls_ok, 1)

            def split_chunks(at, l, b, kind):
                n0 = chunks_before(at, l, kind)
                c = centred_before = 0
                for _, _, n, centred in chunk_plan(b, kind):
                    for _ in range(n):
                        i = c % 2
                        pool.reg_mov(count, n0 * 16 + 16 * (c // 2 + 1))
                        if centred:
                            centred_before += 1
                            m = at.put(count2, 2, centred_before - 2)
                        pool.wait_ge(const_ok, CONST)
                        pool.wait_ge(split_in[i], count)
                        if centred:
                            pool.wait_ge(mean_ok, m)
                            pool.tensor_scalar(wf[:, i, :], wf[:, i, :], WS, row_mean[:, i:i + 1], ALU.mult, ALU.add).then_inc(scaled, 1)
                        else:
                            pool.tensor_scalar(wf[:, i, :], wf[:, i, :], WS, 1.0, ALU.mult, ALU.mult).then_inc(scaled, 1)
                        pool.reg_mov(count, n0 * 2 + (c + 1))
                        pool.reg_mov(count2, n0 * 16 + 16 * (c // 2))
                        pool.wait_ge(const_ok, CONST)
                        pool.wait_ge(scaled, count)
                        pool.wait_ge(split_out[i], count2)
                        pool.tensor_scalar(wh[:, i, 0, :], wf[:, i, :], 1.0, 1.0, ALU.mult, ALU.mult).then_inc(split_hi, 1)
                        pool.wait_ge(split_hi, n0 * 2 + (c + 1))
                        pool.tensor_tensor(wh[:, i, 1, :], wf[:, i, :], wh[:, i, 0, :], ALU.subtract).then_inc(split_lo, 1)
                        c += 1

            for s in range(2 * NP):
                split_projection(At(pool, 0), s)

            def body(at, l, b, kind):
                at1 = At(pool, at.g + 1)
                for h in range(H):
                    for s in slots(h, kind):
                        split_projection(at1, s)
                    if h == 3 and kind.ln2:
                        ln2_newton(at)
                    if h == 4 and kind.ln2:
                        ln2_normalise(at)
                    if h == 5 and kind.ln2:
                        ln2_gain(at)
                    if h == 9 and kind.ln2:
                        ln2_lo(at, (B if kind.entry else b) - 1)
                if chunk_plan(b, kind):
                    split_chunks(at, l, b, kind)

            iterations(pool, body)
            ln2_newton(At(pool, L * B))
            ln2_normalise(At(pool, L * B))
            ln2_gain(At(pool, L * B))
            ln2_lo(At(pool, L * B), B - 1)

        @block.tensor
        def _(pe):
            mm = pe.matmul
            count = pe.alloc_register("pe_count")

            def project(at, s):
                if s >= 2 or not isinstance(at.g, int) or at.g:
                    pe.wait_ge(q_ok if s % 2 == 0 else k_ok, at(8, s // 2))
                for i, (k, (a, m)) in enumerate((k, t) for k in range(KC) for t in TERMS):
                    r = mm(bank[4 + s % 2][:, 0:S], wcol(a, C_QKV, k, 3 * HD, chunk_at(s)), hin[:, m, k, :], start=i == 0, stop=i == 5)
                r.then_inc(proj_done, 1)

            def project_r(atl, j):
                if j >= 2:
                    pe.wait_ge(kr_ok, atl(8, j - 1))
                for i, (k, (a, m)) in enumerate((k, t) for k in range(KC) for t in TERMS):
                    r = mm(bank[4 + j % 2][:, 0:S], wcol(a, C_R, k, HD, j), rT2[:, m, k, :], start=i == 0, stop=i == 5)
                r.then_inc(kr_done, 1)

            def project_v(at, u):
                tt, half = divmod(u, 2)
                c0 = C_QKV + 2 * HD + half * 512
                for i, (k, (a, m)) in enumerate((k, t) for k in range(KC) for t in TERMS):
                    r = mm(bank[VB[u]][:, :], hin[:, m, k, tt * P:(tt + 1) * P],
                           W[:, a, c0 + k * 3 * HD:c0 + k * 3 * HD + 512], start=i == 0, stop=i == 5)
                r.then_inc(v_done, 1)

            def class_v():
                for half in range(2):
                    c0 = C_QKV + 2 * HD + half * 512
                    for i, (k, (a, m)) in enumerate((k, t) for k in range(KC) for t in TERMS):
                        r = mm(bank[6 + half][0:B, :], hcls[:, m, k, :], W[:, a, c0 + k * 3 * HD:c0 + k * 3 * HD + 512],
                               start=i == 0, stop=i == 5)
                    r.then_inc(vcls_done, 1)

            def position_term(atl):
                pe.wait_ge(kr_ok, atl(8, 8))
                for c in range(NP):
                    r = mm(bank[2][0:H, 0:S], wm[:, c, :], kr16[:, c, :], start=c == 0, stop=c == NP - 1)
                r.then_inc(cc_done, 1)

            def variance(ready, n, bk, done):
                pe.wait_ge(ready, n)
                mm(bank[bk][:, 0:S], mean_w[:, :], t1[:, :], start=True, stop=True).then_inc(done, 1)

            def transposes(at, h):
                pe.wait_ge(e_ok, at(32, 2 * h + 2))
                if h >= 2:
                    pe.wait_ge(p_lo, at(16, h - 1))
                for kt in range(QT):
                    for qt in range(QT):
                        r = pe.transpose(bank[2 + h % 2][:, (kt * QT + qt) * P:(kt * QT + qt + 1) * P],
                                         E[:, h % 2, qt, kt * P:(kt + 1) * P], ident[:, :])
                r.then_inc(t_done, 1)

            def pv(at, c):
                pe.wait_ge(p_lo, at(16, 2 * c + 2))
                o = bank[OB[c % 3]]
                for kt in range(QT):
                    for i, (a, m) in enumerate(TERMS):
                        for s_ in range(2):
                            h = 2 * c + s_
                            mm(o[DH * s_:DH * (s_ + 1), 0:S], vs[:, a, kt, h * DH:(h + 1) * DH], pt[:, h, m, kt, :],
                               start=kt + i == 0, stop=False)

            pe.wait_ge(const_ok, CONST)
            pe.wait_ge(setup_ok, SETUP)
            first = At(pe, 0)
            for j in range(NP):
                project_r(first, j)
            class_v()
            position_term(first)
            pe.wait_ge(hin_in, 16)
            for s in range(2 * NP):
                project(first, s)
            pe.wait_ge(vcls_lo, 2)
            for u in range(4):
                project_v(first, u)

            def body(at, l, b, kind):
                at1 = At(pe, at.g + 1)
                atl, atl1 = At(pe, l), At(pe, l + 1)
                pe.wait_ge(v_lo, at(4, 4))
                pe.wait_ge(qbd_ok, at(2, 2))
                for c in range(NP):
                    for i, (a, m) in enumerate(TERMS):
                        r = mm(bank[6][0:H, 0:S], qbd[:, a, c, :], rk[:, m, c, :], start=c + i == 0, stop=(c == NP - 1 and i == 2))
                r.then_inc(cs_done, 1)
                pe.wait_ge(stack_in, at(192, 192))
                if kind.next:
                    pe.wait_ge(hin_in, at(16, 32))
                for h in range(H):
                    for qt in range(QT):
                        if h:
                            pe.wait_ge(s_ok, at(32, 2 * h + qt - 1))
                        q = qs[:, h, qt * P:(qt + 1) * P]
                        mm(bank[qt][:, 0:S], q, kh[:, h, :], start=True, stop=False)
                        mm(bank[qt][:, 0:S], q, kl[:, h, :], start=False, stop=True).then_inc(s_done, 1)
                    if h == 0 and kind.ln2:
                        pe.wait_ge(sq2_ok, at(2, 0))
                        pe.wait_ge(x2_ok, at(2, 0))
                    if kind.closing and h < NP:
                        if h == 0:
                            pe.wait_ge(w_sem["w_r_in"], atl1(16, 0))
                        project_r(atl1, h)
                    if kind.closing and h == NP:
                        pe.wait_ge(kr_ok, atl1(8, 8))
                        pe.wait_ge(w_sem["w_qkv_in"], atl1(16, 0))
                    late = h == H - 1
                    if not late:
                        for s in slots(h, kind):
                            project(at1, s)
                    if h == 0 and kind.ln2:
                        variance(sum2_ok, at(1, 0), 7, var2_done)
                    if h:
                        transposes(at, h - 1)
                    if h == 1:
                        n = at.put(count, 1, 1)
                        pe.wait_ge(setup_ok, SETUP)
                        pe.wait_ge(ec_ok, n)
                        pe.wait_ge(sc_ok, n)
                        for kt in range(QT):
                            r = pe.transpose(bank[6][:, kt * H:(kt + 1) * H], ec[:, kt * P:(kt + 1) * P], ident_s)
                        r.then_inc(clst_done, 1)
                    if h == NP + 3 and kind.entry:
                        pe.wait_ge(hcls_ok, atl(8, 0))
                        pe.wait_ge(pc_lo, at(1, 1))
                        class_v()
                pe.wait_ge(pc_lo, at(1, 1))
                if kind.ln2:
                    pe.wait_ge(vy_ok, at(1, 0))
                if kind.entry:
                    pe.wait_ge(vcls_lo, atl(2, 2))
                pv(at, 0)
                for s in slots(H - 1, kind):
                    project(at1, s)
                transposes(at, H - 1)
                pe.wait_ge(s_ok, at(32, 32))
                pv(at, 1)
                pe.wait_ge(ecol_ok, at(16, 16))
                pe.wait_ge(rs_ok, at(3, 3))
                for i, src in enumerate((ecol, rs)):
                    for qt in range(QT):
                        r = pe.transpose(bank[6][0:H, (i * QT + qt) * P:(i * QT + qt + 1) * P], src[:, qt, :], ident[:, :])
                r.then_inc(key_done, 1)
                for c in range(NP):
                    if c == 0:
                        pe.wait_ge(p_lo, at(16, H - 1))
                        pv(at, 2)
                        pe.wait_ge(key_lo, at(2, 2))
                        pe.wait_ge(vbd_in, at(16, 16))
                    if c >= 2:
                        pe.wait_ge(rb_ok, at(8, c - 1))
                    for i in range(2):
                        r = mm(bank[RB[c % 2]][:, 0:S], sel[:, c, :], pkr[:, i, 1, :], start=i == 0, stop=i == 1)
                    r.then_inc(rb_done, 1)
                    for i, (a, m) in enumerate(TERMS):
                        r = mm(bank[OB[c % 3]][:, 0:S], vbd[:, a, c * P:(c + 1) * P], pkr[:, m, 0, :], start=False, stop=i == 2)
                    r.then_inc(o_done, 1)
                    if 1 <= c < NP - 2:
                        pe.wait_ge(on_ok, at(8, c))
                        pv(at, c + 2)
                pe.wait_ge(hres_in, at(16, 16))
                if kind.entry:
                    pe.wait_ge(w_sem["w_o_in"], atl(16, 0))
                for m_ in range(KC):
                    for i, k in ((i, k) for i in range(2) for k in range(KC)):
                        mm(bank[4 + m_][:, 0:S], res_w[:, int(k != m_), :], hres[:, i, k, :], start=i + k == 0, stop=False)
                    for c in range(NP):
                        if m_ == 0:
                            pe.wait_ge(o_lo, at(8, c + 1))
                        for i, (a, m) in enumerate(TERMS):
                            r = mm(bank[4 + m_][:, 0:S], wcol(a, C_O, c, D, m_), o2[:, m, c, :], start=False, stop=(c == NP - 1 and i == 2))
                    r.then_inc(wo_done, 1)
                if kind.next:
                    project_v(at1, 0)
                variance(sum1_ok, at(1, 1), 3, var1_done)
                if kind.closing:
                    position_term(atl1)
                if kind.next:
                    for u in range(1, 4):
                        project_v(at1, u)
                pe.wait_ge(z1_lo, at(2, 2))
                if kind.next:
                    pe.wait_ge(v_lo, at1(4, 2))
                if kind.closing:
                    pe.wait_ge(cc_ok, atl1(1, 1))
                if kind.entry:
                    pe.wait_ge(w_sem["w_1_in"], atl(16, 0))
                for j in range(FC):
                    if j >= 3:
                        pe.wait_ge(ff1_hi, at(8, j - 2))
                        if j % 2:
                            pe.wait_ge(rel_ok, at(4, (j - 3) // 2 + 1))
                    for i, (k, (a, m)) in enumerate((k, t) for k in range(KC) for t in TERMS):
                        r = mm(bank[FB[j % 3]][:, 0:S], wcol(a, C_1, k, DF, j), hmid[:, m, k, :], start=i == 0, stop=i == 5)
                    r.then_inc(ff1_done, 1)
                if kind.entry:
                    pe.wait_ge(w_sem["w_2_in"], atl(16, 0))
                for m_ in range(KC):
                    for c in range(FC):
                        if m_ == 0:
                            pe.wait_ge(ff1_lo, at(8, c + 1))
                        for i, (a, m) in enumerate(TERMS):
                            r = mm(bank[4 + m_][:, 0:S], wcol(a, C_2, c, D, m_), hid[:, m, c, :], start=c + i == 0, stop=(c == FC - 1 and i == 2))
                    r.then_inc(ff2_done, 1)

            iterations(pe, body)
            variance(sum2_ok, L * B, 7, var2_done)

        @block.scalar
        def _(act):
            def take_q(at, s):
                act.wait_ge(proj_done, at(16, s + 1))
                if s or not isinstance(at.g, int) or at.g:
                    act.wait_ge(proj_lo, at(16, s - 1))
                j = chunk_at(s)
                act.activation(rel[:, s % 2, :], bank[4 + s % 2][:, 0:S], ACT.Identity, bias=u16[:, j:j + 1]).then_inc(q_ok, 1)

            def take_kr(atl, j):
                act.wait_ge(kr_done, atl(8, j + 1))
                act.activation(kr16[:, j, :], bank[4 + j % 2][:, 0:S], ACT.Copy).then_inc(kr_ok, 1)

            def v_part(at, u):
                act.wait_ge(v_done, at(4, u + 1))
                tt, half = divmod(u, 2)
                act.activation(vs[:, 0, tt, half * 512:half * 512 + 512], bank[VB[u]][:, :], ACT.Copy).then_inc(v_hi, 1)

            def class_v(atl):
                for half in range(2):
                    act.wait_ge(vcls_done, atl(2, half + 1))
                    act.activation(vcl[:, 0, half * 512:half * 512 + 512], bank[6 + half][0:B, :], ACT.Copy).then_inc(vcls_hi, 1)

            def first_rstd(var_done, n, bk, log_ok, y_ok):
                act.wait_ge(var_done, n)
                act.activation(y[:, :], bank[bk][:, 0:S], ACT.Ln, bias=eps[:, 0:1]).then_inc(log_ok, 1)
                act.wait_ge(log_ok, n)
                act.activation(y[:, :], y[:, :], ACT.Exp, scale=-0.5).then_inc(y_ok, 1)

            def ln2_hi(at):
                act.wait_ge(hd_out, at(16, -16))
                for k in range(KC):
                    act.wait_ge(z2_ok, at(2, k - 1))
                    act.activation(hout[:, 0, k, :], x[:, k, :], ACT.Copy).then_inc(z2_hi, 1)

            def spread_position_term(atl):
                act.wait_ge(cc_ok, atl(1, 1))
                act.dma_start(io["cc"].rearrange("(h s) -> h s", h=H), cc[:, :]).then_inc(cc_out, 16)

            def load_position_term(atl):
                act.wait_ge(cc_out, atl(16, 16))
                act.dma_start(cb[:, :, :].rearrange("p h s -> p (h s)"), io["cc"].partition_broadcast(P)).then_inc(cb_in, 16)

            nc.scalar.preload_act_table_set("natural_log_exp_and_others")
            act.wait_ge(const_ok, CONST)
            act.wait_ge(setup_ok, SETUP)
            first = At(act, 0)
            for j in range(NP):
                take_kr(first, j)
            class_v(first)
            spread_position_term(first)
            load_position_term(first)
            for s in range(0, 2 * NP, 2):
                take_q(first, s)
            for u in range(4):
                v_part(first, u)

            def p_part(at, h):
                act.wait_ge(t_done, at(16, h + 1))
                act.activation(pt[:, h, 0, :, 0:IMG], bank[2 + h % 2][:, :].rearrange("p (k s) -> p k s", k=QT), ACT.Copy).then_inc(p_hi, 1)

            def o_part(at, c):
                act.wait_ge(on_ok, at(8, c + 1))
                act.activation(o2[:, 0, c, :], x[:, c % 2, :], ACT.Copy).then_inc(o_hi, 1)

            def body(at, l, b, kind):
                at1, atl, atl1 = At(act, at.g + 1), At(act, l), At(act, l + 1)
                act.wait_ge(sc_ok, at(1, 1))
                act.activation(ec[:, :], ec[:, :], ACT.Exp, bias=nbc[:, 0:1], scale=-1.0, accum_out=sumc[:, 0:1]).then_inc(ec_ok, 1)
                for h in range(H):
                    for qt in range(QT):
                        act.wait_ge(s_ok, at(32, 2 * h + qt + 1))
                        act.activation(E[:, h % 2, qt, :], E[:, h % 2, qt, :], ACT.Exp, bias=nb[:, 2 * h + qt:2 * h + qt + 1],
                                       scale=-1.0, accum_out=sums[:, qt, h:h + 1]).then_inc(e_ok, 1)
                    if kind.closing and h < NP:
                        take_kr(atl1, h)
                    for s in slots(h, kind):
                        if s % 2 == 0:
                            take_q(at1, s)
                    if h == 1 and kind.ln2:
                        first_rstd(var2_done, at(1, 0), 7, ln2_ok, y2_ok)
                    if h == 8 and kind.ln2:
                        ln2_hi(at)
                    if h == 2:
                        act.wait_ge(clst_done, at(1, 1))
                        act.activation(pt[:, :, 0, :, CLS], bank[6][:, 0:QT * H].rearrange("p (k h) -> p h k", k=QT), ACT.Copy).then_inc(pc_hi, 1)
                    if h:
                        p_part(at, h - 1)
                    if h == NP + 4 and kind.entry:
                        class_v(atl)
                    act.wait_ge(e_ok, at(32, 2 * h + 2))
                    act.activation(ecol[:, :, h:h + 1], E[:, h % 2, :, CLS:S], ACT.Copy).then_inc(ecol_ok, 1)
                p_part(at, H - 1)
                act.wait_ge(key_done, at(1, 1))
                act.activation(pkr[0:H, 0, :, 0:IMG], bank[6][0:H, :].rearrange("p (t s) -> p t s", t=2), ACT.Copy).then_inc(key_hi, 1)
                act.activation(pkr[0:H, 0, :, CLS:S], ecr[:, :, :], ACT.Copy).then_inc(key_hi, 1)
                for c in range(NP):
                    act.wait_ge(rb_done, at(8, c + 1))
                    if c >= 2:
                        act.wait_ge(on_ok, at(8, c - 1))
                    act.activation(sq[:, c % 2, :], bank[RB[c % 2]][:, 0:S], ACT.Copy, scale=1.0 / WS).then_inc(rb_ok, 1)
                    if c:
                        o_part(at, c - 1)
                o_part(at, NP - 1)
                for m in range(KC):
                    act.wait_ge(wo_done, at(2, m + 1))
                    act.activation(sq[:, m, :], bank[4 + m][:, 0:S], ACT.Square, scale=1.0 / WS).then_inc(sq1_ok, 1)
                if kind.next:
                    v_part(at1, 0)
                first_rstd(var1_done, at(1, 1), 3, ln1_ok, y1_ok)
                if kind.closing:
                    spread_position_term(atl1)
                if kind.next:
                    v_part(at1, 1)
                for k in range(KC):
                    act.wait_ge(z1_ok, at(2, k + 1))
                    act.activation(hmid[:, 0, k, :], x[:, k, :], ACT.Identity, bias=par[:, B1 + k:B1 + k + 1]).then_inc(z1_hi, 1)
                if kind.next:
                    v_part(at1, 2)
                    v_part(at1, 3)
                if kind.closing:
                    load_position_term(atl1)
                if kind.next:
                    act.wait_ge(proj_lo, at1(16, 16))
                for j in range(FC):
                    act.wait_ge(ff1_done, at(8, j + 1))
                    if j % 2:
                        act.wait_ge(ff1_lo, at(8, j - 1))
                        act.activation(rel[:, 1, :], bank[FB[j % 3]][:, 0:S], ACT.Relu, bias=par[:, BF1 + j:BF1 + j + 1], scale=1.0 / WS).then_inc(relu_ok, 1)
                    act.activation(hid[:, 0, j, :], bank[FB[j % 3]][:, 0:S], ACT.Relu, bias=par[:, BF1 + j:BF1 + j + 1], scale=1.0 / WS).then_inc(ff1_hi, 1)
                for m in range(KC):
                    act.wait_ge(ff2_done, at(2, m + 1))
                    act.activation(sq[:, m, :], bank[4 + m][:, 0:S], ACT.Square, bias=par[:, BF2 + m:BF2 + m + 1], scale=1.0 / WS).then_inc(sq2_ok, 1)

            iterations(act, body)
            first_rstd(var2_done, L * B, 7, ln2_ok, y2_ok)
            ln2_hi(At(act, L * B))

        @block.vector
        def _(v):
            n = [0]
            count = v.alloc_register("dve_count")

            def setup(ins):
                n[0] += 1
                ins.then_inc(setup_ok, 1)
                v.wait_ge(setup_ok, n[0])

            v.wait_ge(const_in, 16 * 6)
            v.wait_ge(const_ok, CONST)
            setup(v.tensor_scalar(u16[:, :], uv[:, 0, :], WS, None, ALU.mult))
            setup(v.tensor_tensor(uv[:, 1, :], uv[:, 1, :], uv[:, 0, :], ALU.subtract))
            setup(v.tensor_scalar(uv[:, 1, :], uv[:, 1, :], WS, None, ALU.mult))
            setup(v.tensor_tensor(wm[:, :, :], hmask[:, :, :], uv[:, 1, :].unsqueeze(2).broadcast_to([P, NP, H]), ALU.mult))
            setup(v.tensor_scalar(res_w[:, 0, :], ident[:, :], WS, -WS / D, ALU.mult, ALU.add))
            setup(v.memset(res_w[:, 1, :], -WS / D))
            setup(v.tensor_copy(sel[:, :, :].rearrange("p c m -> p (c m)").rearrange("p (h s) -> p h s", h=4), cb[:, 0:4, 0:IMG]))
            setup(v.tensor_copy(rT2[:, 0, :, :], x[:, :, :]))
            setup(v.tensor_tensor(rT2[:, 1, :, :], x[:, :, :], rT2[:, 0, :, :], ALU.subtract))
            for l in range(L):
                setup(v.tensor_reduce(b2_mean[:, l:l + 1], cb[:, 4 + l, 0:IMG], AX.X, ALU.add))
                setup(v.scalar_tensor_tensor(par_all[:, l, BF2:BF2 + KC], b2_mean[:, l:l + 1].broadcast_to([P, KC]), -1.0 / D,
                                             par_all[:, l, BF2:BF2 + KC], ALU.mult, ALU.add))
                setup(v.tensor_scalar(par_all[:, l, BF1W:BF1W + FC], par_all[:, l, BF1:BF1 + FC], WS, None, ALU.mult))
            setup(v.tensor_copy(par[:, :], par_all[:, 0, :]))

            def take_k(at, s):
                j = chunk_at(s)
                v.wait_ge(proj_done, at(16, s + 1))
                v.wait_ge(proj_lo, at(16, s - 1))
                v.tensor_tensor(rel[:, s % 2, :], bank[4 + s % 2][:, 0:S], kr16[:, j - NP, :], ALU.add).then_inc(k_ok, 1)

            def v_part(at, u):
                v.wait_ge(v_hi, at(4, u + 1))
                tt, half = divmod(u, 2)
                c = slice(half * 512, half * 512 + 512)
                v.tensor_tensor(vs[:, 1, tt, c], bank[VB[u]][:, :], vs[:, 0, tt, c], ALU.subtract).then_inc(v_lo, 1)

            def class_v(atl):
                for half in range(2):
                    v.wait_ge(vcls_hi, atl(2, half + 1))
                    c = slice(half * 512, half * 512 + 512)
                    v.tensor_tensor(vcl[:, 1, c], bank[6 + half][0:B, :], vcl[:, 0, c], ALU.subtract).then_inc(vcls_lo, 1)

            def class_q(at):
                v.wait_ge(proj_lo, at(16, 16))
                for a in range(2):
                    rows = slice(DH * a, DH * a + DH)
                    v.tensor_copy(qbd[rows, :, :, :].rearrange("p t c h -> p t (c h)")[:, :, a::H + 2][:, :, 0:NP],
                                  rq[rows, :, :, CLS]).then_inc(qbd_ok, 1)

            def position_term(atl):
                v.wait_ge(cc_done, atl(1, 1))
                v.tensor_copy(cc[:, :], bank[2][0:H, 0:S]).then_inc(cc_ok, 1)

            def sum_squares(ready, n, done):
                v.wait_ge(ready, n)
                v.tensor_tensor(t1[:, :], sq[:, 0, :], sq[:, 1, :], ALU.add).then_inc(done, 1)

            def variance_y(y_ok, n, bk, done):
                v.wait_ge(y_ok, n)
                v.scalar_tensor_tensor(t1[:, :], bank[bk][:, 0:S], EPS, y[:, :], ALU.add, ALU.mult).then_inc(done, 1)

            first = At(v, 0)
            class_v(first)
            position_term(first)
            v.wait_ge(kr_ok, NP)
            for s in range(1, 2 * NP, 2):
                take_k(first, s)
            for u in range(4):
                v_part(first, u)
            class_q(first)

            def p_part(at, h):
                v.wait_ge(p_hi, at(16, h + 1))
                v.tensor_tensor(pt[:, h, 1, :, 0:IMG], bank[2 + h % 2][:, :].rearrange("p (k s) -> p k s", k=QT),
                                pt[:, h, 0, :, 0:IMG], ALU.subtract).then_inc(p_lo, 1)

            def o_part(at, c):
                v.wait_ge(o_hi, at(8, c + 1))
                v.tensor_tensor(o2[:, 1, c, :], x[:, c % 2, :], o2[:, 0, c, :], ALU.subtract).then_inc(o_lo, 1)

            def chunk_mean(at, l, kind, c, k):
                i = c % 2
                n0 = chunks_before(at, l, kind)
                v.wait_ge(split_in[i], n0 * 16 + 16 * (c // 2 + 1))
                v.tensor_reduce(row_mean[:, i:i + 1], wf[:, i, :], AX.X, ALU.add).then_inc(sum_ok, 1)
                v.wait_ge(sum_ok, at(2, k - 1))
                v.tensor_scalar(row_mean[:, i:i + 1], row_mean[:, i:i + 1], -WS / SPLIT, None, ALU.mult).then_inc(mean_ok, 1)

            def body(at, l, b, kind):
                at1, atl, atl1 = At(v, at.g + 1), At(v, l), At(v, l + 1)
                cs_count = at.put(count, 1, 1)
                v.wait_ge(setup_ok, SETUP)
                v.wait_ge(cs_done, cs_count)
                v.tensor_tensor_reduce(ec[:, :], bank[6][0:H, 0:S], cc[:, :], -SCORE, 3e38, ALU.add, ALU.min, nbc[:, :]).then_inc(sc_ok, 1)
                if kind.first:
                    v.wait_ge(cb_in, atl(16, 16))
                for h in range(H):
                    if h >= 2:
                        v.wait_ge(t_done, at(16, h - 1))
                        v.wait_ge(ecol_ok, at(16, h - 1))
                    for qt in range(QT):
                        s_count = at.put(count, 32, 2 * h + qt + 1)
                        v.wait_ge(setup_ok, SETUP)
                        v.wait_ge(s_done, s_count)
                        v.tensor_tensor_reduce(E[:, h % 2, qt, :], bank[qt][:, 0:S], cb[:, h, :], -SCORE, 3e38,
                                               ALU.add, ALU.min, nb[:, 2 * h + qt:2 * h + qt + 1]).then_inc(s_ok, 1)
                    if h < H - 1:
                        for s in slots(h, kind):
                            if s % 2:
                                take_k(at1, s)
                    if h >= 2:
                        p_part(at, h - 2)
                    if h == 2 and kind.ln2:
                        variance_y(y2_ok, at(1, 0), 7, vy_ok)
                    if h == 3:
                        v.wait_ge(pc_hi, at(1, 1))
                        v.tensor_tensor(pt[:, :, 1, :, CLS], bank[6][:, 0:QT * H].rearrange("p (k h) -> p h k", k=QT),
                                        pt[:, :, 0, :, CLS], ALU.subtract).then_inc(pc_lo, 1)
                    if h == NP + 5 and kind.entry:
                        class_v(atl)
                p_part(at, H - 2)
                for s in slots(H - 1, kind):
                    if s % 2:
                        take_k(at1, s)
                v.wait_ge(e_ok, at(32, 32))
                v.reciprocal(rs[:, :, :], sums[:, :, :]).then_inc(rs_ok, 1)
                v.wait_ge(ec_ok, at(1, 1))
                v.tensor_copy(ecr[:, 0, :], ec[:, CLS:S]).then_inc(rs_ok, 1)
                v.reciprocal(ecr[:, 1, :], sumc[:, :]).then_inc(rs_ok, 1)
                p_part(at, H - 1)
                v.wait_ge(key_hi, at(2, 2))
                v.tensor_tensor(pkr[0:H, 1, :, 0:IMG], bank[6][0:H, :].rearrange("p (t s) -> p t s", t=2),
                                pkr[0:H, 0, :, 0:IMG], ALU.subtract).then_inc(key_lo, 1)
                v.tensor_tensor(pkr[0:H, 1, :, CLS:S], ecr[:, :, :], pkr[0:H, 0, :, CLS:S], ALU.subtract).then_inc(key_lo, 1)
                if kind.ln2:
                    v.wait_ge(z2_lo, at(2, 0))
                if kind is MIDDLE or kind is CLOSING:
                    chunk_mean(at, l, kind, 0, 0)
                    chunk_mean(at, l, kind, 1, 1)
                for c in range(NP):
                    v.wait_ge(o_done, at(8, c + 1))
                    v.wait_ge(rb_ok, at(8, c + 1))
                    if c >= 2:
                        v.wait_ge(o_lo, at(8, c - 1))
                    v.tensor_tensor(x[:, c % 2, :], bank[OB[c % 3]][:, 0:S], sq[:, c % 2, :], ALU.mult).then_inc(on_ok, 1)
                    if c:
                        o_part(at, c - 1)
                o_part(at, NP - 1)
                if kind.entry:
                    v.wait_ge(z2_lo, at(2, 0))
                    v.tensor_copy(par[:, :], par_all[:, l, :]).then_inc(par_ok, 1)
                    v.wait_ge(par_ok, atl(1, 0))
                v.wait_ge(o_lo, at(8, 8))
                for m in range(KC):
                    if m == KC - 1:
                        sum_squares(sq1_ok, at(2, 2), sum1_ok)
                    v.wait_ge(sq1_ok, at(2, m + 1))
                    v.tensor_scalar(x[:, m, :], bank[4 + m][:, 0:S], 1.0 / WS, None, ALU.mult).then_inc(x1_ok, 1)
                if kind.next:
                    v_part(at1, 0)
                variance_y(y1_ok, at(1, 1), 3, newton1)
                v.wait_ge(newton1, at(3, 1))
                v.scalar_tensor_tensor(t1[:, :], t1[:, :], -0.5, y[:, :], ALU.mult, ALU.mult).then_inc(newton1, 1)
                v.wait_ge(newton1, at(3, 2))
                v.scalar_tensor_tensor(y[:, :], t1[:, :], 1.5, y[:, :], ALU.add, ALU.mult).then_inc(newton1, 1)
                v.wait_ge(newton1, at(3, 3))
                v.wait_ge(x1_ok, at(2, 2))
                for k in range(KC):
                    v.scalar_tensor_tensor(x[:, k, :], x[:, k, :], par[:, G1 + k:G1 + k + 1], y[:, :], ALU.mult, ALU.mult).then_inc(z1_ok, 1)
                if kind.closing:
                    position_term(atl1)
                if kind.next:
                    v_part(at1, 1)
                for k in range(KC):
                    v.wait_ge(z1_hi, at(2, k + 1))
                    v.scalar_tensor_tensor(hmid[:, 1, k, :], x[:, k, :], par[:, B1 + k:B1 + k + 1], hmid[:, 0, k, :],
                                           ALU.add, ALU.subtract).then_inc(z1_lo, 1)
                if kind.next:
                    v_part(at1, 2)
                    v_part(at1, 3)
                if kind.next:
                    class_q(at1)
                if kind is CLOSING:
                    chunk_mean(at, l, kind, 6, 2)
                    chunk_mean(at, l, kind, 7, 3)
                def hidden_lo(j):
                    v.wait_ge(ff1_hi, at(8, j + 1))
                    if j % 2:
                        v.wait_ge(relu_ok, at(4, j // 2 + 1))
                        v.tensor_tensor(hid[:, 1, j, :], rel[:, 1, :], hid[:, 0, j, :], ALU.subtract).then_inc(ff1_lo, 1)
                    else:
                        v.wait_ge(rel_ok, at(4, j // 2 + 1))
                        v.scalar_tensor_tensor(hid[:, 1, j, :], rel[:, 0, :], 1.0 / WS, hid[:, 0, j, :],
                                               ALU.mult, ALU.subtract).then_inc(ff1_lo, 1)

                for j in range(0, FC, 2):
                    v.wait_ge(ff1_hi, at(8, j + 1))
                    v.wait_ge(ff1_lo, at(8, max(j - 1, 0)))
                    v.tensor_scalar(rel[:, 0, :], bank[FB[j % 3]][:, 0:S], par[:, BF1W + j:BF1W + j + 1], 0.0, ALU.add, ALU.max).then_inc(rel_ok, 1)
                    if j:
                        hidden_lo(j - 1)
                    hidden_lo(j)
                hidden_lo(FC - 1)
                v.wait_ge(z1_lo, at(2, 2))
                for m in range(KC):
                    if m == KC - 1:
                        sum_squares(sq2_ok, at(2, 2), sum2_ok)
                    v.wait_ge(sq2_ok, at(2, m + 1))
                    v.tensor_scalar(x[:, m, :], bank[4 + m][:, 0:S], 1.0 / WS, par[:, BF2 + m:BF2 + m + 1], ALU.mult, ALU.add).then_inc(x2_ok, 1)

            iterations(v, body)
            variance_y(y2_ok, L * B, 7, vy_ok)


def expert_stage(nc, io, keep):
    with ExitStack() as ctx:
        sb = lambda n, s, d=F32: ctx.enter_context(nc.sbuf_tensor(n, s, d))
        sem = lambda n: ctx.enter_context(nc.semaphore(n))
        ident = keep["ident"]
        ident_h = sb("ident_h", [P, P], F16)
        ha = sb("ha", [P, B, 2, KC, S], F16)
        y = sb("y_rows", [P, NT, D])
        xn = sb("xn_rows", [P, NT, D])
        xT = sb("xT_cols", [P, 2, KC, TOKENS], F16)
        stats = sb("stats2", [P, NT, 6])
        mv = sb("mv2", [P, NT, 2])
        rstd = sb("rstd2", [P, 3, NT])
        rw = sb("rw", [P, KC, E_G + E_N])
        rw2 = sb("rw2", [P, 2, KC, E_G + E_N], F16)
        s_ = sb("route_s", [P, NT, E_G + E_N])
        top = sb("route_top", [P, NT, 1])
        val = sb("route_val", [P, NT, 1])
        eq = sb("route_eq", [P, NT, E_G])
        rem = sb("route_rem", [P, NT, 1])
        pair_sum = sb("route_pair", [P, NT, E_G])
        wgt = sb("route_w", [P, E_N, NT])
        we = sb("we_sb", [P, 2, E_CHUNKS, 2, SPLIT], F16)
        gs = sb("gate_silu", [P, 2, 512])
        hf = sb("hidden_f", [P, 2, 512])
        hd = sb("hidden", [P, 2, 2, EFC, 512], F16)
        hc = sb("hidden_cls", [P, 2, EFC, B], F16)
        bank = [ctx.enter_context(nc.psum_tensor(f"ex{i}", [P, 512], F32)) for i in range(8)]

        ha_in, h0_in, rw_in = map(sem, ("ha_in", "h0_in3", "rw_in"))
        we_in = [sem("we_in0"), sem("we_in1")]
        zero_ok, identh_ok, res_done, h1_ok, var_ok, y0_ok, ln_ok, xn_ok = map(sem, (
            "zero_ok", "identh_ok", "res_done", "h1_ok", "var_ok3", "y0_ok3", "ln_ok3", "xn_ok3"))
        tr_done, xt_hi, xt_lo, route_done, rexp_ok, route_ok, dve = map(sem, (
            "tr_done", "xt_hi", "xt_lo", "route_done", "rexp_ok", "route_ok", "dve_step3"))
        gu_done, silu_ok, hf_ok, h_hi, h_lo, dn_done, acc_ok, out_done = map(sem, (
            "gu_done", "silu_ok", "hf_ok", "h_hi", "h_lo", "dn_done", "acc_ok", "out_done"))
        TERMS = ((0, 0), (0, 1), (1, 0))
        GATE, UP, DOWN = 0, 1024, 2048
        BLOCKS = [(i * 512, 512) for i in range(4)] + [(B * IMG, B)]
        PER = len(BLOCKS) * EFC
        cols = lambda t: slice(t * P, (t + 1) * P) if t < NT - 1 else slice(B * IMG, TOKENS)
        rows = lambda t: P if t < NT - 1 else B
        ORDER = (("h", 0), ("h", 1), ("d", 0), ("h", 2), ("d", 1), ("h", 3), ("h", 4), ("d", 2), ("d", 3), ("d", 4))
        tiles = lambda n: range(4 * n, 4 * n + 4) if n < 4 else (NT - 1,)
        block = ctx.enter_context(nc.Block())

        def images(b):
            if b < B:
                return bank[b][:, :].rearrange("p (k s) -> p k s", k=KC), (lambda t: xT[:, t, :, b * IMG:(b + 1) * IMG])
            return bank[0][:, 0:KC * B].rearrange("p (k b) -> p k b", k=KC), (lambda t: xT[:, t, :, B * IMG:TOKENS])

        def hidden(nb, t, f):
            return hd[:, nb % 2, t, f, :] if nb < 4 else hc[:, t, f, :]

        @block.sync
        def _(sp):
            sp.dma_start(ha[:, :, :, :, :].rearrange("p b t k s -> p b (t k s)"), io["hd"].rearrange("b p n -> p b n")).then_inc(ha_in, 16)
            sp.dma_start(y[:, 0:NT - 1, :], io["h0"][0:B * IMG, :].rearrange("(t p) d -> p t d", p=P)).then_inc(h0_in, 16)
            sp.dma_start(y[0:B, NT - 1, :], io["h0"][B * IMG:TOKENS, :]).then_inc(h0_in, 16)
            sp.dma_start(rw[:, :, :], io["rw"]).then_inc(rw_in, 16)
            for e in range(E_N):
                if e >= 2:
                    sp.wait_ge(dn_done, NT * (e - 1))
                sp.dma_start(we[:, e % 2, :, :, :].rearrange("p j t c -> p j (t c)"),
                             io["we_split"][e * E_CHUNKS:(e + 1) * E_CHUNKS].rearrange("j p t c -> p j (t c)")).then_inc(we_in[e % 2], 16)
            for b in range(B):
                sp.wait_ge(acc_ok, NT * (E_N - 1) + QT * (b + 1))
                sp.dma_start(io["out"][b, 1:S, :].rearrange("(j p) d -> p j d", p=P), y[:, QT * b:QT * b + QT, :]).then_inc(out_done, 16)
            sp.wait_ge(acc_ok, NT * E_N)
            sp.dma_start(io["out"][:, 0, :], y[0:B, NT - 1, :]).then_inc(out_done, 16)
            sp.wait_ge(out_done, 16 * (B + 1))

        @block.gpsimd
        def _(pool):
            pool.memset(mv[:, :, :], 1.0).then_inc(zero_ok, 1)
            pool.memset(s_[:, :, :], 0.0).then_inc(zero_ok, 1)

        @block.scalar
        def _(act):
            nc.scalar.preload_act_table_set("natural_log_exp_and_others")
            act.wait_ge(var_ok, 1)
            act.activation(rstd[:, 0, :], rstd[:, 2, :], ACT.Ln).then_inc(ln_ok, 1)
            act.wait_ge(ln_ok, 1)
            act.activation(rstd[:, 1, :], rstd[:, 0, :], ACT.Exp, scale=-0.5).then_inc(y0_ok, 1)
            for b in range(B + 1):
                act.wait_ge(tr_done, b + 1)
                src, dst = images(b)
                act.activation(dst(0), src, ACT.Copy).then_inc(xt_hi, 1)
            act.wait_ge(route_done, 1)
            act.wait_ge(zero_ok, 2)
            n = E_G + E_N
            act.activation(s_[:, 0:NT - 1, :], bank[1][:, 0:(NT - 1) * n].rearrange("p (t n) -> p t n", n=n), ACT.Exp, scale=-1.0 / WS).then_inc(rexp_ok, 1)
            act.activation(s_[0:B, NT - 1, :], bank[1][0:B, (NT - 1) * n:NT * n], ACT.Exp, scale=-1.0 / WS).then_inc(rexp_ok, 1)
            nc.scalar.preload_act_table(ACT.Silu)

            def expert(at):
                i = 0
                for kind, nb in ORDER:
                    if kind == "d":
                        continue
                    w = BLOCKS[nb][1]
                    for f in range(EFC):
                        act.wait_ge(gu_done, at(PER, i + 1))
                        act.activation(gs[:, f % 2, 0:w], bank[f % 2][:, 0:w], ACT.Silu, scale=1.0 / WS).then_inc(silu_ok, 1)
                        act.wait_ge(hf_ok, at(PER, i + 1))
                        act.activation(hidden(nb, 0, f), hf[:, f % 2, 0:w], ACT.Copy).then_inc(h_hi, 1)
                        i += 1

            with act.Fori(0, E_N // 2) as ep:
                for eo in range(2):
                    expert(At(act, act.snap(ep * 2 + eo)))

        @block.vector
        def _(v):
            n = [0]

            def step(ins, wait=True):
                ins.then_inc(dve, 1)
                n[0] += 1
                if wait:
                    v.wait_ge(dve, n[0])

            v.tensor_copy(ident_h[:, :], ident[:, :]).then_inc(identh_ok, 1)
            v.wait_ge(rw_in, 16)
            step(v.tensor_scalar(rw[:, :, :], rw[:, :, :], WS, None, ALU.mult))
            step(v.tensor_copy(rw2[:, 0, :, :], rw[:, :, :]))
            step(v.tensor_tensor(rw2[:, 1, :, :], rw[:, :, :], rw2[:, 0, :, :], ALU.subtract))
            v.wait_ge(h0_in, 32)
            for b in range(B + 1):
                v.wait_ge(res_done, b + 1)
                if b < B:
                    r = y[:, QT * b:QT * b + QT, :]
                    src = bank[b][:, :].rearrange("p (j d) -> p j d", j=QT)
                else:
                    r, src = y[0:B, NT - 1, :], bank[0][0:B, 0:D]
                v.tensor_tensor(r, src, r, ALU.add).then_inc(h1_ok, 1)
            v.wait_ge(h1_ok, B + 1)
            v.wait_ge(zero_ok, 2)
            layer_norm_rows(v, step, y, xn, stats, mv, rstd, var_ok, y0_ok)
            v.sem_inc(xn_ok, 1)
            for b in range(B + 1):
                v.wait_ge(xt_hi, b + 1)
                src, dst = images(b)
                v.tensor_tensor(dst(1), src, dst(0), ALU.subtract).then_inc(xt_lo, 1)
            v.wait_ge(rexp_ok, 2)
            step(v.tensor_scalar(s_[:, :, :], s_[:, :, :], 1.0, None, ALU.add))
            step(v.reciprocal(s_[:, :, :], s_[:, :, :]))
            g, m = s_[:, :, 0:E_G], s_[:, :, E_G:].rearrange("p t (g e) -> p t g e", e=E_K)
            step(v.tensor_reduce(top[:, :, :], g, AX.X, ALU.max))
            step(v.tensor_tensor(eq[:, :, :], g, top[:, :, :].broadcast_to([P, NT, E_G]), ALU.is_equal), False)
            step(v.tensor_scalar(val[:, :, :], top[:, :, :], 1e-9, None, ALU.add))
            step(v.reciprocal(val[:, :, :], val[:, :, :]), False)
            step(v.memset(rem[:, :, :], 1.0))
            step(v.tensor_tensor(val[:, :, :], val[:, :, :], top[:, :, :], ALU.mult))
            step(v.tensor_scalar(val[:, :, :], val[:, :, :], 1.0 / WS, None, ALU.mult))
            for i in range(E_G):
                step(v.tensor_tensor(eq[:, :, i:i + 1], eq[:, :, i:i + 1], rem[:, :, :], ALU.mult))
                step(v.tensor_tensor(rem[:, :, :], rem[:, :, :], eq[:, :, i:i + 1], ALU.subtract))
            step(v.tensor_tensor(eq[:, :, :], eq[:, :, :], val[:, :, :].broadcast_to([P, NT, E_G]), ALU.mult))
            step(v.tensor_reduce(pair_sum[:, :, :], m, AX.X, ALU.add))
            step(v.tensor_scalar(pair_sum[:, :, :], pair_sum[:, :, :], 1e-9, None, ALU.add))
            step(v.reciprocal(pair_sum[:, :, :], pair_sum[:, :, :]))
            step(v.tensor_tensor(eq[:, :, :], eq[:, :, :], pair_sum[:, :, :], ALU.mult))
            for i in range(E_K):
                out = wgt[:, :, :].rearrange("p (g e) t -> p e t g", e=E_K)[:, i]
                step(v.tensor_tensor(out, m[:, :, :, i], eq[:, :, :], ALU.mult))
            v.sem_inc(route_ok, 1)

            def expert(at, e):
                v.wait_ge(acc_ok, at(NT, 0))
                i = j = 0
                for kind, nb in ORDER:
                    if kind == "h":
                        w = BLOCKS[nb][1]
                        if nb < 2:
                            v.wait_ge(dn_done, at(NT, 0))
                        elif nb < 4:
                            v.wait_ge(dn_done, at(NT, 4 * (nb - 1)))
                        for f in range(EFC):
                            v.wait_ge(silu_ok, at(PER, i + 1))
                            v.wait_ge(h_lo, at(PER, max(i - 1, 0)))
                            v.scalar_tensor_tensor(hf[:, f % 2, 0:w], bank[2 + f % 2][:, 0:w], 1.0 / WS, gs[:, f % 2, 0:w],
                                                   ALU.mult, ALU.mult).then_inc(hf_ok, 1)
                            v.wait_ge(h_hi, at(PER, i + 1))
                            v.tensor_tensor(hidden(nb, 1, f), hf[:, f % 2, 0:w], hidden(nb, 0, f), ALU.subtract).then_inc(h_lo, 1)
                            i += 1
                    else:
                        for t in tiles(nb):
                            v.wait_ge(dn_done, at(NT, j + 1))
                            r = rows(t)
                            v.scalar_tensor_tensor(y[0:r, t, :], bank[4 + j % 4][0:r, 0:D], wgt[0:r, e, t:t + 1], y[0:r, t, :],
                                                   ALU.mult, ALU.add).then_inc(acc_ok, 1)
                            j += 1

            with v.Fori(0, E_N // 2) as ep:
                for eo in range(2):
                    e = v.snap(ep * 2 + eo)
                    expert(At(v, e), e)

        @block.tensor
        def _(pe):
            mm = pe.matmul
            pe.wait_ge(identh_ok, 1)
            pe.wait_ge(ha_in, 16)
            for b in range(B + 1):
                if b == B:
                    pe.wait_ge(h1_ok, 1)
                for j in range(QT if b < B else 1):
                    for k in range(KC):
                        for t in range(2):
                            lhs = ha[:, b, t, k, j * P:(j + 1) * P] if b < B else ha[:, :, t, k, CLS]
                            out = bank[b % B][0:P if b < B else B, j * D + k * P:j * D + (k + 1) * P]
                            r = mm(out, lhs, ident_h[:, :], start=t == 0, stop=t == 1)
                r.then_inc(res_done, 1)
            pe.wait_ge(xn_ok, 1)
            for b in range(B):
                for k in range(KC):
                    for j in range(QT):
                        r = pe.transpose(bank[b][:, (k * QT + j) * P:(k * QT + j + 1) * P], xn[:, QT * b + j, k * P:(k + 1) * P], ident[:, :])
                r.then_inc(tr_done, 1)
            pe.wait_ge(xt_lo, 1)
            for k in range(KC):
                r = pe.transpose(bank[0][:, k * B:(k + 1) * B], xn[0:B, NT - 1, k * P:(k + 1) * P], ident[0:B, 0:B])
            r.then_inc(tr_done, 1)
            pe.wait_ge(xt_lo, B + 1)
            n = E_G + E_N
            for t in range(NT):
                for i, (k, a, m) in enumerate((k, a, m) for k in range(KC) for a in range(2) for m in range(2)):
                    r = mm(bank[1][0:rows(t), t * n:(t + 1) * n], xT[:, m, k, cols(t)], rw2[:, a, k, :], start=i == 0, stop=i == 7)
            r.then_inc(route_done, 1)
            pe.wait_ge(rexp_ok, 2)
            pe.wait_ge(route_ok, 1)

            def expert(at, eo, loads):
                pe.wait_ge(we_in[eo], loads)
                i = j = 0
                for kind, nb in ORDER:
                    if kind == "h":
                        c0, w = BLOCKS[nb]
                        for f in range(EFC):
                            pe.wait_ge(hf_ok, at(PER, max(i - 1, 0)))
                            for base, bk in ((GATE, f % 2), (UP, 2 + f % 2)):
                                for q, (k, (a, m)) in enumerate((k, t) for k in range(KC) for t in TERMS):
                                    c = base + k * E_F + f * P
                                    r = mm(bank[bk][:, 0:w], we[:, eo, c // SPLIT, a, c % SPLIT:c % SPLIT + P], xT[:, m, k, c0:c0 + w], start=q == 0, stop=q == 5)
                            r.then_inc(gu_done, 1)
                            i += 1
                    else:
                        last_h = 4 * (nb + 1) if nb < 4 else PER
                        pe.wait_ge(h_lo, at(PER, last_h))
                        for ti, t in enumerate(tiles(nb)):
                            pe.wait_ge(acc_ok, at(NT, max(j - 3, 0)))
                            r0 = rows(t)
                            s0 = slice(ti * P, ti * P + r0)
                            for q, (f, (a, m)) in enumerate((f, tm) for f in range(EFC) for tm in TERMS):
                                c = DOWN + f * D
                                r = mm(bank[4 + j % 4][0:r0, 0:D], hidden(nb, m, f)[:, s0], we[:, eo, c // SPLIT, a, :],
                                       start=q == 0, stop=q == EFC * 3 - 1)
                            r.then_inc(dn_done, 1)
                            j += 1

            with pe.Fori(0, E_N // 2) as ep:
                for eo in range(2):
                    expert(At(pe, pe.snap(ep * 2 + eo)), eo, pe.snap(ep * 16 + 16))


def vit_tower(nc, io):
    half = lambda n, s: nc.dram_tensor(n, s, F16, kind="Internal").ap()
    io["hd"] = half("hd_dram", [B, P, 2 * KC * S])
    io["w_split"] = half("w_split_dram", [L, P, 2, W_COLS])
    io["we_split"] = half("we_split_dram", [E_N * E_CHUNKS, P, 2, SPLIT])
    io["cc"] = nc.dram_tensor("cc_dram", [H * S], F32, kind="Internal").ap()
    io["vbd"] = half("vbd_dram", [B, VBD_IMAGE])
    io["h0"] = nc.dram_tensor("h0_dram", [TOKENS, D], F32, kind="Internal").ap()
    with ExitStack() as ctx:
        sb = lambda n, s, d=F32: ctx.enter_context(nc.sbuf_tensor(n, s, d))
        keep = {"ident": sb("ident", [P, P])}
        with ExitStack() as inner:
            keep["w"] = inner.enter_context(nc.sbuf_tensor("w_sb", [P, 2, W_COLS], F16))
            keep["hcls"] = inner.enter_context(nc.sbuf_tensor("hcls", [P, 2, KC, B], F16))
            token_stage(nc, io, keep)
            attention_stage(nc, io, keep)
        expert_stage(nc, io, keep)


def laid_out(i):
    g = lambda n: np.asarray(i[n])
    by_row = lambda w: w.reshape(w.shape[0], -1, P, w.shape[2]).transpose(0, 2, 1, 3).reshape(w.shape[0], P, -1)
    by_col = lambda a: a.reshape(L, -1, P).transpose(0, 2, 1)

    def wavelet(w, n):
        r, c = n // 32, n // 4
        return w.reshape(3, 32, r, 4, c, 3).transpose(3, 1, 0, 2, 4, 5).reshape(P, 3 * r * c, 3)

    a = {
        "x": g("x").reshape(B, 32, 8, 4, 64).transpose(3, 1, 0, 2, 4).reshape(P, B, 8, 64),
        "cls_tok": g("cls_tok").reshape(D),
        "wa": g("L0_tok_Wa").reshape(32, 4, 8).transpose(1, 0, 2).reshape(P, 8),
        "wd1": wavelet(g("L0_tok_Wd1"), 32), "wd2": wavelet(g("L0_tok_Wd2"), 64), "wd3": wavelet(g("L0_tok_Wd3"), 128),
        "gate_bias": np.concatenate([g("L0_tok_" + n) for n in ("ba", "bd1", "bd2", "bd3")]),
        "w": np.concatenate([by_row(g("L0_attn_" + n)) for n in ("W_qkv", "W_r", "W_ff1", "W_o", "W_ff2")], axis=2)
        .reshape(L, P, -1, SPLIT).transpose(0, 2, 1, 3),
        "par": np.concatenate([by_col(g("L0_attn_" + n)) for n in ("ln1_g", "ln1_b", "ln2_g", "ln2_b", "b_ff2", "b_ff1")], axis=2).transpose(1, 0, 2),
        "b2": g("L0_attn_b_ff2").reshape(-1),
        "uv": np.stack([g("L0_attn_" + n).reshape(NP, P).T for n in ("u", "v")], axis=1),
        "we": np.concatenate([by_row(g("L0_ffn_" + n)) for n in ("gate_w", "up_w", "down_w")], axis=2)
        .reshape(E_N, P, -1, SPLIT).transpose(0, 2, 1, 3).reshape(-1, P, SPLIT),
        "rw": np.concatenate([g("L0_ffn_macro_w"), g("L0_ffn_micro_w").transpose(1, 0, 2).reshape(D, E_N)], axis=1)
        .reshape(KC, P, E_G + E_N).transpose(1, 0, 2),
    }
    return {k: np.ascontiguousarray(x) for k, x in {**a, **const_arrays()}.items()}


def kernel(**inputs):
    from concourse import bacc
    from concourse.bass_utils import run_bass_kernel_spmd

    nc = bacc.Bacc("TRN2", target_bir_lowering=False, num_devices=1)
    arrays = {f"in_{n}_dram": a for n, a in laid_out(inputs).items()}
    io = {n[3:-5]: nc.dram_tensor(n, a.shape, mybir.dt.from_np(a.dtype), kind="ExternalInput").ap() for n, a in arrays.items()}
    io["out"] = nc.dram_tensor("out_dram", [B, S, D], F32, kind="ExternalOutput").ap()
    vit_tower(nc, io)
    return run_bass_kernel_spmd(nc, [arrays], core_ids=[0]).results[0]["out_dram"]
```

```python
from contextlib import ExitStack

import numpy as np

import concourse.bass as bass
from concourse import mybir

F32 = mybir.dt.float32
F16 = mybir.dt.float16
I32 = mybir.dt.int32
ALU = mybir.AluOpType
ACT = mybir.ActivationFunctionType
AX = mybir.AxisListType

P = 128
B = 8
IMG = 256
D = IMG
KC = D // P
S = IMG + 1
CLS = IMG
L, H, DH, DF = 4, 16, 64, 1024
HD = H * DH
NP = HD // P
QT = 2
FC = DF // P
EPS = 1e-5
WS = 16.0
NT = B * QT + 1
E_N, E_F, E_G, E_K = 8, 512, 4, 2
EFC = E_F // P
TOKENS = B * S
SLOT_TILES = (TOKENS + E_G * (P - 1)) // P
ROW = D + E_K

C_QKV, C_R, C_1, C_O, C_2 = 0, 6144, 8192, 10240, 12288
W_COLS = 14336
E_COLS = 3072
SPLIT = 256

G1, B1, G2, B2, BF2, BF1 = 0, 2, 4, 6, 8, 10
PAR_COLS = 18
BF1W = PAR_COLS
PAR_ALL = BF1W + FC


def const_arrays():
    pos = np.arange(S - 1, -1, -1, dtype=np.float32)
    freq = (np.float32(1.0) / np.power(np.float32(10000.0), np.arange(0, D, 2, dtype=np.float32) / np.float32(D))).astype(np.float32)
    ang = pos[:, None] * freq[None, :]
    r = np.concatenate([np.sin(ang), np.cos(ang)], axis=-1).astype(np.float32)
    r = np.concatenate([r[1:], r[:1]], axis=0)
    rT = np.ascontiguousarray(r.T.reshape(KC, P, S).transpose(1, 0, 2))
    p = np.arange(P)
    head = 2 * np.arange(NP)[None, :] + (p[:, None] >= DH)
    hmask = (head[:, :, None] == np.arange(H)[None, None, :]).astype(np.float32)
    sel = np.zeros((P, NP, P), np.float32)
    for c in range(NP):
        for m in range(P):
            sel[2 * c + (m >= DH), c, m] = 1.0
    upper = (p[:, None] < p[None, :]).astype(np.float32)
    steps = np.concatenate([P * np.arange(NT), np.arange(SLOT_TILES)]).astype(np.float32)
    row_on = (p[:, None] < B).astype(np.float32)
    return {"c_upper": upper, "c_steps": steps, "c_row_on": row_on, "c_rT": rT, "c_hmask": hmask, "c_sel": sel, "c_ident": np.eye(P, dtype=np.float32)}


def token_stage(nc, io, keep):
    NS = 3
    with ExitStack() as ctx:
        sb = lambda n, s, d=F32: ctx.enter_context(nc.sbuf_tensor(n, s, d))
        used = []

        def sem(n):
            used.append(ctx.enter_context(nc.semaphore(n)))
            return used[-1]

        img = sb("img", [P, B, 8, 64])
        wd = [sb("wd_l1", [P, 384, 3]), sb("wd_l2", [P, 96, 3]), sb("wd_l3", [P, 24, 3])]
        wa = sb("wa", [P, 8])
        bias = sb("gate_bias", [P, 10])
        scale = sb("gate_scale", [P, 10])
        half = sb("half", [P, 2, B, 8, 32])
        det = [sb("det1", [P, B, 3, 128]), sb("det2", [P, B, 3, 32]), sb("det3", [P, B, 3, 8])]
        app = [sb("app1", [P, B, 4, 32]), sb("app2", [P, B, 2, 16]), sb("app3", [P, B, 1, 8])]
        junk = sb("junk", [P, 4, 384])
        part = sb("part", [P, B, 10])
        z = sb("z", [P, B, 10])
        top = sb("top", [P, B, 3])
        e = sb("e", [P, B, 10])
        den = sb("den", [P, B, 4])
        gate = sb("gate", [P, B, 10])
        ones = sb("ones", [P, P])
        xt = sb("xt", [P, NT, D])
        stats = sb("stats", [P, NT, 6])
        mv = sb("mv", [P, NT, 2])
        rstd = sb("rstd", [P, 3, NT])
        hs = sb("hs", [P, B, 2, KC, S], F16)
        wst = sb("wst", [P, NS, 2048])
        hmask = sb("hmask", [P, NP, H])
        uv = sb("uv", [P, 2, NP])
        r_f = sb("r_f", [P, KC, S])
        sel_f = sb("sel_f", [P, NP * P])
        b2_rows = sb("b2_rows", [P, L, D])
        b2_sum = sb("b2_sum", [P, L])
        wmean = sb("wmean", [P, 2048 // SPLIT])
        cls_row = sb("cls_row", [B, D])
        bank = [ctx.enter_context(nc.psum_tensor(f"ta{i}", [P, 512], F32)) for i in range(8)]
        ident, W, u16, wm, rT2, kr16, sel, res_w, par_all, par, cc = (keep[k] for k in (
            "ident", "w", "u16", "wm", "rT2", "kr16", "sel", "res_w", "par_all", "par", "cc"))

        img_in, wd_in, small_in = sem("img_in"), sem("wd_in"), sem("small_in")
        dve = sem("dve_step")
        const_ok, part_ok, tot_ok, logit_ok, exp_ok, rec_ok = map(sem, (
            "const_ok", "part_ok", "tot_ok", "logit_ok", "exp_ok", "rec_ok"))
        h0_out, h0_in, var_ok, ln_ok, y0_ok, xn_ok = map(sem, (
            "h0_out", "h0_in", "var_ok", "ln_ok", "y0_ok", "xn_ok"))
        tr_ok, hi_ok, lo_ok, hd_out = map(sem, ("tr_ok", "hi_ok", "lo_ok", "hd_out"))
        w_in = [sem(f"w_in{i}") for i in range(NS)]
        w_hi, w_scaled, w_lo, w_lo_v, w_centred = map(sem, ("w_hi", "w_scaled", "w_lo", "w_lo_v", "w_centred"))
        set_in, pool_step, kr_done, kr_ok, cc_done, cc_ok = map(sem, (
            "set_in", "pool_step", "kr_done0", "kr_ok0", "cc_done0", "cc_ok0"))
        NW = W_COLS // 2048
        BY_POOL = C_1 // 2048
        POOL_STEPS = 9
        CJ = 2048 // SPLIT
        ctx.callback(clear, nc, used)
        block = ctx.enter_context(nc.Block())

        @block.sync
        def _(sp):
            sp.dma_start(img[:, :, :, :], io["x"]).then_inc(img_in, 16)
            for i, n in enumerate(("wd3", "wd2", "wd1")):
                sp.dma_start(wd[i][:, :, :], io[n]).then_inc(wd_in, 16)
            sp.dma_start(wa[:, :], io["wa"]).then_inc(wd_in, 16)
            sp.dma_start(bias[:, :], io["gate_bias"].partition_broadcast(P)).then_inc(wd_in, 16)
            sp.dma_start(ident[:, :], io["c_ident"]).then_inc(small_in, 16)
            sp.dma_start(cls_row[:, :], io["cls_tok"].partition_broadcast(B)).then_inc(small_in, 16)
            for dst, src in ((uv[:, :, :], io["uv"]), (hmask[:, :, :], io["c_hmask"]), (r_f[:, :, :], io["c_rT"]),
                             (sel_f[:, :], io["c_sel"].rearrange("p c m -> p (c m)")), (par_all[:, :, 0:PAR_COLS], io["par"]),
                             (b2_rows[:, :, :].rearrange("p l d -> p (l d)"), io["b2"].partition_broadcast(P))):
                sp.dma_start(dst, src).then_inc(set_in, 16)
            for i in range(NS):
                sp.dma_start(wst[:, i % NS, :].rearrange("p (j c) -> p j c", c=SPLIT),
                             io["w"][0, i * CJ:(i + 1) * CJ].rearrange("j p c -> p j c")).then_inc(w_in[i % NS], 16)
            sp.wait_ge(small_in, 32)
            sp.dma_start(io["h0c"], cls_row[:, :]).then_inc(h0_out, 16)
            sp.wait_ge(rec_ok, 1)
            for cg in range(4):
                sp.dma_start(io["h0"][cg].rearrange("b (br n) -> br b n", br=32),
                             img[cg * 32:(cg + 1) * 32, :, :, :].rearrange("p b r c -> p b (r c)")).then_inc(h0_out, 16)
            sp.wait_ge(h0_out, 16 * 5)
            load_tokens(sp, io, xt, h0_in)
            sp.wait_ge(lo_ok, B + 1)
            sp.dma_start(io["hd"].rearrange("b p n -> p b n"), hs[:, :, :, :, :].rearrange("p b t k s -> p b (t k s)")).then_inc(hd_out, 16)
            sp.wait_ge(hd_out, 16)

        @block.gpsimd
        def _(pool):
            n = [0]

            def step(ins):
                ins.then_inc(pool_step, 1)
                n[0] += 1
                pool.wait_ge(pool_step, n[0])

            pool.memset(ones[:, :], 1.0).then_inc(const_ok, 1)
            for a, b_, v in ((0, 1, -0.125), (1, 4, 0.125), (4, 7, 0.25), (7, 10, 0.5)):
                pool.memset(scale[:, a:b_], v).then_inc(const_ok, 1)
            pool.memset(mv[:, :, :], 1.0).then_inc(const_ok, 1)
            pool.wait_ge(set_in, 16 * 6)
            pool.wait_ge(small_in, 32)
            step(pool.tensor_scalar(u16[:, :], uv[:, 0, :], WS, None, ALU.mult))
            step(pool.tensor_tensor(uv[:, 1, :], uv[:, 1, :], uv[:, 0, :], ALU.subtract))
            step(pool.tensor_scalar(uv[:, 1, :], uv[:, 1, :], WS, None, ALU.mult))
            step(pool.tensor_tensor(wm[:, :, :], hmask[:, :, :], uv[:, 1, :].unsqueeze(2).broadcast_to([P, NP, H]), ALU.mult))
            step(pool.tensor_scalar(rT2[:, 0, :, :], r_f[:, :, :], 1.0, None, ALU.mult))
            step(pool.tensor_tensor(rT2[:, 1, :, :], r_f[:, :, :], rT2[:, 0, :, :], ALU.subtract))
            step(pool.tensor_scalar(res_w[:, 0, :], ident[:, :], WS, -WS / D, ALU.mult, ALU.add))
            step(pool.memset(res_w[:, 1, :], -WS / D))
            step(pool.tensor_scalar(sel[:, :, :].rearrange("p c m -> p (c m)"), sel_f[:, :], 1.0, None, ALU.mult))
            for i in range(BY_POOL):
                t, c = wst[:, i % NS, :], slice(i * 2048, (i + 1) * 2048)
                pool.wait_ge(w_hi, i + 1)
                pool.tensor_tensor(W[:, 1, c], t, W[:, 0, c], ALU.subtract).then_inc(w_lo, 1)

        @block.scalar
        def _(act):
            def load_weights(i):
                if i - NS < BY_POOL:
                    act.wait_ge(w_lo, i - NS + 1)
                else:
                    act.wait_ge(w_lo_v, i - NS - BY_POOL + 1)
                act.dma_start(wst[:, i % NS, :].rearrange("p (j c) -> p j c", c=SPLIT),
                              io["w"][0, i * CJ:(i + 1) * CJ].rearrange("j p c -> p j c")).then_inc(w_in[i % NS], 16)

            def weights_hi(i):
                act.wait_ge(w_in[i % NS], 16 * (i // NS + 1))
                if i * 2048 >= C_O:
                    act.wait_ge(w_centred, i - C_O // 2048 + 1)
                t, hi = wst[:, i % NS, :], W[:, 0, i * 2048:(i + 1) * 2048]
                if i < BY_POOL:
                    act.activation(t, t, ACT.Copy, scale=WS).then_inc(w_scaled, 1)
                    act.wait_ge(w_scaled, i + 1)
                    act.activation(hi, t, ACT.Copy).then_inc(w_hi, 1)
                else:
                    act.activation(hi, t, ACT.Copy, scale=WS).then_inc(w_hi, 1)

            nc.scalar.preload_act_table_set("natural_log_exp_and_others")
            for i in range(NS):
                weights_hi(i)
            load_weights(NS)
            weights_hi(NS)
            load_weights(NS + 1)
            load_weights(NS + 2)
            act.wait_ge(logit_ok, 1)
            act.activation(e[:, :, :], z[:, :, :], ACT.Exp).then_inc(exp_ok, 1)
            load_weights(NS + 3)
            weights_hi(NS + 1)
            for j in range(NP):
                act.wait_ge(kr_done, j + 1)
                act.activation(kr16[:, j, :], bank[4 + j % 2][:, 0:S], ACT.Copy).then_inc(kr_ok, 1)
            act.wait_ge(cc_done, 1)
            act.activation(cc[:, :], bank[2][0:H, 0:S], ACT.Copy).then_inc(cc_ok, 1)
            for i in range(NS + 2, NW):
                weights_hi(i)
            act.wait_ge(var_ok, 1)
            act.activation(rstd[:, 0, :], rstd[:, 2, :], ACT.Ln).then_inc(ln_ok, 1)
            act.wait_ge(ln_ok, 1)
            act.activation(rstd[:, 1, :], rstd[:, 0, :], ACT.Exp, scale=-0.5).then_inc(y0_ok, 1)
            for b in range(B + 1):
                act.wait_ge(tr_ok, b + 1)
                if b < B:
                    dst, src = hs[:, b, 0, :, 0:IMG], bank[b][:, :].rearrange("p (k s) -> p k s", k=KC)
                else:
                    dst, src = hs[:, :, 0, :, CLS].rearrange("p b k -> p k b"), bank[0][:, 0:KC * B].rearrange("p (k b) -> p k b", k=KC)
                act.activation(dst, src, ACT.Copy).then_inc(hi_ok, 1)

        @block.vector
        def _(v):
            n = [0]

            def step(ins, wait=True):
                ins.then_inc(dve, 1)
                n[0] += 1
                if wait:
                    v.wait_ge(dve, n[0])

            def centre_weights(i):
                t = wst[:, i % NS, :].rearrange("p (j c) -> p j c", c=SPLIT)
                v.wait_ge(w_in[i % NS], 16 * (i // NS + 1))
                step(v.tensor_reduce(wmean[:, :], t, AX.X, ALU.add))
                step(v.tensor_scalar(wmean[:, :], wmean[:, :], -1.0 / SPLIT, None, ALU.mult))
                v.tensor_tensor(t, t, wmean[:, :].unsqueeze(2).broadcast_to([P, CJ, SPLIT]), ALU.add).then_inc(w_centred, 1)

            def split_weights(i):
                if i * 2048 >= C_O:
                    centre_weights(i)
                v.wait_ge(w_hi, i + 1)
                c = slice(i * 2048, (i + 1) * 2048)
                v.scalar_tensor_tensor(W[:, 1, c], wst[:, i % NS, :], WS, W[:, 0, c],
                                       ALU.mult, ALU.subtract).then_inc(w_lo_v, 1)

            v.wait_ge(img_in, 16)
            src = img[:, :, :, :]
            for lv in range(3):
                r, c = 8 >> lv, 32 >> lv
                lo, hi = half[:, 0, :, 0:r, 0:c], half[:, 1, :, 0:r, 0:c]
                step(v.tensor_tensor(lo, src[:, :, :, 0:2 * c:2], src[:, :, :, 1:2 * c:2], ALU.add), False)
                step(v.tensor_tensor(hi, src[:, :, :, 0:2 * c:2], src[:, :, :, 1:2 * c:2], ALU.subtract))
                d = det[lv][:, :, :, :].rearrange("p b k (r c) -> p b k r c", c=c)
                for out, x, op in ((app[lv][:, :, :, :], lo, ALU.add), (d[:, :, 0], lo, ALU.subtract),
                                   (d[:, :, 1], hi, ALU.add), (d[:, :, 2], hi, ALU.subtract)):
                    step(v.tensor_tensor(out, x[:, :, 0:r:2, :], x[:, :, 1:r:2, :], op), False)
                v.wait_ge(dve, n[0])
                src = app[lv][:, :, :, :]
            v.wait_ge(wd_in, 16 * 5)
            d0 = n[0]
            for b in range(B):
                for col, a, w in [(0, app[2][:, b, 0, :], wa[:, :])] + [
                        (1 + 3 * (2 - lv) + k, det[lv][:, b, :, :].rearrange("p k n -> p (k n)"), wd[lv][:, :, k])
                        for lv in range(3) for k in range(3)]:
                    if n[0] - d0 >= 4:
                        v.wait_ge(dve, n[0] - 3)
                    step(v.tensor_tensor_reduce(junk[:, n[0] % 4, 0:a.shape[1]], a, w, 1.0, 0.0, ALU.mult, ALU.add,
                                                part[:, b, col:col + 1]), False)
            v.wait_ge(dve, n[0])
            v.sem_inc(part_ok, 1)
            v.wait_ge(tot_ok, 1)
            v.wait_ge(const_ok, 6)
            bc = lambda t, m: t.unsqueeze(1).broadcast_to([P, B, m])
            step(v.tensor_tensor(z[:, :, :], bank[0][:, 0:B * 10].rearrange("p (b m) -> p b m", m=10), bc(scale[:, :], 10), ALU.mult))
            step(v.tensor_scalar(bias[:, 0:1], bias[:, 0:1], -1.0, None, ALU.mult))
            step(v.tensor_tensor(z[:, :, :], z[:, :, :], bc(bias[:, :], 10), ALU.add))
            z3 = z[:, :, 1:10].rearrange("p b (l k) -> p b l k", k=3)
            step(v.tensor_reduce(top[:, :, :], z3, AX.X, ALU.max))
            v.tensor_tensor(z3, z3, top[:, :, :].unsqueeze(3).broadcast_to([P, B, 3, 3]), ALU.subtract).then_inc(logit_ok, 1)
            v.wait_ge(exp_ok, 1)
            step(v.tensor_scalar(den[:, :, 0:1], e[:, :, 0:1], 1.0, None, ALU.add), False)
            step(v.tensor_reduce(den[:, :, 1:4], e[:, :, 1:10].rearrange("p b (l k) -> p b l k", k=3), AX.X, ALU.add))
            step(v.memset(e[:, :, 0:1], 1.0))
            step(v.reciprocal(den[:, :, :], den[:, :, :]))
            for i, f in ((0, 1 / 64), (1, 1 / 64), (2, 1 / 16), (3, 1 / 4)):
                step(v.tensor_scalar(den[:, :, i:i + 1], den[:, :, i:i + 1], f, None, ALU.mult), False)
            v.wait_ge(dve, n[0])
            step(v.tensor_tensor(gate[:, :, 0:1], e[:, :, 0:1], den[:, :, 0:1], ALU.mult), False)
            step(v.tensor_tensor(gate[:, :, 1:10].rearrange("p b (l k) -> p b l k", k=3),
                                 e[:, :, 1:10].rearrange("p b (l k) -> p b l k", k=3),
                                 den[:, :, 1:4].unsqueeze(3).broadcast_to([P, B, 3, 3]), ALU.mult))
            a3 = app[2][:, :, 0, :]
            step(v.tensor_tensor(a3, a3, gate[:, :, 0:1].broadcast_to([P, B, 8]), ALU.mult), False)
            for lv in range(3):
                g = gate[:, :, 1 + 3 * (2 - lv):4 + 3 * (2 - lv)]
                m = (4 >> lv) * (32 >> lv)
                step(v.tensor_tensor(det[lv][:, :, :, :], det[lv][:, :, :, :], g.unsqueeze(3).broadcast_to([P, B, 3, m]), ALU.mult), False)
            v.wait_ge(dve, n[0])
            for lv in (2, 1, 0):
                r, c = 8 >> lv, 32 >> lv
                lo, hi = half[:, 0, :, 0:r, 0:c], half[:, 1, :, 0:r, 0:c]
                d = det[lv][:, :, :, :].rearrange("p b k (r c) -> p b k r c", c=c)
                a = app[lv][:, :, :, :]
                for out, x, y in ((lo, a, d[:, :, 0]), (hi, d[:, :, 1], d[:, :, 2])):
                    step(v.tensor_tensor(out[:, :, 0:r:2, :], x, y, ALU.add), False)
                    step(v.tensor_tensor(out[:, :, 1:r:2, :], x, y, ALU.subtract), False)
                v.wait_ge(dve, n[0])
                dst = img[:, :, :, :] if lv == 0 else app[lv - 1][:, :, :, :]
                step(v.tensor_tensor(dst[:, :, :, 0:2 * c:2], lo, hi, ALU.add), False)
                step(v.tensor_tensor(dst[:, :, :, 1:2 * c:2], lo, hi, ALU.subtract))
            v.sem_inc(rec_ok, 1)
            v.wait_ge(set_in, 16 * 6)
            step(v.tensor_reduce(b2_sum[:, :], b2_rows[:, :, :], AX.X, ALU.add))
            step(v.tensor_scalar(b2_sum[:, :], b2_sum[:, :], -1.0 / D, None, ALU.mult))
            step(v.tensor_tensor(par_all[:, :, BF2:BF2 + KC], par_all[:, :, BF2:BF2 + KC],
                                 b2_sum[:, :].unsqueeze(2).broadcast_to([P, L, KC]), ALU.add))
            step(v.tensor_scalar(par_all[:, :, BF1W:BF1W + FC], par_all[:, :, BF1:BF1 + FC], WS, None, ALU.mult))
            step(v.tensor_copy(par[:, :], par_all[:, 0, :]))
            for i in range(BY_POOL, NW):
                split_weights(i)
            v.wait_ge(h0_in, 16 * 5)
            layer_norm_rows(v, step, xt, xt, stats, mv, rstd, var_ok, y0_ok)
            v.sem_inc(xn_ok, 1)
            for b in range(B + 1):
                v.wait_ge(hi_ok, b + 1)
                if b < B:
                    dst, hi, src = hs[:, b, 1, :, 0:IMG], hs[:, b, 0, :, 0:IMG], bank[b][:, :].rearrange("p (k s) -> p k s", k=KC)
                else:
                    q = lambda t: hs[:, :, t, :, CLS].rearrange("p b k -> p k b")
                    dst, hi, src = q(1), q(0), bank[0][:, 0:KC * B].rearrange("p (k b) -> p k b", k=KC)
                v.tensor_tensor(dst, src, hi, ALU.subtract).then_inc(lo_ok, 1)
            v.wait_ge(lo_ok, B + 1)
            for t in range(2):
                step(v.tensor_copy(keep["hcls"][:, t, :, :], hs[:, :, t, :, CLS].rearrange("p b k -> p k b")))

        @block.tensor
        def _(pe):
            pe.wait_ge(const_ok, 6)
            pe.wait_ge(part_ok, 1)
            pe.matmul(bank[0][:, 0:B * 10], ones[:, :], part[:, :, :].rearrange("p b m -> p (b m)"), start=True, stop=True).then_inc(tot_ok, 1)
            pe.wait_ge(w_lo, BY_POOL)
            pe.wait_ge(pool_step, POOL_STEPS)
            for j in range(NP):
                if j >= 2:
                    pe.wait_ge(kr_ok, j - 1)
                for i, (k, a, m) in enumerate((k, a, m) for k in range(KC) for a, m in ((0, 0), (0, 1), (1, 0))):
                    c = C_R + k * HD + j * P
                    t = pe.matmul(bank[4 + j % 2][:, 0:S], W[:, a, c:c + P], rT2[:, m, k, :], start=i == 0, stop=i == 5)
                t.then_inc(kr_done, 1)
            pe.wait_ge(kr_ok, NP)
            for c in range(NP):
                t = pe.matmul(bank[2][0:H, 0:S], wm[:, c, :], kr16[:, c, :], start=c == 0, stop=c == NP - 1)
            t.then_inc(cc_done, 1)
            pe.wait_ge(small_in, 32)
            pe.wait_ge(cc_ok, 1)
            pe.wait_ge(xn_ok, 1)
            for b in range(B):
                for k in range(KC):
                    for j in range(QT):
                        t = pe.transpose(bank[b][:, (k * QT + j) * P:(k * QT + j + 1) * P], xt[:, QT * b + j, k * P:(k + 1) * P], ident[:, :])
                t.then_inc(tr_ok, 1)
            pe.wait_ge(lo_ok, 1)
            for k in range(KC):
                t = pe.transpose(bank[0][:, k * B:(k + 1) * B], xt[0:B, NT - 1, k * P:(k + 1) * P], ident[0:B, 0:B])
            t.then_inc(tr_ok, 1)


def load_tokens(sp, io, rows, done):
    for cg in range(4):
        sp.dma_start(rows[:, 0:NT - 1, cg * 64:(cg + 1) * 64],
                     io["h0"][cg].rearrange("b n -> (b n)").rearrange("(t p c) -> p t c", p=P, c=64)).then_inc(done, 16)
    sp.dma_start(rows[0:B, NT - 1, :], io["h0c"]).then_inc(done, 16)


def layer_norm_rows(v, step, x, out, stats, mv, rstd, var_ok, y0_ok):
    rows = lambda t: P if t < NT - 1 else B
    for t in range(NT):
        step(v.bn_stats(stats[0:rows(t), t, :], x[0:rows(t), t, :]), t == NT - 1)
    for t in range(NT):
        step(v.bn_aggr(mv[0:rows(t), t, :], stats[0:rows(t), t, :]), t == NT - 1)
    var, y, y2 = rstd[:, 2, :], rstd[:, 1, :], rstd[:, 0, :]
    step(v.tensor_scalar(var, mv[:, :, 1], EPS, None, ALU.add))
    v.sem_inc(var_ok, 1)
    v.wait_ge(y0_ok, 1)
    step(v.tensor_tensor(y2, y, y, ALU.mult))
    step(v.tensor_tensor(y2, y2, var, ALU.mult))
    step(v.tensor_scalar(y2, y2, -0.5, 1.5, ALU.mult, ALU.add))
    step(v.tensor_tensor(y, y, y2, ALU.mult))
    for t in range(NT):
        step(v.tensor_scalar(out[0:rows(t), t, :], x[0:rows(t), t, :], mv[0:rows(t), t, 0:1], rstd[0:rows(t), 1, t:t + 1],
                             ALU.subtract, ALU.mult), t == NT - 1)


class At:

    def __init__(self, eng, g):
        self.eng, self.g, self.kept = eng, g, {}

    def __call__(self, per, off):
        if isinstance(self.g, int):
            return per * self.g + off
        if per not in self.kept:
            self.kept[per] = self.eng.snap(self.g * per)
        return self.kept[per] + off if off else self.kept[per]

    def put(self, reg, per, off):
        value = self(per, off)
        if isinstance(value, int):
            return value
        self.eng.reg_mov(reg, value)
        return reg

    def prepare(self, *pers):
        for per in pers:
            self(per, 0)


VBD_IMAGE = H * (2 * HD + DH)


def vbd_rows(vbd, b):
    return vbd[b, 0:H * 2 * HD].rearrange("(h n) -> h n", h=H)


def vbd_diagonal(vbd, t):
    return vbd.rearrange("b (h n) -> b h n", h=H)[:, :, t * HD:t * HD + DH]


class Kind:

    def __init__(self, first, last, last_layer, opening, final):
        self.first, self.last, self.last_layer = first, last, last_layer
        self.ln2 = not opening
        self.next = not final
        self.entry = first and not opening
        self.closing = last and not final


OPENING = Kind(True, False, False, True, False)
MIDDLE = Kind(False, False, False, False, False)
CLOSING = Kind(False, True, False, False, False)
ENTRY = Kind(True, False, False, False, False)
TAIL = Kind(False, False, True, False, False)
FINAL = Kind(False, True, True, False, True)


def iterations(eng, body):
    body(At(eng, 0), 0, 0, OPENING)
    with eng.Fori(0, L - 1) as l:
        l8 = eng.snap(l * B)
        with eng.Fori(1, B - 1) as b:
            body(At(eng, eng.snap(l8 + b)), l, b, MIDDLE)
        body(At(eng, eng.snap(l8 + (B - 1))), l, B - 1, CLOSING)
        body(At(eng, eng.snap(l8 + B)), eng.snap(l + 1), 0, ENTRY)
    with eng.Fori(1, B - 1) as b:
        body(At(eng, eng.snap(b + (L - 1) * B)), L - 1, b, TAIL)
    body(At(eng, L * B - 1), L - 1, B - 1, FINAL)


PLAIN, CENTRED = C_O // SPLIT, (W_COLS - C_O) // SPLIT
E_CHUNKS = E_COLS // SPLIT


def chunk_plan(b, kind):
    if kind.first:
        return (("we", None, E_CHUNKS, False),)
    if kind is MIDDLE:
        return (("w", PLAIN + (b - 1) * 2, 2, True), ("w", (b - 1) * 6, 6, False))
    if kind is CLOSING:
        return (("w", PLAIN + 12, 2, True), ("w", 36, 4, False), ("w", PLAIN + 14, 2, True))
    if kind is TAIL:
        return (("we", L * E_CHUNKS + (b - 1) * 8, 8, False),)
    return ()


def chunks_before(at, l, kind):
    if isinstance(at.g, int):
        return 4 * at.g + 2 * l + (0 if kind.first else 2)
    return at.eng.snap(at.g * 4 + l * 2 + (0 if kind.first else 2))


def attention_stage(nc, io, keep):
    with ExitStack() as ctx:
        sb = lambda n, s, d=F32: ctx.enter_context(nc.sbuf_tensor(n, s, d))
        sem = lambda n: ctx.enter_context(nc.semaphore(n))
        W, ident, hcls, u16, wm, rT2, kr16, sel, res_w, par_all, par, cc = (keep[k] for k in (
            "w", "ident", "hcls", "u16", "wm", "rT2", "kr16", "sel", "res_w", "par_all", "par", "cc"))
        cb = sb("cb", [P, H, S])
        hin = sb("hin", [P, 2, KC, S], F16)
        hres = sb("hres", [P, 2, KC, S], F16)
        hmid = hres
        hout = sb("hout", [P, 2, KC, S], F16)
        rq = sb("rq", [P, 2, NP, S], F16)
        rk = sb("rk", [P, 2, NP, S], F16)
        qs = sb("qs", [P, H, S], F16)
        kh = sb("kh", [P, H, S], F16)
        kl = sb("kl", [P, H, S], F16)
        qbd = sb("qbd", [P, 2, NP, H], F16)
        vs = sb("vs", [P, 2, QT, HD], F16)
        vbd = sb("vbd", [P, 2, HD], F16)
        E = sb("E", [P, 2, QT, S])
        ec = sb("ec", [H, S])
        nb = sb("nb", [P, QT * H])
        nbc = sb("nbc", [H, 1])
        sums = sb("sums", [P, QT, H])
        sumc = sb("sumc", [H, 1])
        rs = sb("rs", [P, QT, H])
        ecr = sb("ecr", [H, 2, 1])
        ecol = sb("ecol", [P, QT, H])
        pt = sb("pt", [P, H, 2, QT, S], F16)
        hid = pt[:, 0:4, :, :, :].rearrange("p h t k s -> p (h t k s)").rearrange("p (t f s) -> p t f s", t=2, f=FC)
        pkr = sb("pkr", [P, 2, 2, S], F16)
        mean_w = sb("mean_w", [P, P])
        o2 = sb("o2", [P, 2, NP, S], F16)
        vcl = o2[0:B, :, :, :].rearrange("b t c s -> b (t c s)")[:, 0:2 * HD].rearrange("b (t n) -> b t n", t=2)
        x = sb("x", [P, KC, S])
        sq = sb("sq", [P, KC, S])
        y = sb("y", [P, S])
        t1 = sb("t1", [P, S])
        rel = sb("rel", [P, 2, S])
        eps = sb("eps", [P, 1])
        wf = sb("wf", [P, 2, SPLIT])
        wh = sb("wh", [P, 2, 2, SPLIT], F16)
        row_mean = sb("row_mean", [P, 2])
        bank = [ctx.enter_context(nc.psum_tensor(f"bk{i}", [P, 512], F32)) for i in range(8)]
        ident_s = ident[0:H, 0:H]

        const_ok = sem("const_ok2")
        zero_out, hin_in, hres_in, vbd_in, stack_in, hd_out, vbd_out, cc_out, cb_in = map(sem, (
            "zero_out", "hin_in", "hres_in", "vbd_in", "stack_in", "hd_out2", "vbd_out", "cc_out", "cb_in"))
        w_sem = {n: sem(n) for n in ("w_qkv_in", "w_r_in", "w_o_in", "w_1_in", "w_2_in")}
        vcls_done, kr_done, cc_done, proj_done, v_done = map(sem, ("vcls_done", "kr_done", "cc_done", "proj_done", "v_done"))
        cs_done, s_done, t_done, clst_done, key_done = map(sem, ("cs_done", "s_done", "t_done", "clst_done", "key_done"))
        rb_done, o_done, wo_done, var1_done, ff1_done, ff2_done, var2_done = map(sem, (
            "rb_done", "o_done", "wo_done", "var1_done", "ff1_done", "ff2_done", "var2_done"))
        vcls_hi, kr_ok, q_ok, v_hi, ecol_ok = map(sem, ("vcls_hi", "kr_ok", "q_ok", "v_hi", "ecol_ok"))
        e_ok, ec_ok, p_hi, pc_hi, key_hi, rb_ok, o_hi = map(sem, ("e_ok", "ec_ok", "p_hi", "pc_hi", "key_hi", "rb_ok", "o_hi"))
        sq1_ok, ln1_ok, y1_ok, z1_hi, relu_ok, ff1_hi = map(sem, ("sq1_ok", "ln1_ok", "y1_ok", "z1_hi", "relu_ok", "ff1_hi"))
        sq2_ok, ln2_ok, y2_ok, z2_hi = map(sem, ("sq2_ok", "ln2_ok", "y2_ok", "z2_hi"))
        cc_ok, vcls_lo, k_ok, v_lo = map(sem, ("cc_ok", "vcls_lo", "k_ok", "v_lo"))
        qbd_ok, sc_ok, s_ok, p_lo, pc_lo, rs_ok, key_lo, on_ok, o_lo = map(sem, (
            "qbd_ok", "sc_ok", "s_ok", "p_lo", "pc_lo", "rs_ok", "key_lo", "on_ok", "o_lo"))
        par_ok, x1_ok, sum1_ok, newton1, z1_ok, z1_lo, rel_ok, ff1_lo = map(sem, (
            "par_ok", "x1_ok", "sum1_ok", "newton1", "z1_ok", "z1_lo", "rel_ok", "ff1_lo"))
        x2_ok, sum2_ok, vy_ok, sum_ok, mean_ok = map(sem, ("x2_ok", "sum2_ok", "vy_ok", "chunk_sum_ok", "chunk_mean_ok"))
        proj_hi, proj_lo, newton2, scaled2, z2_ok, z2_lo, hcls_ok = map(sem, (
            "proj_hi", "proj_lo", "newton2", "scaled2", "z2_ok", "z2_lo", "hcls_ok"))
        split_in = [sem("split_in0"), sem("split_in1")]
        split_out = [sem("split_out0"), sem("split_out1")]
        scaled, split_hi, split_lo = map(sem, ("scaled", "split_hi", "split_lo"))
        CONST = 5
        SCORE = 1.0 / (DH ** 0.5 * WS * WS)
        block = ctx.enter_context(nc.Block())

        TERMS = ((0, 0), (0, 1), (1, 0))
        OB = (7, 0, 2)
        RB = (1, 6)
        VB = (6, 7, 0, 1)
        FB = (2, 6, 7)
        wcol = lambda t, base, k, n, m: W[:, t, base + k * n + m * P:base + k * n + (m + 1) * P]
        chunk_at = lambda s: s // 2 + NP * (s % 2)
        slots = lambda h, kind: () if not kind.next else (h,) if not kind.closing else () if h < NP else (2 * h - H, 2 * h - H + 1)
        flat = lambda t: t[:, :, :, :].rearrange("p t k s -> p (t k s)")

        @block.sync
        def _(sp):
            sp.dma_start(flat(hin), io["hd"][0]).then_inc(hin_in, 16)
            sp.wait_ge(const_ok, CONST)
            for b in range(B):
                sp.dma_start(vbd_rows(io["vbd"], b), vbd[0:H, :, :].rearrange("h t n -> h (t n)")).then_inc(zero_out, 16)
            sp.wait_ge(zero_out, 16 * B)
            count = sp.alloc_register("sp_count")

            def hold(signal, n):
                if not isinstance(n, int):
                    sp.reg_mov(count, n)
                    n = count
                sp.wait_ge(const_ok, CONST)
                sp.wait_ge(signal, n)

            def store_vcls(atl):
                hold(vcls_lo, atl(2, 2))
                for t in range(2):
                    sp.dma_start(vbd_diagonal(io["vbd"], t), vcl[:, t, :].rearrange("b (h d) -> b h d", h=H)).then_inc(vbd_out, 16)
                hold(vbd_out, atl(32, 32))

            def stack(at):
                hold(proj_lo, at(16, 16))
                hold(s_done, at(32, 0))
                for a in range(2):
                    rows = slice(64 * a, 64 * a + 64)
                    for dst, src, lo in ((qs, rq, (0, 1)), (kh, rk, (0, 0)), (kl, rk, (1, 1))):
                        for half in range(2):
                            sp.dma_start(dst[64 * half:64 * half + 64, a:H:2, :], src[rows, lo[half], :, :]).then_inc(stack_in, 16)

            def chunk_list(l, b, kind):
                out = []
                for name, base, n, _ in chunk_plan(b, kind):
                    for i in range(n):
                        if name == "we":
                            j = (l * E_CHUNKS if base is None else base) + i
                            out.append((io["we"][j], io["we_split"][j]))
                        else:
                            j = base + i
                            out.append((io["w"][l + 1, j], io["w_split"][l + 1, :, :, bass.ds(j * SPLIT, SPLIT)]))
                return out

            def load_w(name, a, b, layer):
                sp.dma_start(W[:, :, a:b], io["w_split"][layer, :, :, a:b]).then_inc(w_sem[name], 16)

            def body(at, l, b, kind):
                at.prepare(2, 4, 8, 16)
                n0 = chunks_before(at, l, kind)
                at1 = At(sp, at.g + 1)
                at1.prepare(16, 32)
                plan = chunk_list(l, b, kind)

                def load_chunk(c):
                    hold(split_lo, n0 * 2 + (c - 1) if c >= 2 else n0 * 2)
                    sp.dma_start(wf[:, c % 2, :], plan[c][0]).then_inc(split_in[c % 2], 16)

                if not kind.entry:
                    hold(o_done, at(8, 0))
                    sp.dma_start(vbd[0:H, :, :].rearrange("h t n -> h (t n)"), vbd_rows(io["vbd"], b)).then_inc(vbd_in, 16)
                hold(ff1_done, at(8, 0))
                sp.dma_start(flat(hres), io["hd"][b]).then_inc(hres_in, 16)
                if kind.next:
                    hold(v_done, at(4, 4))
                    sp.dma_start(flat(hin), io["hd"][0 if kind.closing else b + 1]).then_inc(hin_in, 16)
                if kind.closing:
                    for i in range(2):
                        hold(split_out[i], n0 * 16)
                    load_w("w_r_in", C_R, C_1, l + 1)
                    load_w("w_qkv_in", C_QKV, C_R, l + 1)
                for c in range(2 if plan else 0):
                    load_chunk(c)
                if kind.entry:
                    load_w("w_1_in", C_1, C_O, l)
                    hold(ff2_done, at(2, 0))
                    load_w("w_2_in", C_2, W_COLS, l)
                if kind.ln2:
                    store(at, (B if kind.entry else b) - 1)
                if kind.entry:
                    store_vcls(At(sp, l))
                    sp.dma_start(vbd[0:H, :, :].rearrange("h t n -> h (t n)"), vbd_rows(io["vbd"], b)).then_inc(vbd_in, 16)
                if kind.next:
                    stack(at1)
                for c in range(len(plan)):
                    hold(split_lo, n0 * 2 + (c + 1))
                    sp.dma_start(plan[c][1], wh[:, c % 2, :, :]).then_inc(split_out[c % 2], 16)
                    if c + 2 < len(plan):
                        load_chunk(c + 2)
                if kind.closing:
                    for i in range(2):
                        hold(split_out[i], (n0 + 4) * 16)
                    hold(wo_done, at(2, 2))
                    load_w("w_o_in", C_O, C_2, l + 1)

            def store(at, b):
                hold(z2_lo, at(2, 0))
                hold(hd_out, at(16, -16))
                sp.dma_start(io["hd"][b], flat(hout)).then_inc(hd_out, 16)

            store_vcls(At(sp, 0))
            stack(At(sp, 0))
            iterations(sp, body)
            store(At(sp, L * B), B - 1)
            sp.wait_ge(hd_out, 16 * L * B)
            for i in range(2):
                sp.wait_ge(split_out[i], 16 * ((L - 1) * (PLAIN + CENTRED) + E_N * E_CHUNKS) // 2)

        @block.gpsimd
        def _(pool):
            count, count2 = pool.alloc_register("pool_count"), pool.alloc_register("pool_count2")
            pool.memset(mean_w[:, :], 1.0 / D).then_inc(const_ok, 1)
            pool.memset(qbd[:, :, :, :], 0.0).then_inc(const_ok, 1)
            pool.memset(vbd[:, :, :], 0.0).then_inc(const_ok, 1)
            pool.memset(pkr[:, :, :, :], 0.0).then_inc(const_ok, 1)
            pool.memset(eps[:, :], EPS).then_inc(const_ok, 1)

            def split_projection(at, s):
                j = chunk_at(s)
                dst = rq if j < NP else rk
                n = at.put(count, 8, s // 2 + 1)
                pool.wait_ge(const_ok, CONST)
                pool.wait_ge(q_ok if j < NP else k_ok, n)
                pool.tensor_scalar(dst[:, 0, j % NP, :], rel[:, s % 2, :], 1.0, 1.0, ALU.mult, ALU.mult).then_inc(proj_hi, 1)
                pool.wait_ge(proj_hi, at(16, s + 1))
                pool.tensor_tensor(dst[:, 1, j % NP, :], rel[:, s % 2, :], dst[:, 0, j % NP, :], ALU.subtract).then_inc(proj_lo, 1)

            def ln2_newton(at):
                pool.wait_ge(vy_ok, at(1, 0))
                pool.tensor_tensor(t1[:, :], t1[:, :], y[:, :], ALU.mult).then_inc(newton2, 1)
                n = at.put(count, 3, -2)
                pool.wait_ge(const_ok, CONST)
                pool.wait_ge(newton2, n)
                pool.tensor_scalar(t1[:, :], t1[:, :], -0.5, 1.5, ALU.mult, ALU.add).then_inc(newton2, 1)
                pool.wait_ge(newton2, at(3, -1))
                pool.tensor_tensor(y[:, :], y[:, :], t1[:, :], ALU.mult).then_inc(newton2, 1)

            def ln2_normalise(at):
                for k in range(KC):
                    pool.wait_ge(newton2, at(3, 0))
                    pool.tensor_tensor(x[:, k, :], x[:, k, :], y[:, :], ALU.mult).then_inc(scaled2, 1)

            def ln2_gain(at):
                for k in range(KC):
                    n = at.put(count, 2, k - 1)
                    pool.wait_ge(const_ok, CONST)
                    pool.wait_ge(scaled2, n)
                    pool.tensor_scalar(x[:, k, :], x[:, k, :], par[:, G2 + k:G2 + k + 1], par[:, B2 + k:B2 + k + 1],
                                       ALU.mult, ALU.add).then_inc(z2_ok, 1)

            def ln2_lo(at, b):
                for k in range(KC):
                    pool.wait_ge(z2_hi, at(2, k - 1))
                    pool.tensor_tensor(hout[:, 1, k, :], x[:, k, :], hout[:, 0, k, :], ALU.subtract).then_inc(z2_lo, 1)
                n = at.put(count, 2, 0)
                pool.wait_ge(const_ok, CONST)
                pool.wait_ge(z2_lo, n)
                pool.tensor_copy(hcls[:, :, :, b], hout[:, :, :, CLS]).then_inc(hcls_ok, 1)

            def split_chunks(at, l, b, kind):
                n0 = chunks_before(at, l, kind)
                c = centred_before = 0
                for _, _, n, centred in chunk_plan(b, kind):
                    for _ in range(n):
                        i = c % 2
                        pool.reg_mov(count, n0 * 16 + 16 * (c // 2 + 1))
                        if centred:
                            centred_before += 1
                            m = at.put(count2, 2, centred_before - 2)
                        pool.wait_ge(const_ok, CONST)
                        pool.wait_ge(split_in[i], count)
                        if centred:
                            pool.wait_ge(mean_ok, m)
                            pool.tensor_scalar(wf[:, i, :], wf[:, i, :], WS, row_mean[:, i:i + 1], ALU.mult, ALU.add).then_inc(scaled, 1)
                        else:
                            pool.tensor_scalar(wf[:, i, :], wf[:, i, :], WS, 1.0, ALU.mult, ALU.mult).then_inc(scaled, 1)
                        pool.reg_mov(count, n0 * 2 + (c + 1))
                        pool.reg_mov(count2, n0 * 16 + 16 * (c // 2))
                        pool.wait_ge(const_ok, CONST)
                        pool.wait_ge(scaled, count)
                        pool.wait_ge(split_out[i], count2)
                        pool.tensor_scalar(wh[:, i, 0, :], wf[:, i, :], 1.0, 1.0, ALU.mult, ALU.mult).then_inc(split_hi, 1)
                        pool.wait_ge(split_hi, n0 * 2 + (c + 1))
                        pool.tensor_tensor(wh[:, i, 1, :], wf[:, i, :], wh[:, i, 0, :], ALU.subtract).then_inc(split_lo, 1)
                        c += 1

            for s in range(2 * NP):
                split_projection(At(pool, 0), s)

            def body(at, l, b, kind):
                at1 = At(pool, at.g + 1)
                for h in range(H):
                    for s in slots(h, kind):
                        split_projection(at1, s)
                    if h == 3 and kind.ln2:
                        ln2_newton(at)
                    if h == 4 and kind.ln2:
                        ln2_normalise(at)
                    if h == 5 and kind.ln2:
                        ln2_gain(at)
                    if h == 9 and kind.ln2:
                        ln2_lo(at, (B if kind.entry else b) - 1)
                if chunk_plan(b, kind):
                    split_chunks(at, l, b, kind)

            iterations(pool, body)
            ln2_newton(At(pool, L * B))
            ln2_normalise(At(pool, L * B))
            ln2_gain(At(pool, L * B))
            ln2_lo(At(pool, L * B), B - 1)

        @block.tensor
        def _(pe):
            mm = pe.matmul
            count = pe.alloc_register("pe_count")

            def project(at, s):
                if s >= 2 or not isinstance(at.g, int) or at.g:
                    pe.wait_ge(q_ok if s % 2 == 0 else k_ok, at(8, s // 2))
                for i, (k, (a, m)) in enumerate((k, t) for k in range(KC) for t in TERMS):
                    r = mm(bank[4 + s % 2][:, 0:S], wcol(a, C_QKV, k, 3 * HD, chunk_at(s)), hin[:, m, k, :], start=i == 0, stop=i == 5)
                r.then_inc(proj_done, 1)

            def project_r(atl, j):
                if j >= 2:
                    pe.wait_ge(kr_ok, atl(8, j - 1))
                for i, (k, (a, m)) in enumerate((k, t) for k in range(KC) for t in TERMS):
                    r = mm(bank[4 + j % 2][:, 0:S], wcol(a, C_R, k, HD, j), rT2[:, m, k, :], start=i == 0, stop=i == 5)
                r.then_inc(kr_done, 1)

            def project_v(at, u):
                tt, half = divmod(u, 2)
                c0 = C_QKV + 2 * HD + half * 512
                for i, (k, (a, m)) in enumerate((k, t) for k in range(KC) for t in TERMS):
                    r = mm(bank[VB[u]][:, :], hin[:, m, k, tt * P:(tt + 1) * P],
                           W[:, a, c0 + k * 3 * HD:c0 + k * 3 * HD + 512], start=i == 0, stop=i == 5)
                r.then_inc(v_done, 1)

            def class_v():
                for half in range(2):
                    c0 = C_QKV + 2 * HD + half * 512
                    for i, (k, (a, m)) in enumerate((k, t) for k in range(KC) for t in TERMS):
                        r = mm(bank[6 + half][0:B, :], hcls[:, m, k, :], W[:, a, c0 + k * 3 * HD:c0 + k * 3 * HD + 512],
                               start=i == 0, stop=i == 5)
                    r.then_inc(vcls_done, 1)

            def position_term(atl):
                pe.wait_ge(kr_ok, atl(8, 8))
                for c in range(NP):
                    r = mm(bank[2][0:H, 0:S], wm[:, c, :], kr16[:, c, :], start=c == 0, stop=c == NP - 1)
                r.then_inc(cc_done, 1)

            def variance(ready, n, bk, done):
                pe.wait_ge(ready, n)
                mm(bank[bk][:, 0:S], mean_w[:, :], t1[:, :], start=True, stop=True).then_inc(done, 1)

            def transposes(at, h):
                pe.wait_ge(e_ok, at(32, 2 * h + 2))
                if h >= 2:
                    pe.wait_ge(p_lo, at(16, h - 1))
                for kt in range(QT):
                    for qt in range(QT):
                        r = pe.transpose(bank[2 + h % 2][:, (kt * QT + qt) * P:(kt * QT + qt + 1) * P],
                                         E[:, h % 2, qt, kt * P:(kt + 1) * P], ident[:, :])
                r.then_inc(t_done, 1)

            def pv(at, c):
                pe.wait_ge(p_lo, at(16, 2 * c + 2))
                o = bank[OB[c % 3]]
                for kt in range(QT):
                    for i, (a, m) in enumerate(TERMS):
                        for s_ in range(2):
                            h = 2 * c + s_
                            mm(o[DH * s_:DH * (s_ + 1), 0:S], vs[:, a, kt, h * DH:(h + 1) * DH], pt[:, h, m, kt, :],
                               start=kt + i == 0, stop=False)

            pe.wait_ge(const_ok, CONST)
            first = At(pe, 0)
            class_v()
            pe.wait_ge(hin_in, 16)
            for s in range(2 * NP):
                project(first, s)
            pe.wait_ge(vcls_lo, 2)
            for u in range(4):
                project_v(first, u)

            def body(at, l, b, kind):
                at1 = At(pe, at.g + 1)
                atl, atl1 = At(pe, l), At(pe, l + 1)
                pe.wait_ge(v_lo, at(4, 4))
                pe.wait_ge(qbd_ok, at(2, 2))
                for c in range(NP):
                    for i, (a, m) in enumerate(TERMS):
                        r = mm(bank[6][0:H, 0:S], qbd[:, a, c, :], rk[:, m, c, :], start=c + i == 0, stop=(c == NP - 1 and i == 2))
                r.then_inc(cs_done, 1)
                pe.wait_ge(stack_in, at(192, 192))
                if kind.next:
                    pe.wait_ge(hin_in, at(16, 32))
                for h in range(H):
                    for qt in range(QT):
                        if h:
                            pe.wait_ge(s_ok, at(32, 2 * h + qt - 1))
                        q = qs[:, h, qt * P:(qt + 1) * P]
                        mm(bank[qt][:, 0:S], q, kh[:, h, :], start=True, stop=False)
                        mm(bank[qt][:, 0:S], q, kl[:, h, :], start=False, stop=True).then_inc(s_done, 1)
                    if h == 0 and kind.ln2:
                        pe.wait_ge(sq2_ok, at(2, 0))
                        pe.wait_ge(x2_ok, at(2, 0))
                    if kind.closing and h < NP:
                        if h == 0:
                            pe.wait_ge(w_sem["w_r_in"], atl1(16, 0))
                        project_r(atl, h)
                    if kind.closing and h == NP:
                        pe.wait_ge(kr_ok, atl(8, 8))
                        pe.wait_ge(w_sem["w_qkv_in"], atl1(16, 0))
                    for s in slots(h, kind):
                        project(at1, s)
                    if h == 0 and kind.ln2:
                        variance(sum2_ok, at(1, 0), 7, var2_done)
                    if h:
                        transposes(at, h - 1)
                    if h == 1:
                        n = at.put(count, 1, 1)
                        pe.wait_ge(const_ok, CONST)
                        pe.wait_ge(ec_ok, n)
                        pe.wait_ge(sc_ok, n)
                        for kt in range(QT):
                            r = pe.transpose(bank[6][:, kt * H:(kt + 1) * H], ec[:, kt * P:(kt + 1) * P], ident_s)
                        r.then_inc(clst_done, 1)
                    if h == NP + 3 and kind.entry:
                        pe.wait_ge(hcls_ok, atl(8, 0))
                        pe.wait_ge(pc_lo, at(1, 1))
                        class_v()
                pe.wait_ge(pc_lo, at(1, 1))
                if kind.ln2:
                    pe.wait_ge(vy_ok, at(1, 0))
                if kind.entry:
                    pe.wait_ge(vcls_lo, atl(2, 2))
                pv(at, 0)
                transposes(at, H - 1)
                pe.wait_ge(s_ok, at(32, 32))
                pv(at, 1)
                pe.wait_ge(ecol_ok, at(16, 16))
                pe.wait_ge(rs_ok, at(3, 3))
                for i, src in enumerate((ecol, rs)):
                    for qt in range(QT):
                        r = pe.transpose(bank[6][0:H, (i * QT + qt) * P:(i * QT + qt + 1) * P], src[:, qt, :], ident[:, :])
                r.then_inc(key_done, 1)
                for c in range(NP):
                    if c == 0:
                        pe.wait_ge(p_lo, at(16, H - 1))
                        pv(at, 2)
                        pe.wait_ge(key_lo, at(2, 2))
                        pe.wait_ge(vbd_in, at(16, 16))
                    if c >= 2:
                        pe.wait_ge(rb_ok, at(8, c - 1))
                    for i in range(2):
                        r = mm(bank[RB[c % 2]][:, 0:S], sel[:, c, :], pkr[:, i, 1, :], start=i == 0, stop=i == 1)
                    r.then_inc(rb_done, 1)
                    for i, (a, m) in enumerate(TERMS):
                        r = mm(bank[OB[c % 3]][:, 0:S], vbd[:, a, c * P:(c + 1) * P], pkr[:, m, 0, :], start=False, stop=i == 2)
                    r.then_inc(o_done, 1)
                    if 1 <= c < NP - 2:
                        pe.wait_ge(on_ok, at(8, c))
                        pv(at, c + 2)
                pe.wait_ge(hres_in, at(16, 16))
                if kind.entry:
                    pe.wait_ge(w_sem["w_o_in"], atl(16, 0))
                for m_ in range(KC):
                    for i, k in ((i, k) for i in range(2) for k in range(KC)):
                        mm(bank[4 + m_][:, 0:S], res_w[:, int(k != m_), :], hres[:, i, k, :], start=i + k == 0, stop=False)
                    for c in range(NP):
                        if m_ == 0:
                            pe.wait_ge(o_lo, at(8, c + 1))
                        for i, (a, m) in enumerate(TERMS):
                            r = mm(bank[4 + m_][:, 0:S], wcol(a, C_O, c, D, m_), o2[:, m, c, :], start=False, stop=(c == NP - 1 and i == 2))
                    r.then_inc(wo_done, 1)
                if kind.next:
                    project_v(at1, 0)
                variance(sum1_ok, at(1, 1), 3, var1_done)
                if kind.closing:
                    position_term(atl)
                if kind.next:
                    for u in range(1, 4):
                        project_v(at1, u)
                pe.wait_ge(z1_lo, at(2, 2))
                if kind.closing:
                    pe.wait_ge(cc_ok, atl(1, 1))
                if kind.entry:
                    pe.wait_ge(w_sem["w_1_in"], atl(16, 0))
                for j in range(FC):
                    if kind.next and 1 <= j <= 2:
                        pe.wait_ge(v_lo, at1(4, j))
                    if j >= 3:
                        pe.wait_ge(ff1_hi, at(8, j - 2))
                        if j % 2:
                            pe.wait_ge(rel_ok, at(4, (j - 3) // 2 + 1))
                    for i, (k, (a, m)) in enumerate((k, t) for k in range(KC) for t in TERMS):
                        r = mm(bank[FB[j % 3]][:, 0:S], wcol(a, C_1, k, DF, j), hmid[:, m, k, :], start=i == 0, stop=i == 5)
                    r.then_inc(ff1_done, 1)
                if kind.entry:
                    pe.wait_ge(w_sem["w_2_in"], atl(16, 0))
                for m_ in range(KC):
                    for c in range(FC):
                        if m_ == 0:
                            pe.wait_ge(ff1_lo, at(8, c + 1))
                        for i, (a, m) in enumerate(TERMS):
                            r = mm(bank[4 + m_][:, 0:S], wcol(a, C_2, c, D, m_), hid[:, m, c, :], start=c + i == 0, stop=(c == FC - 1 and i == 2))
                    r.then_inc(ff2_done, 1)

            iterations(pe, body)
            variance(sum2_ok, L * B, 7, var2_done)

        @block.scalar
        def _(act):
            def take_q(at, s):
                act.wait_ge(proj_done, at(16, s + 1))
                if s or not isinstance(at.g, int) or at.g:
                    act.wait_ge(proj_lo, at(16, s - 1))
                j = chunk_at(s)
                act.activation(rel[:, s % 2, :], bank[4 + s % 2][:, 0:S], ACT.Identity, bias=u16[:, j:j + 1]).then_inc(q_ok, 1)

            def take_kr(atl, j):
                act.wait_ge(kr_done, atl(8, j + 1))
                act.activation(kr16[:, j, :], bank[4 + j % 2][:, 0:S], ACT.Copy).then_inc(kr_ok, 1)

            def v_part(at, u):
                act.wait_ge(v_done, at(4, u + 1))
                tt, half = divmod(u, 2)
                act.activation(vs[:, 0, tt, half * 512:half * 512 + 512], bank[VB[u]][:, :], ACT.Copy).then_inc(v_hi, 1)

            def class_v(atl):
                for half in range(2):
                    act.wait_ge(vcls_done, atl(2, half + 1))
                    act.activation(vcl[:, 0, half * 512:half * 512 + 512], bank[6 + half][0:B, :], ACT.Copy).then_inc(vcls_hi, 1)

            def first_rstd(var_done, n, bk, log_ok, y_ok):
                act.wait_ge(var_done, n)
                act.activation(y[:, :], bank[bk][:, 0:S], ACT.Ln, bias=eps[:, 0:1]).then_inc(log_ok, 1)
                act.wait_ge(log_ok, n)
                act.activation(y[:, :], y[:, :], ACT.Exp, scale=-0.5).then_inc(y_ok, 1)

            def ln2_hi(at):
                act.wait_ge(hd_out, at(16, -16))
                for k in range(KC):
                    act.wait_ge(z2_ok, at(2, k - 1))
                    act.activation(hout[:, 0, k, :], x[:, k, :], ACT.Copy).then_inc(z2_hi, 1)

            def spread_position_term(atl):
                act.wait_ge(cc_ok, atl(1, 1))
                act.dma_start(io["cc"].rearrange("(h s) -> h s", h=H), cc[:, :]).then_inc(cc_out, 16)

            def load_position_term(atl):
                act.wait_ge(cc_out, atl(16, 16))
                act.dma_start(cb[:, :, :].rearrange("p h s -> p (h s)"), io["cc"].partition_broadcast(P)).then_inc(cb_in, 16)

            nc.scalar.preload_act_table_set("natural_log_exp_and_others")
            act.wait_ge(const_ok, CONST)
            first = At(act, 0)
            act.dma_start(io["cc"].rearrange("(h s) -> h s", h=H), cc[:, :]).then_inc(cc_out, 16)
            class_v(first)
            load_position_term(first)
            for s in range(0, 2 * NP, 2):
                take_q(first, s)
            for u in range(4):
                v_part(first, u)

            def p_part(at, h):
                act.wait_ge(t_done, at(16, h + 1))
                act.activation(pt[:, h, 0, :, 0:IMG], bank[2 + h % 2][:, :].rearrange("p (k s) -> p k s", k=QT), ACT.Copy).then_inc(p_hi, 1)

            def o_part(at, c):
                act.wait_ge(on_ok, at(8, c + 1))
                act.activation(o2[:, 0, c, :], x[:, c % 2, :], ACT.Copy).then_inc(o_hi, 1)

            def body(at, l, b, kind):
                at1, atl, atl1 = At(act, at.g + 1), At(act, l), At(act, l + 1)
                act.wait_ge(sc_ok, at(1, 1))
                act.activation(ec[:, :], ec[:, :], ACT.Exp, bias=nbc[:, 0:1], scale=-1.0, accum_out=sumc[:, 0:1]).then_inc(ec_ok, 1)
                for h in range(H):
                    for qt in range(QT):
                        act.wait_ge(s_ok, at(32, 2 * h + qt + 1))
                        act.activation(E[:, h % 2, qt, :], E[:, h % 2, qt, :], ACT.Exp, bias=nb[:, 2 * h + qt:2 * h + qt + 1],
                                       scale=-1.0, accum_out=sums[:, qt, h:h + 1]).then_inc(e_ok, 1)
                    if kind.closing and h < NP:
                        take_kr(atl, h)
                    for s in slots(h, kind):
                        if s % 2 == 0:
                            take_q(at1, s)
                    if h == 1 and kind.ln2:
                        first_rstd(var2_done, at(1, 0), 7, ln2_ok, y2_ok)
                    if h == 8 and kind.ln2:
                        ln2_hi(at)
                    if h == 2:
                        act.wait_ge(clst_done, at(1, 1))
                        act.activation(pt[:, :, 0, :, CLS], bank[6][:, 0:QT * H].rearrange("p (k h) -> p h k", k=QT), ACT.Copy).then_inc(pc_hi, 1)
                    if h:
                        p_part(at, h - 1)
                    if h == NP + 4 and kind.entry:
                        class_v(atl)
                    act.wait_ge(e_ok, at(32, 2 * h + 2))
                    act.activation(ecol[:, :, h:h + 1], E[:, h % 2, :, CLS:S], ACT.Copy).then_inc(ecol_ok, 1)
                p_part(at, H - 1)
                act.wait_ge(key_done, at(1, 1))
                act.activation(pkr[0:H, 0, :, 0:IMG], bank[6][0:H, :].rearrange("p (t s) -> p t s", t=2), ACT.Copy).then_inc(key_hi, 1)
                act.activation(pkr[0:H, 0, :, CLS:S], ecr[:, :, :], ACT.Copy).then_inc(key_hi, 1)
                for c in range(NP):
                    act.wait_ge(rb_done, at(8, c + 1))
                    if c >= 2:
                        act.wait_ge(on_ok, at(8, c - 1))
                    act.activation(sq[:, c % 2, :], bank[RB[c % 2]][:, 0:S], ACT.Copy, scale=1.0 / WS).then_inc(rb_ok, 1)
                    if c:
                        o_part(at, c - 1)
                o_part(at, NP - 1)
                for m in range(KC):
                    act.wait_ge(wo_done, at(2, m + 1))
                    act.activation(sq[:, m, :], bank[4 + m][:, 0:S], ACT.Square, scale=1.0 / WS).then_inc(sq1_ok, 1)
                if kind.next:
                    v_part(at1, 0)
                first_rstd(var1_done, at(1, 1), 3, ln1_ok, y1_ok)
                if kind.closing:
                    spread_position_term(atl)
                if kind.next:
                    v_part(at1, 1)
                for k in range(KC):
                    act.wait_ge(z1_ok, at(2, k + 1))
                    act.activation(hmid[:, 0, k, :], x[:, k, :], ACT.Identity, bias=par[:, B1 + k:B1 + k + 1]).then_inc(z1_hi, 1)
                if kind.next:
                    act.wait_ge(proj_lo, at1(16, 16))
                for j in range(FC):
                    act.wait_ge(ff1_done, at(8, j + 1))
                    if j % 2:
                        act.wait_ge(ff1_lo, at(8, j - 1))
                        act.activation(rel[:, 1, :], bank[FB[j % 3]][:, 0:S], ACT.Relu, bias=par[:, BF1 + j:BF1 + j + 1], scale=1.0 / WS).then_inc(relu_ok, 1)
                    act.activation(hid[:, 0, j, :], bank[FB[j % 3]][:, 0:S], ACT.Relu, bias=par[:, BF1 + j:BF1 + j + 1], scale=1.0 / WS).then_inc(ff1_hi, 1)
                    if kind.closing and j == 2:
                        load_position_term(atl1)
                if kind.next:
                    v_part(at1, 2)
                    v_part(at1, 3)
                for m in range(KC):
                    act.wait_ge(ff2_done, at(2, m + 1))
                    act.activation(sq[:, m, :], bank[4 + m][:, 0:S], ACT.Square, bias=par[:, BF2 + m:BF2 + m + 1], scale=1.0 / WS).then_inc(sq2_ok, 1)

            iterations(act, body)
            first_rstd(var2_done, L * B, 7, ln2_ok, y2_ok)
            ln2_hi(At(act, L * B))

        @block.vector
        def _(v):
            count = v.alloc_register("dve_count")

            def take_k(at, s):
                j = chunk_at(s)
                v.wait_ge(proj_done, at(16, s + 1))
                v.wait_ge(proj_lo, at(16, s - 1))
                v.tensor_tensor(rel[:, s % 2, :], bank[4 + s % 2][:, 0:S], kr16[:, j - NP, :], ALU.add).then_inc(k_ok, 1)

            def v_part(at, u):
                v.wait_ge(v_hi, at(4, u + 1))
                tt, half = divmod(u, 2)
                c = slice(half * 512, half * 512 + 512)
                v.tensor_tensor(vs[:, 1, tt, c], bank[VB[u]][:, :], vs[:, 0, tt, c], ALU.subtract).then_inc(v_lo, 1)

            def class_v(atl):
                for half in range(2):
                    v.wait_ge(vcls_hi, atl(2, half + 1))
                    c = slice(half * 512, half * 512 + 512)
                    v.tensor_tensor(vcl[:, 1, c], bank[6 + half][0:B, :], vcl[:, 0, c], ALU.subtract).then_inc(vcls_lo, 1)

            def class_q(at):
                v.wait_ge(proj_lo, at(16, 16))
                for a in range(2):
                    rows = slice(DH * a, DH * a + DH)
                    v.tensor_copy(qbd[rows, :, :, :].rearrange("p t c h -> p t (c h)")[:, :, a::H + 2][:, :, 0:NP],
                                  rq[rows, :, :, CLS]).then_inc(qbd_ok, 1)

            def position_term(atl):
                v.wait_ge(cc_done, atl(1, 1))
                v.tensor_copy(cc[:, :], bank[2][0:H, 0:S]).then_inc(cc_ok, 1)

            def sum_squares(ready, n, done):
                v.wait_ge(ready, n)
                v.tensor_tensor(t1[:, :], sq[:, 0, :], sq[:, 1, :], ALU.add).then_inc(done, 1)

            def variance_y(y_ok, n, bk, done):
                v.wait_ge(y_ok, n)
                v.scalar_tensor_tensor(t1[:, :], bank[bk][:, 0:S], EPS, y[:, :], ALU.add, ALU.mult).then_inc(done, 1)

            first = At(v, 0)
            class_v(first)
            for s in range(1, 2 * NP, 2):
                take_k(first, s)
            for u in range(4):
                v_part(first, u)
            class_q(first)

            def p_part(at, h):
                v.wait_ge(p_hi, at(16, h + 1))
                v.tensor_tensor(pt[:, h, 1, :, 0:IMG], bank[2 + h % 2][:, :].rearrange("p (k s) -> p k s", k=QT),
                                pt[:, h, 0, :, 0:IMG], ALU.subtract).then_inc(p_lo, 1)

            def o_part(at, c):
                v.wait_ge(o_hi, at(8, c + 1))
                v.tensor_tensor(o2[:, 1, c, :], x[:, c % 2, :], o2[:, 0, c, :], ALU.subtract).then_inc(o_lo, 1)

            def chunk_mean(at, l, kind, c, k):
                i = c % 2
                n0 = chunks_before(at, l, kind)
                v.wait_ge(split_in[i], n0 * 16 + 16 * (c // 2 + 1))
                v.tensor_reduce(row_mean[:, i:i + 1], wf[:, i, :], AX.X, ALU.add).then_inc(sum_ok, 1)
                v.wait_ge(sum_ok, at(2, k - 1))
                v.tensor_scalar(row_mean[:, i:i + 1], row_mean[:, i:i + 1], -WS / SPLIT, None, ALU.mult).then_inc(mean_ok, 1)

            def body(at, l, b, kind):
                at1, atl, atl1 = At(v, at.g + 1), At(v, l), At(v, l + 1)
                cs_count = at.put(count, 1, 1)
                v.wait_ge(const_ok, CONST)
                v.wait_ge(cs_done, cs_count)
                v.tensor_tensor_reduce(ec[:, :], bank[6][0:H, 0:S], cc[:, :], -SCORE, 3e38, ALU.add, ALU.min, nbc[:, :]).then_inc(sc_ok, 1)
                if kind.first:
                    v.wait_ge(cb_in, atl(16, 16))
                for h in range(H):
                    if h >= 2:
                        v.wait_ge(t_done, at(16, h - 1))
                        v.wait_ge(ecol_ok, at(16, h - 1))
                    for qt in range(QT):
                        s_count = at.put(count, 32, 2 * h + qt + 1)
                        v.wait_ge(const_ok, CONST)
                        v.wait_ge(s_done, s_count)
                        v.tensor_tensor_reduce(E[:, h % 2, qt, :], bank[qt][:, 0:S], cb[:, h, :], -SCORE, 3e38,
                                               ALU.add, ALU.min, nb[:, 2 * h + qt:2 * h + qt + 1]).then_inc(s_ok, 1)
                    for s in slots(h, kind):
                        if s % 2:
                            take_k(at1, s)
                    if h >= 2:
                        p_part(at, h - 2)
                    if h == 2 and kind.ln2:
                        variance_y(y2_ok, at(1, 0), 7, vy_ok)
                    if h == 3:
                        v.wait_ge(pc_hi, at(1, 1))
                        v.tensor_tensor(pt[:, :, 1, :, CLS], bank[6][:, 0:QT * H].rearrange("p (k h) -> p h k", k=QT),
                                        pt[:, :, 0, :, CLS], ALU.subtract).then_inc(pc_lo, 1)
                    if h == NP + 5 and kind.entry:
                        class_v(atl)
                v.wait_ge(e_ok, at(32, 32))
                v.reciprocal(rs[:, :, :], sums[:, :, :]).then_inc(rs_ok, 1)
                v.wait_ge(ec_ok, at(1, 1))
                v.tensor_copy(ecr[:, 0, :], ec[:, CLS:S]).then_inc(rs_ok, 1)
                v.reciprocal(ecr[:, 1, :], sumc[:, :]).then_inc(rs_ok, 1)
                p_part(at, H - 2)
                p_part(at, H - 1)
                v.wait_ge(key_hi, at(2, 2))
                v.tensor_tensor(pkr[0:H, 1, :, 0:IMG], bank[6][0:H, :].rearrange("p (t s) -> p t s", t=2),
                                pkr[0:H, 0, :, 0:IMG], ALU.subtract).then_inc(key_lo, 1)
                v.tensor_tensor(pkr[0:H, 1, :, CLS:S], ecr[:, :, :], pkr[0:H, 0, :, CLS:S], ALU.subtract).then_inc(key_lo, 1)
                if kind.ln2:
                    v.wait_ge(z2_lo, at(2, 0))
                if kind is MIDDLE or kind is CLOSING:
                    chunk_mean(at, l, kind, 0, 0)
                    chunk_mean(at, l, kind, 1, 1)
                for c in range(NP):
                    v.wait_ge(o_done, at(8, c + 1))
                    v.wait_ge(rb_ok, at(8, c + 1))
                    if c >= 2:
                        v.wait_ge(o_lo, at(8, c - 1))
                    v.tensor_tensor(x[:, c % 2, :], bank[OB[c % 3]][:, 0:S], sq[:, c % 2, :], ALU.mult).then_inc(on_ok, 1)
                    if c:
                        o_part(at, c - 1)
                o_part(at, NP - 1)
                if kind.entry:
                    v.wait_ge(z2_lo, at(2, 0))
                    v.tensor_copy(par[:, :], par_all[:, l, :]).then_inc(par_ok, 1)
                    v.wait_ge(par_ok, atl(1, 0))
                v.wait_ge(o_lo, at(8, 8))
                for m in range(KC):
                    if m == KC - 1:
                        sum_squares(sq1_ok, at(2, 2), sum1_ok)
                    v.wait_ge(sq1_ok, at(2, m + 1))
                    v.tensor_scalar(x[:, m, :], bank[4 + m][:, 0:S], 1.0 / WS, None, ALU.mult).then_inc(x1_ok, 1)
                if kind.next:
                    v_part(at1, 0)
                variance_y(y1_ok, at(1, 1), 3, newton1)
                v.wait_ge(newton1, at(3, 1))
                v.scalar_tensor_tensor(t1[:, :], t1[:, :], -0.5, y[:, :], ALU.mult, ALU.mult).then_inc(newton1, 1)
                v.wait_ge(newton1, at(3, 2))
                v.scalar_tensor_tensor(y[:, :], t1[:, :], 1.5, y[:, :], ALU.add, ALU.mult).then_inc(newton1, 1)
                v.wait_ge(newton1, at(3, 3))
                v.wait_ge(x1_ok, at(2, 2))
                for k in range(KC):
                    v.scalar_tensor_tensor(x[:, k, :], x[:, k, :], par[:, G1 + k:G1 + k + 1], y[:, :], ALU.mult, ALU.mult).then_inc(z1_ok, 1)
                if kind.closing:
                    position_term(atl)
                for k in range(KC):
                    v.wait_ge(z1_hi, at(2, k + 1))
                    v.scalar_tensor_tensor(hmid[:, 1, k, :], x[:, k, :], par[:, B1 + k:B1 + k + 1], hmid[:, 0, k, :],
                                           ALU.add, ALU.subtract).then_inc(z1_lo, 1)
                if kind.next:
                    v_part(at1, 1)
                if kind is CLOSING:
                    chunk_mean(at, l, kind, 6, 2)
                    chunk_mean(at, l, kind, 7, 3)

                def hidden_lo(j):
                    v.wait_ge(ff1_hi, at(8, j + 1))
                    if j % 2:
                        v.wait_ge(relu_ok, at(4, j // 2 + 1))
                        v.tensor_tensor(hid[:, 1, j, :], rel[:, 1, :], hid[:, 0, j, :], ALU.subtract).then_inc(ff1_lo, 1)
                    else:
                        v.wait_ge(rel_ok, at(4, j // 2 + 1))
                        v.scalar_tensor_tensor(hid[:, 1, j, :], rel[:, 0, :], 1.0 / WS, hid[:, 0, j, :],
                                               ALU.mult, ALU.subtract).then_inc(ff1_lo, 1)

                for j in range(0, FC, 2):
                    v.wait_ge(ff1_hi, at(8, j + 1))
                    v.wait_ge(ff1_lo, at(8, max(j - 1, 0)))
                    v.tensor_scalar(rel[:, 0, :], bank[FB[j % 3]][:, 0:S], par[:, BF1W + j:BF1W + j + 1], 0.0, ALU.add, ALU.max).then_inc(rel_ok, 1)
                    if j:
                        hidden_lo(j - 1)
                    hidden_lo(j)
                hidden_lo(FC - 1)
                if kind.next:
                    v_part(at1, 2)
                    v_part(at1, 3)
                    class_q(at1)
                v.wait_ge(z1_lo, at(2, 2))
                for m in range(KC):
                    if m == KC - 1:
                        sum_squares(sq2_ok, at(2, 2), sum2_ok)
                    v.wait_ge(sq2_ok, at(2, m + 1))
                    v.tensor_scalar(x[:, m, :], bank[4 + m][:, 0:S], 1.0 / WS, par[:, BF2 + m:BF2 + m + 1], ALU.mult, ALU.add).then_inc(x2_ok, 1)

            iterations(v, body)
            variance_y(y2_ok, L * B, 7, vy_ok)


def expert_stage(nc, io, keep):
    with ExitStack() as ctx:
        sb = lambda n, s, d=F32: ctx.enter_context(nc.sbuf_tensor(n, s, d))
        sem = lambda n: ctx.enter_context(nc.semaphore(n))
        ident = keep["ident"]
        ident_h = sb("ident_h", [P, P], F16)
        upper = sb("upper", [P, P])
        upper_h = sb("upper_h", [P, P], F16)
        ones_h = sb("ones_h", [P, P], F16)
        steps = sb("steps", [P, NT + SLOT_TILES])
        row_on = sb("row_on", [P, 1])
        ha = sb("ha", [P, B, 2, KC, S], F16)
        y = sb("y_rows", [P, NT, D])
        xn = sb("xn_rows", [P, NT, ROW])
        back = xn
        xT = sb("xT_cols", [P, 2, KC, TOKENS], F16)
        stats = sb("stats2", [P, NT, 6])
        mv = sb("mv2", [P, NT, 2])
        rstd = sb("rstd2", [P, 3, NT])
        rw = sb("rw", [P, KC, E_G + E_N])
        rw2 = sb("rw2", [P, 2, KC, E_G + E_N], F16)
        s_ = sb("route_s", [P, NT, E_G + E_N])
        top = sb("route_top", [P, NT, 1])
        val = sb("route_val", [P, NT, 1])
        eq = sb("route_eq", [P, NT, E_G])
        eq_h = sb("route_eq_h", [P, NT, E_G], F16)
        rem = sb("route_rem", [P, NT, 1])
        pair_sum = sb("route_pair", [P, NT, E_G])
        share = sb("route_share", [P, NT, E_G, E_K])
        total = sb("slot_total", [P, NT, E_G])
        upto = sb("slot_upto", [P, 2, NT, E_G])
        cmp = sb("slot_cmp", [P, E_G, SLOT_TILES])
        tiles_n = sb("slot_tiles", [P, E_G])
        end = sb("slot_end", [P, E_G])
        base = sb("slot_base", [P, E_G])
        place = sb("slot_place", [P, NT, E_G])
        slot_f = sb("slot_f", [P, NT])
        slot = sb("slot", [P, NT], I32)
        group_f = sb("group_f", [P, SLOT_TILES])
        group = sb("group", [P, SLOT_TILES], I32)
        zero = sb("zero_row", [P, ROW])
        we = sb("we_sb", [P, E_N, E_CHUNKS, 2, SPLIT], F16)
        xs = sb("xs", [P, 2, ROW])
        xt = sb("xt_slots", [P, 2, 2, KC, P], F16)
        ys = sb("ys", [P, 2, D])
        gs = sb("gate_silu", [P, E_K, E_F])
        hf = sb("hidden_f", [P, E_K, E_F])
        hid = sb("hidden", [P, E_K, 2, E_F], F16)
        bank = [ctx.enter_context(nc.psum_tensor(f"ex{i}", [P, 512], F32)) for i in range(8)]

        ha_in, h0_in, rw_in, we_in, zeros_in = map(sem, ("ha_in", "h0_in3", "rw_in", "we_in", "zeros_in"))
        scattered, out_done = map(sem, ("scattered", "out_done"))
        gathered = [sem(f"gathered{i}") for i in range(B + 1)]
        xs_in, ys_out = [sem("xs_in0"), sem("xs_in1")], [sem("ys_out0"), sem("ys_out1")]
        zero_ok, identh_ok, res_done, h1_ok, var_ok, y0_ok, ln_ok, xn_ok = map(sem, (
            "zero_ok", "identh_ok", "res_done", "h1_ok", "var_ok3", "y0_ok3", "ln_ok3", "xn_ok3"))
        tr_done, xt_hi, xt_lo, route_done, rexp_ok, dve = map(sem, (
            "tr_done", "xt_hi", "xt_lo", "route_done", "rexp_ok", "dve_step3"))
        eq_ok, rank_done, slot_ok, weights_ok = map(sem, ("eq_ok", "rank_done", "slot_ok", "weights_ok"))
        x_done, x_hi, x_lo, down_done, y_ok, added = map(sem, ("x_done", "x_hi", "x_lo", "down_done", "y_ok", "added"))
        per_expert = lambda n: [sem(f"{n}{k}") for k in range(E_K)]
        gu_done, silu_ok, h_ok, t_done, hid_hi, hid_lo = map(per_expert, ("gu_done", "silu_ok", "h_ok", "ht_done", "hid_hi", "hid_lo"))
        TERMS = ((0, 0), (0, 1), (1, 0))
        GATE, UP, DOWN = 0, 1024 // SPLIT, 2048 // SPLIT
        ZEROS = 4
        FCH = E_F // SPLIT
        cols = lambda t: slice(t * P, (t + 1) * P) if t < NT - 1 else slice(B * IMG, TOKENS)
        rows = lambda t: P if t < NT - 1 else B
        block = ctx.enter_context(nc.Block())

        def images(b):
            if b < B:
                return bank[b][:, :].rearrange("p (k s) -> p k s", k=KC), (lambda t: xT[:, t, :, b * IMG:(b + 1) * IMG])
            return bank[0][:, 0:KC * B].rearrange("p (k b) -> p k b", k=KC), (lambda t: xT[:, t, :, B * IMG:TOKENS])

        def slot_tiles(eng, tile):
            with eng.Fori(0, SLOT_TILES // 2 - 1) as i:
                for parity in range(2):
                    tile(At(eng, eng.snap(i * 2 + parity)), parity, False)
            for parity in range(2):
                tile(At(eng, SLOT_TILES - 2 + parity), parity, parity == 1)

        @block.sync
        def _(sp):
            count = sp.alloc_register("sp_count3")
            sp.dma_start(ha[:, :, :, :, :].rearrange("p b t k s -> p b (t k s)"), io["hd"].rearrange("b p n -> p b n")).then_inc(ha_in, 16)
            load_tokens(sp, io, y, h0_in)
            sp.dma_start(rw[:, :, :], io["rw"]).then_inc(rw_in, 16)
            sp.dma_start(upper[:, :], io["c_upper"]).then_inc(rw_in, 16)
            sp.dma_start(steps[:, :], io["c_steps"].partition_broadcast(P)).then_inc(rw_in, 16)
            sp.dma_start(row_on[:, :], io["c_row_on"]).then_inc(rw_in, 16)
            sp.wait_ge(zero_ok, ZEROS)
            sp.dma_start(io["xs"].rearrange("(j p) c -> p j c", p=P), zero[:, :].unsqueeze(1).broadcast_to([P, SLOT_TILES, ROW])).then_inc(zeros_in, 16)
            for e in range(E_N):
                sp.dma_start(we[:, e, :, :, :].rearrange("p j t c -> p j (t c)"),
                             io["we_split"][e * E_CHUNKS:(e + 1) * E_CHUNKS].rearrange("j p t c -> p j (t c)")).then_inc(we_in, 16)

            def hold(signal, n):
                if not isinstance(n, int):
                    sp.reg_mov(count, n)
                    n = count
                sp.wait_ge(zero_ok, ZEROS)
                sp.wait_ge(signal, n)

            def load(j, parity):
                sp.dma_start(xs[:, parity, :], io["xs"][bass.ds(j * P, P), :]).then_inc(xs_in[parity], 16)

            def tile(at, parity, last):
                if not isinstance(at.g, int):
                    hold(x_done, at(1, 1))
                    hold(h_ok[1], at(1, 1))
                    load(at(1, 2), parity)
                hold(y_ok, at(1, 1))
                sp.dma_start(io["ys"][bass.ds(at(P, 0), P), :], ys[:, parity, :]).then_inc(ys_out[parity], 16)

            sp.wait_ge(scattered, 16 * NT)
            for j in range(2):
                load(j, j)
            slot_tiles(sp, tile)
            for b in range(B):
                sp.wait_ge(added, QT * (b + 1))
                sp.dma_start(io["out"][b, 1:S, :].rearrange("(j p) d -> p j d", p=P), y[:, QT * b:QT * b + QT, :]).then_inc(out_done, 16)
            sp.wait_ge(added, NT)
            sp.dma_start(io["out"][:, 0, :], y[0:B, NT - 1, :]).then_inc(out_done, 16)
            sp.wait_ge(out_done, 16 * (B + 1))

        @block.gpsimd
        def _(pool):
            pool.memset(mv[:, :, :], 1.0).then_inc(zero_ok, 1)
            pool.memset(s_[:, :, :], 0.0).then_inc(zero_ok, 1)
            pool.memset(zero[:, :], 0.0).then_inc(zero_ok, 1)
            pool.memset(ones_h[:, :], 1.0).then_inc(zero_ok, 1)
            pool.wait_ge(zeros_in, 16)
            pool.wait_ge(slot_ok, 1)
            pool.wait_ge(weights_ok, 1)
            for t in range(NT):
                r = rows(t)
                pool.indirect_dma_start(io["xs"], bass.IndirectOffsetOnAxis(slot[0:r, t:t + 1], 0), xn[0:r, t, :], None).then_inc(scattered, 16)
            pool.wait_ge(scattered, 16 * NT)
            for i in range(2):
                pool.wait_ge(ys_out[i], 16 * SLOT_TILES // 2)
            for t in range(NT):
                r = rows(t)
                pool.indirect_dma_start(back[0:r, t, 0:D], None, io["ys"], bass.IndirectOffsetOnAxis(slot[0:r, t:t + 1], 0)).then_inc(gathered[t // QT], 16)

        @block.scalar
        def _(act):
            nc.scalar.preload_act_table_set("natural_log_exp_and_others")
            act.wait_ge(var_ok, 1)
            act.activation(rstd[:, 0, :], rstd[:, 2, :], ACT.Ln).then_inc(ln_ok, 1)
            act.wait_ge(ln_ok, 1)
            act.activation(rstd[:, 1, :], rstd[:, 0, :], ACT.Exp, scale=-0.5).then_inc(y0_ok, 1)
            for b in range(B + 1):
                act.wait_ge(tr_done, b + 1)
                src, dst = images(b)
                act.activation(dst(0), src, ACT.Copy).then_inc(xt_hi, 1)
            act.wait_ge(route_done, 1)
            act.wait_ge(zero_ok, ZEROS)
            n = E_G + E_N
            act.activation(s_[:, 0:NT - 1, :], bank[1][:, 0:(NT - 1) * n].rearrange("p (t n) -> p t n", n=n), ACT.Exp, scale=-1.0 / WS).then_inc(rexp_ok, 1)
            act.activation(s_[0:B, NT - 1, :], bank[1][0:B, (NT - 1) * n:NT * n], ACT.Exp, scale=-1.0 / WS).then_inc(rexp_ok, 1)
            nc.scalar.preload_act_table(ACT.Silu)

            def rows_hi(at, parity):
                act.wait_ge(x_done, at(1, 1))
                act.activation(xt[:, parity, 0, :, :].rearrange("p k s -> p (k s)"), bank[7][:, 0:D], ACT.Copy).then_inc(x_hi, 1)

            def silu(at, k):
                act.wait_ge(gu_done[k], at(1, 1))
                act.wait_ge(h_ok[k], at(1, 0))
                act.activation(gs[:, k, :], bank[2 * k][:, :], ACT.Silu, scale=1.0 / WS).then_inc(silu_ok[k], 1)

            def hidden_hi(at, k):
                act.wait_ge(t_done[k], at(1, 1))
                act.activation(hid[:, k, 0, :], bank[4 + k][:, :], ACT.Copy).then_inc(hid_hi[k], 1)

            def tile(at, parity, last):
                at1 = At(act, at.g + 1)
                if not last:
                    rows_hi(at1, 1 - parity)
                silu(at, 1)
                hidden_hi(at, 0)
                if not last:
                    silu(at1, 0)
                hidden_hi(at, 1)

            rows_hi(At(act, 0), 0)
            silu(At(act, 0), 0)
            slot_tiles(act, tile)

        @block.vector
        def _(v):
            n = [0]

            def step(ins, wait=True):
                ins.then_inc(dve, 1)
                n[0] += 1
                if wait:
                    v.wait_ge(dve, n[0])

            v.tensor_copy(ident_h[:, :], ident[:, :]).then_inc(identh_ok, 1)
            v.wait_ge(rw_in, 16 * 4)
            step(v.tensor_scalar(rw[:, :, :], rw[:, :, :], WS, None, ALU.mult))
            step(v.tensor_copy(rw2[:, 0, :, :], rw[:, :, :]))
            step(v.tensor_tensor(rw2[:, 1, :, :], rw[:, :, :], rw2[:, 0, :, :], ALU.subtract))
            step(v.tensor_copy(upper_h[:, :], upper[:, :]))
            v.wait_ge(h0_in, 16 * 5)
            for b in range(B + 1):
                v.wait_ge(res_done, b + 1)
                if b < B:
                    r = y[:, QT * b:QT * b + QT, :]
                    src = bank[b][:, :].rearrange("p (j d) -> p j d", j=QT)
                else:
                    r, src = y[0:B, NT - 1, :], bank[0][0:B, 0:D]
                v.tensor_tensor(r, src, r, ALU.add).then_inc(h1_ok, 1)
            v.wait_ge(h1_ok, B + 1)
            v.wait_ge(zero_ok, ZEROS)
            layer_norm_rows(v, step, y, xn[:, :, 0:D], stats, mv, rstd, var_ok, y0_ok)
            v.sem_inc(xn_ok, 1)
            for b in range(B + 1):
                v.wait_ge(xt_hi, b + 1)
                src, dst = images(b)
                v.tensor_tensor(dst(1), src, dst(0), ALU.subtract).then_inc(xt_lo, 1)
            v.wait_ge(rexp_ok, 2)
            step(v.tensor_scalar(s_[:, :, :], s_[:, :, :], 1.0, None, ALU.add))
            step(v.reciprocal(s_[:, :, :], s_[:, :, :]))
            g, m = s_[:, :, 0:E_G], s_[:, :, E_G:].rearrange("p t (g e) -> p t g e", e=E_K)
            step(v.tensor_reduce(top[:, :, :], g, AX.X, ALU.max), False)
            step(v.memset(rem[:, :, :], 1.0))
            step(v.tensor_tensor(eq[:, :, :], g, top[:, :, :].broadcast_to([P, NT, E_G]), ALU.is_equal))
            for i in range(E_G):
                step(v.tensor_tensor(eq[:, :, i:i + 1], eq[:, :, i:i + 1], rem[:, :, :], ALU.mult))
                step(v.tensor_tensor(rem[:, :, :], rem[:, :, :], eq[:, :, i:i + 1], ALU.subtract))
            step(v.tensor_scalar(eq[:, NT - 1, :], eq[:, NT - 1, :], row_on[:, 0:1], None, ALU.mult))
            v.tensor_copy(eq_h[:, :, :], eq[:, :, :]).then_inc(eq_ok, 1)
            v.wait_ge(rank_done, 1)
            tg = lambda bk: bank[bk][:, 0:NT * E_G].rearrange("p (t g) -> p t g", g=E_G)
            step(v.tensor_copy(total[:, :, :], tg(3)), False)
            step(v.tensor_copy(upto[:, 0, :, :], tg(3)))
            now, reach = 0, 1
            while reach < NT:
                a, b_ = upto[:, now, :, :], upto[:, 1 - now, :, :]
                step(v.tensor_copy(b_[:, 0:reach, :], a[:, 0:reach, :]), False)
                step(v.tensor_tensor(b_[:, reach:NT, :], a[:, reach:NT, :], a[:, 0:NT - reach, :], ALU.add))
                now, reach = 1 - now, 2 * reach
            upto_n = upto[:, now, :, :]
            step(v.tensor_tensor(cmp[:, :, 0:NT], upto_n[:, NT - 1, :].unsqueeze(2).broadcast_to([P, E_G, NT]),
                                 steps[:, 0:NT].unsqueeze(1).broadcast_to([P, E_G, NT]), ALU.is_gt))
            step(v.tensor_reduce(tiles_n[:, :], cmp[:, :, 0:NT], AX.X, ALU.add))
            step(v.tensor_copy(end[:, 0:1], tiles_n[:, 0:1]))
            for i in range(1, E_G):
                step(v.tensor_tensor(end[:, i:i + 1], end[:, i - 1:i], tiles_n[:, i:i + 1], ALU.add))
            step(v.tensor_tensor(base[:, :], end[:, :], tiles_n[:, :], ALU.subtract))
            step(v.tensor_scalar(base[:, :], base[:, :], float(P), None, ALU.mult))
            step(v.tensor_tensor(place[:, :, :], tg(2), upto_n, ALU.add))
            step(v.tensor_tensor(place[:, :, :], place[:, :, :], total[:, :, :], ALU.subtract))
            step(v.tensor_tensor(place[:, :, :], place[:, :, :], base[:, :].unsqueeze(1).broadcast_to([P, NT, E_G]), ALU.add))
            step(v.tensor_tensor(place[:, :, :], place[:, :, :], eq[:, :, :], ALU.mult))
            step(v.tensor_reduce(slot_f[:, :], place[:, :, :], AX.X, ALU.add))
            step(v.tensor_copy(slot[:, :], slot_f[:, :]))
            step(v.tensor_tensor(cmp[:, 0:E_G - 1, :], steps[:, NT:].unsqueeze(1).broadcast_to([P, E_G - 1, SLOT_TILES]),
                                 end[:, 0:E_G - 1].unsqueeze(2).broadcast_to([P, E_G - 1, SLOT_TILES]), ALU.is_ge))
            step(v.tensor_reduce(group_f[:, :], cmp[:, 0:E_G - 1, :].rearrange("p g j -> p j g"), AX.X, ALU.add))
            step(v.tensor_copy(group[:, :], group_f[:, :]))
            v.sem_inc(slot_ok, 1)
            step(v.tensor_scalar(val[:, :, :], top[:, :, :], 1e-9, None, ALU.add))
            step(v.reciprocal(val[:, :, :], val[:, :, :]))
            step(v.tensor_tensor(val[:, :, :], val[:, :, :], top[:, :, :], ALU.mult))
            step(v.tensor_tensor(eq[:, :, :], eq[:, :, :], val[:, :, :].broadcast_to([P, NT, E_G]), ALU.mult))
            step(v.tensor_reduce(pair_sum[:, :, :], m, AX.X, ALU.add))
            step(v.tensor_scalar(pair_sum[:, :, :], pair_sum[:, :, :], 1e-9, None, ALU.add))
            step(v.reciprocal(pair_sum[:, :, :], pair_sum[:, :, :]))
            step(v.tensor_tensor(eq[:, :, :], eq[:, :, :], pair_sum[:, :, :], ALU.mult))
            for i in range(E_K):
                step(v.tensor_tensor(share[:, :, :, i], m[:, :, :, i], eq[:, :, :], ALU.mult))
            for i in range(E_K):
                step(v.tensor_reduce(xn[:, :, D + i], share[:, :, :, i], AX.X, ALU.add))
            v.sem_inc(weights_ok, 1)

            def rows_lo(at, parity):
                v.wait_ge(x_hi, at(1, 1))
                v.tensor_tensor(xt[:, parity, 1, :, :].rearrange("p k s -> p (k s)"), bank[7][:, 0:D],
                                xt[:, parity, 0, :, :].rearrange("p k s -> p (k s)"), ALU.subtract).then_inc(x_lo, 1)

            def hidden(at, parity, k):
                v.wait_ge(silu_ok[k], at(1, 1))
                v.wait_ge(t_done[k], at(1, 0))
                v.scalar_tensor_tensor(hf[:, k, :], bank[2 * k + 1][:, :], xs[:, parity, D + k:D + k + 1], gs[:, k, :],
                                       ALU.mult, ALU.mult).then_inc(h_ok[k], 1)

            def hidden_lo(at, k):
                v.wait_ge(hid_hi[k], at(1, 1))
                v.tensor_tensor(hid[:, k, 1, :], bank[4 + k][:, :], hid[:, k, 0, :], ALU.subtract).then_inc(hid_lo[k], 1)

            def tile(at, parity, last):
                at1 = At(v, at.g + 1)
                if not last:
                    rows_lo(at1, 1 - parity)
                hidden(at, parity, 1)
                hidden_lo(at, 0)
                if not last:
                    hidden(at1, 1 - parity, 0)
                hidden_lo(at, 1)
                if isinstance(at.g, int):
                    stored = 16 * (at.g // 2)
                else:
                    stored = at(8, -8 * parity)
                v.wait_ge(ys_out[parity], stored)
                v.wait_ge(down_done, at(1, 1))
                v.tensor_scalar(ys[:, parity, :], bank[6][:, 0:D], 1.0 / (WS * WS), None, ALU.mult).then_inc(y_ok, 1)

            rows_lo(At(v, 0), 0)
            hidden(At(v, 0), 0, 0)
            slot_tiles(v, tile)
            for t in range(NT):
                r = rows(t)
                v.wait_ge(gathered[t // QT], 16 * (QT if t < NT - 1 else 1))
                v.tensor_tensor(y[0:r, t, :], y[0:r, t, :], back[0:r, t, 0:D], ALU.add).then_inc(added, 1)

        @block.tensor
        def _(pe):
            mm = pe.matmul
            pe.wait_ge(identh_ok, 1)
            pe.wait_ge(ha_in, 16)
            for b in range(B + 1):
                if b == B:
                    pe.wait_ge(h1_ok, 1)
                for j in range(QT if b < B else 1):
                    for k in range(KC):
                        for t in range(2):
                            lhs = ha[:, b, t, k, j * P:(j + 1) * P] if b < B else ha[:, :, t, k, CLS]
                            out = bank[b % B][0:P if b < B else B, j * D + k * P:j * D + (k + 1) * P]
                            r = mm(out, lhs, ident_h[:, :], start=t == 0, stop=t == 1)
                r.then_inc(res_done, 1)
            pe.wait_ge(xn_ok, 1)
            for b in range(B):
                for k in range(KC):
                    for j in range(QT):
                        r = pe.transpose(bank[b][:, (k * QT + j) * P:(k * QT + j + 1) * P], xn[:, QT * b + j, k * P:(k + 1) * P], ident[:, :])
                r.then_inc(tr_done, 1)
            pe.wait_ge(xt_lo, 1)
            for k in range(KC):
                r = pe.transpose(bank[0][:, k * B:(k + 1) * B], xn[0:B, NT - 1, k * P:(k + 1) * P], ident[0:B, 0:B])
            r.then_inc(tr_done, 1)
            pe.wait_ge(xt_lo, B + 1)
            n = E_G + E_N
            for t in range(NT):
                for i, (k, a, m) in enumerate((k, a, m) for k in range(KC) for a in range(2) for m in range(2)):
                    r = mm(bank[1][0:rows(t), t * n:(t + 1) * n], xT[:, m, k, cols(t)], rw2[:, a, k, :], start=i == 0, stop=i == 7)
            r.then_inc(route_done, 1)
            pe.wait_ge(zero_ok, ZEROS)
            pe.wait_ge(eq_ok, 1)
            flat = eq_h[:, :, :].rearrange("p t g -> p (t g)")
            mm(bank[2][:, 0:NT * E_G], upper_h[:, :], flat, start=True, stop=True)
            mm(bank[3][:, 0:NT * E_G], ones_h[:, :], flat, start=True, stop=True).then_inc(rank_done, 1)

            def chosen(at):
                j = at(1, 0)
                return pe.value_load(group[0:1, bass.ds(j, 1)] if not isinstance(j, int) else group[0:1, j:j + 1], min_val=0, max_val=E_G - 1)

            def transpose_rows(at, parity, loads):
                pe.wait_ge(xs_in[parity], loads)
                pe.wait_ge(x_lo, at(1, 0))
                for k in range(KC):
                    r = pe.transpose(bank[7][:, k * P:(k + 1) * P], xs[:, parity, k * P:(k + 1) * P], ident[:, :])
                r.then_inc(x_done, 1)

            def gate_up(at, parity, k, g):
                if k == 0:
                    pe.wait_ge(x_lo, at(1, 1))
                pe.wait_ge(h_ok[k], at(1, 0))
                for first, bk in ((GATE, 2 * k), (UP, 2 * k + 1)):
                    for i, (q, (a, m)) in enumerate((q, t) for q in range(KC) for t in TERMS):
                        w = we[:, bass.ds(g * E_K + k, 1), first + q * FCH:first + (q + 1) * FCH, a, :]
                        r = mm(bank[bk][:, :], xt[:, parity, m, q, :], w.rearrange("p e j c -> p (e j) c"), start=i == 0, stop=i == 5)
                r.then_inc(gu_done[k], 1)

            def transpose_hidden(at, k):
                pe.wait_ge(h_ok[k], at(1, 1))
                pe.wait_ge(hid_lo[k], at(1, 0))
                for f in range(EFC):
                    r = pe.transpose(bank[4 + k][:, f * P:(f + 1) * P], hf[:, k, f * P:(f + 1) * P], ident[:, :])
                r.then_inc(t_done[k], 1)

            def down(at, k, g):
                pe.wait_ge(hid_lo[k], at(1, 1))
                if k == 0:
                    pe.wait_ge(y_ok, at(1, 0))
                for i, (f, (a, m)) in enumerate((f, t) for f in range(EFC) for t in TERMS):
                    w = we[:, bass.ds(g * E_K + k, 1), DOWN + f, a, :].rearrange("p e c -> p (e c)")
                    r = mm(bank[6][:, 0:D], hid[:, k, m, f * P:(f + 1) * P], w, start=k + i == 0, stop=(k == E_K - 1 and i == EFC * 3 - 1))
                if k == E_K - 1:
                    r.then_inc(down_done, 1)

            def tile(at, parity, last):
                g = chosen(at)
                at1 = At(pe, at.g + 1)
                if not last:
                    g1 = chosen(at1)
                    loads = 16 * ((at.g + 1) // 2 + 1) if isinstance(at.g, int) else at(8, 16 + 8 * parity)
                    transpose_rows(at1, 1 - parity, loads)
                gate_up(at, parity, 1, g)
                transpose_hidden(at, 0)
                if not last:
                    gate_up(at1, 1 - parity, 0, g1)
                transpose_hidden(at, 1)
                down(at, 0, g)
                down(at, 1, g)

            pe.wait_ge(we_in, 16 * E_N)
            pe.wait_ge(slot_ok, 1)
            transpose_rows(At(pe, 0), 0, 16)
            gate_up(At(pe, 0), 0, 0, chosen(At(pe, 0)))
            slot_tiles(pe, tile)


def clear(nc, semaphores):
    with nc.Block() as block:
        @block.gpsimd
        def _(pool):
            for s in semaphores:
                pool.sem_clear(s)


def vit_tower(nc, io):
    half = lambda n, s: nc.dram_tensor(n, s, F16, kind="Internal").ap()
    io["hd"] = half("hd_dram", [B, P, 2 * KC * S])
    io["w_split"] = half("w_split_dram", [L, P, 2, W_COLS])
    io["we_split"] = half("we_split_dram", [E_N * E_CHUNKS, P, 2, SPLIT])
    io["cc"] = nc.dram_tensor("cc_dram", [H * S], F32, kind="Internal").ap()
    io["xs"] = nc.dram_tensor("xs_dram", [SLOT_TILES * P, ROW], F32, kind="Internal").ap()
    io["ys"] = nc.dram_tensor("ys_dram", [SLOT_TILES * P, D], F32, kind="Internal").ap()
    io["vbd"] = half("vbd_dram", [B, VBD_IMAGE])
    io["h0"] = nc.dram_tensor("h0_dram", [4, B, IMG * 64], F32, kind="Internal").ap()
    io["h0c"] = nc.dram_tensor("h0_cls_dram", [B, D], F32, kind="Internal").ap()
    with ExitStack() as ctx:
        sb = lambda n, s, d=F32: ctx.enter_context(nc.sbuf_tensor(n, s, d))
        keep = {"ident": sb("ident", [P, P])}
        with ExitStack() as inner:
            keep["w"] = inner.enter_context(nc.sbuf_tensor("w_sb", [P, 2, W_COLS], F16))
            held = lambda n, s, d=F32: keep.update({n: inner.enter_context(nc.sbuf_tensor(n, s, d))})
            held("hcls", [P, 2, KC, B], F16)
            held("u16", [P, NP])
            held("wm", [P, NP, H])
            held("rT2", [P, 2, KC, S], F16)
            held("kr16", [P, NP, S])
            held("cc", [H, S])
            held("sel", [P, NP, P], F16)
            held("res_w", [P, 2, P], F16)
            held("par_all", [P, L, PAR_ALL])
            held("par", [P, PAR_ALL])
            token_stage(nc, io, keep)
            attention_stage(nc, io, keep)
        expert_stage(nc, io, keep)


def laid_out(i):
    g = lambda n: np.asarray(i[n])
    by_row = lambda w: w.reshape(w.shape[0], -1, P, w.shape[2]).transpose(0, 2, 1, 3).reshape(w.shape[0], P, -1)
    by_col = lambda a: a.reshape(L, -1, P).transpose(0, 2, 1)

    def wavelet(w, n):
        r, c = n // 32, n // 4
        return w.reshape(3, 32, r, 4, c, 3).transpose(3, 1, 0, 2, 4, 5).reshape(P, 3 * r * c, 3)

    a = {
        "x": g("x").reshape(B, 32, 8, 4, 64).transpose(3, 1, 0, 2, 4).reshape(P, B, 8, 64),
        "cls_tok": g("cls_tok").reshape(D),
        "wa": g("L0_tok_Wa").reshape(32, 4, 8).transpose(1, 0, 2).reshape(P, 8),
        "wd1": wavelet(g("L0_tok_Wd1"), 32), "wd2": wavelet(g("L0_tok_Wd2"), 64), "wd3": wavelet(g("L0_tok_Wd3"), 128),
        "gate_bias": np.concatenate([g("L0_tok_" + n) for n in ("ba", "bd1", "bd2", "bd3")]),
        "w": np.concatenate([by_row(g("L0_attn_" + n)) for n in ("W_qkv", "W_r", "W_ff1", "W_o", "W_ff2")], axis=2)
        .reshape(L, P, -1, SPLIT).transpose(0, 2, 1, 3),
        "par": np.concatenate([by_col(g("L0_attn_" + n)) for n in ("ln1_g", "ln1_b", "ln2_g", "ln2_b", "b_ff2", "b_ff1")], axis=2).transpose(1, 0, 2),
        "b2": g("L0_attn_b_ff2").reshape(-1),
        "uv": np.stack([g("L0_attn_" + n).reshape(NP, P).T for n in ("u", "v")], axis=1),
        "we": np.concatenate([by_row(g("L0_ffn_" + n)) for n in ("gate_w", "up_w", "down_w")], axis=2)
        .reshape(E_N, P, -1, SPLIT).transpose(0, 2, 1, 3).reshape(-1, P, SPLIT),
        "rw": np.concatenate([g("L0_ffn_macro_w"), g("L0_ffn_micro_w").transpose(1, 0, 2).reshape(D, E_N)], axis=1)
        .reshape(KC, P, E_G + E_N).transpose(1, 0, 2),
    }
    return {k: np.ascontiguousarray(x) for k, x in {**a, **const_arrays()}.items()}


def kernel(**inputs):
    from concourse import bacc
    from concourse.bass_utils import run_bass_kernel_spmd

    nc = bacc.Bacc("TRN2", target_bir_lowering=False, num_devices=1)
    arrays = {f"in_{n}_dram": a for n, a in laid_out(inputs).items()}
    io = {n[3:-5]: nc.dram_tensor(n, a.shape, mybir.dt.from_np(a.dtype), kind="ExternalInput").ap() for n, a in arrays.items()}
    io["out"] = nc.dram_tensor("out_dram", [B, S, D], F32, kind="ExternalOutput").ap()
    vit_tower(nc, io)
    return run_bass_kernel_spmd(nc, [arrays], core_ids=[0]).results[0]["out_dram"]
```
